# Optimizing a Trainium2 kernel written in Bass

```python
import numpy as np
import jax
import jax.numpy as jnp

def _softmax(x, axis=-1):
    return jax.nn.softmax(x, axis=axis)
def _gelu(x):
    return jax.nn.gelu(x, approximate=True)
def _silu(x):
    return jax.nn.silu(x)
def _sigmoid(x):
    return jax.nn.sigmoid(x)
def _layernorm(x, axis=-1, eps=1e-5):
    m = jnp.mean(x, axis=axis, keepdims=True)
    v = jnp.var(x, axis=axis, keepdims=True)
    return (x - m) / jnp.sqrt(v + eps)
def _scatter_add(tgt, idx, src, axis=0):
    return tgt.at[idx].add(src)
def _segment_sum(src, seg, n):
    return jax.ops.segment_sum(src, seg, n)

kernel_name = 'mk_audio_tower_d1_tok_audfeat512_276640'

def setup_inputs(seed: int = 0):
    np.random.seed(seed)
    _w = jnp.asarray
    def _rec_inputs():
        import jax
        import jax.numpy as jnp
        _rk = jax.random.key(seed)
        x = (-0.000350306 + 0.999962 * jax.random.normal(jax.random.fold_in(_rk, 1), (256, 256, 207), jnp.float32))
        return x
    x = _rec_inputs()
    def _L0_tok_setup():
        import jax, jax.numpy as jnp
        import numpy as np
        B, STEPS, F = (256, 256, 207)
        P = 16
        D_MODEL = 512
        HID = 4 * P
        key = jax.random.key(seed)
        k1, k2, k3, k4, k5 = jax.random.split(key, 5)
        x = jax.random.normal(k1, (B, STEPS, F), dtype=jnp.float32)
        adj = jax.random.uniform(k2, (F, F), dtype=jnp.float32)
        w1 = jax.random.normal(k3, (P, HID), dtype=jnp.float32) / np.sqrt(P)
        w2 = jax.random.normal(k4, (HID, P), dtype=jnp.float32) / np.sqrt(HID)
        wp = jax.random.normal(k5, (P * F, D_MODEL), dtype=jnp.float32) / np.sqrt(P * F)
        return {'x': x, 'adj': adj, 'w1': w1, 'w2': w2, 'wp': wp}
    _L0_tok_all = _L0_tok_setup()
    _L0_tok_in = {k: v for k, v in _L0_tok_all.items() if k in ('adj', 'w1', 'w2', 'wp', )}
    del _L0_tok_all

    def _L0_attn_setup():
        import jax, jax.numpy as jnp
        import numpy as np
        DIM = 512
        HEADS = 8
        DIM_HEAD = 64
        SLICE = 32
        INNER = HEADS * DIM_HEAD
        key = jax.random.key(seed)
        ks = jax.random.split(key, 8)
        B, N = (8, 8192)
        s = 0.02
        return {'x': jax.random.normal(ks[0], (B, N, DIM), dtype=jnp.float32), 'W_in': jax.random.normal(ks[1], (DIM, INNER), dtype=jnp.float32) * s, 'b_in': jnp.zeros((INNER,), dtype=jnp.float32), 'Wq': jax.random.normal(ks[2], (DIM_HEAD, SLICE), dtype=jnp.float32) * s, 'Wk': jax.random.normal(ks[3], (DIM_HEAD, SLICE), dtype=jnp.float32) * s, 'Wv': jax.random.normal(ks[4], (DIM_HEAD, DIM_HEAD), dtype=jnp.float32) * s, 'W_out': jax.random.normal(ks[5], (INNER, DIM), dtype=jnp.float32) * s, 'b_out': jnp.zeros((DIM,), dtype=jnp.float32)}
    _L0_attn_all = _L0_attn_setup()
    _L0_attn_in = {k: v for k, v in _L0_attn_all.items() if k in ('W_in', 'b_in', 'Wq', 'Wk', 'Wv', 'W_out', 'b_out', )}
    del _L0_attn_all

    def _L0_ffn_setup():
        import jax, jax.numpy as jnp
        import numpy as np
        B, S, D = (8, 8192, 512)
        E, DFF = (16, 512)
        CAPACITY = 2
        key = jax.random.key(seed)
        ks = jax.random.split(key, 4)
        x = jax.random.normal(ks[0], (B, S, D), dtype=jnp.float32)
        gate_weight = jax.random.normal(ks[1], (D, E), dtype=jnp.float32) * 0.006
        w1 = jax.random.normal(ks[2], (E, D, DFF), dtype=jnp.float32) * 0.02
        b1 = jnp.zeros((E, DFF), dtype=jnp.float32)
        w2 = jax.random.normal(ks[3], (E, DFF, D), dtype=jnp.float32) * 0.02
        b2 = jnp.zeros((E, D), dtype=jnp.float32)
        return {'x': x, 'gate_weight': gate_weight, 'w1': w1, 'b1': b1, 'w2': w2, 'b2': b2}
    _L0_ffn_all = _L0_ffn_setup()
    _L0_ffn_in = {k: v for k, v in _L0_ffn_all.items() if k in ('gate_weight', 'w1', 'b1', 'w2', 'b2', )}
    del _L0_ffn_all

    return {
        "x": x,
        "L0_tok_adj": _L0_tok_in["adj"],
        "L0_tok_w1": _L0_tok_in["w1"],
        "L0_tok_w2": _L0_tok_in["w2"],
        "L0_tok_wp": _L0_tok_in["wp"],
        "L0_attn_W_in": _L0_attn_in["W_in"],
        "L0_attn_b_in": _L0_attn_in["b_in"],
        "L0_attn_Wq": _L0_attn_in["Wq"],
        "L0_attn_Wk": _L0_attn_in["Wk"],
        "L0_attn_Wv": _L0_attn_in["Wv"],
        "L0_attn_W_out": _L0_attn_in["W_out"],
        "L0_attn_b_out": _L0_attn_in["b_out"],
        "L0_ffn_gate_weight": _L0_ffn_in["gate_weight"],
        "L0_ffn_w1": _L0_ffn_in["w1"],
        "L0_ffn_b1": _L0_ffn_in["b1"],
        "L0_ffn_w2": _L0_ffn_in["w2"],
        "L0_ffn_b2": _L0_ffn_in["b2"],
    }

def reference(x, L0_tok_adj, L0_tok_w1, L0_tok_w2, L0_tok_wp, L0_attn_W_in, L0_attn_b_in, L0_attn_Wq, L0_attn_Wk, L0_attn_Wv, L0_attn_W_out, L0_attn_b_out, L0_ffn_gate_weight, L0_ffn_w1, L0_ffn_b1, L0_ffn_w2, L0_ffn_b2):
    import jax
    import jax.numpy as jnp
    def _L0_tok_ref(x, adj, w1, w2, wp):
        import jax, jax.numpy as jnp
        import numpy as np
        B, STEPS, F = (256, 256, 207)
        P = 16
        D_MODEL = 512
        HID = 4 * P
        b, steps, f = x.shape
        p = P
        s2 = steps // p
        xg = x.reshape(b, p, s2, f).transpose(0, 1, 3, 2)
        h = jax.nn.gelu(jnp.einsum('nm,bpmd->bpnd', adj, xg) @ w1, approximate=False)
        g = jnp.einsum('nm,bpnd->bpnd'.replace('bpnd->', 'bpmd->'), adj, h) @ w2
        out = g.reshape(b, p, f * s2) @ wp
        return out

    def _L0_attn_ref(x, W_in, b_in, Wq, Wk, Wv, W_out, b_out):
        import jax, jax.numpy as jnp
        import numpy as np
        DIM = 512
        HEADS = 8
        DIM_HEAD = 64
        SLICE = 32
        INNER = HEADS * DIM_HEAD
        B, N, C = x.shape
        x_mid = (x @ W_in + b_in).reshape(B, N, HEADS, DIM_HEAD).transpose(0, 2, 1, 3)
        q = x_mid @ Wq
        k = x_mid @ Wk
        v = x_mid @ Wv
        q = jax.nn.softmax(q, axis=-1)
        k = jax.nn.softmax(k, axis=-2)
        kv = jnp.einsum('bhns,bhnc->bhsc', k, v)
        qkv = jnp.einsum('bhns,bhsc->bhnc', q, kv)
        qkv = qkv.transpose(0, 2, 1, 3).reshape(B, N, INNER)
        return qkv @ W_out + b_out

    def _L0_ffn_ref(x, gate_weight, w1, b1, w2, b2):
        import jax, jax.numpy as jnp
        import numpy as np
        B, S, D = (8, 8192, 512)
        E, DFF = (16, 512)
        CAPACITY = 2
        Bx, Sx, Dx = x.shape
        num_experts = gate_weight.shape[1]
        k = Sx // num_experts * CAPACITY
        logits = jnp.einsum('bsd,de->bse', x, gate_weight)
        affinity = jax.nn.softmax(logits, axis=-1).transpose(0, 2, 1)
        gating, index = jax.lax.top_k(affinity, k)
        x_in = jnp.take_along_axis(x[:, None, :, :], index[..., None], axis=2)
        h = jax.nn.gelu(jnp.einsum('bekd,edh->bekh', x_in, w1) + b1[None, :, None, :])
        x_e = jnp.einsum('bekh,ehd->bekd', h, w2) + b2[None, :, None, :]
        weighted = gating[..., None] * x_e
        out = jnp.zeros_like(x)
        idx_flat = index.reshape(Bx, num_experts * k)
        vals_flat = weighted.reshape(Bx, num_experts * k, Dx)
        out = out.at[jnp.arange(Bx)[:, None], idx_flat].add(vals_flat)
        return out

    h = _L0_tok_ref(x, L0_tok_adj, L0_tok_w1, L0_tok_w2, L0_tok_wp)
    h = h + _L0_attn_ref(_layernorm(h, axis=-1), L0_attn_W_in, L0_attn_b_in, L0_attn_Wq, L0_attn_Wk, L0_attn_Wv, L0_attn_W_out, L0_attn_b_out)
    h = h + _L0_ffn_ref(_layernorm(h, axis=-1), L0_ffn_gate_weight, L0_ffn_w1, L0_ffn_b1, L0_ffn_w2, L0_ffn_b2)
    return h


_drawn_inputs = setup_inputs


def setup_inputs(seed=0):
    import zlib

    import numpy as np

    out = dict(_drawn_inputs(seed))
    spreads = {'L0_attn_b_in': (0.0, 2.0),
     'L0_attn_b_out': (0.0, 2.0),
     'L0_ffn_b1': (0.0, 2.0),
     'L0_ffn_b2': (0.0, 2.0)}
    factors = {'L0_attn_W_in': 8.0,
     'L0_attn_Wq': 23.505,
     'L0_attn_Wk': 23.106,
     'L0_attn_Wv': 8.0,
     'L0_attn_W_out': 8.0,
     'L0_ffn_gate_weight': 64.0,
     'L0_ffn_w1': 64.0,
     'L0_ffn_w2': 64.0}
    for name, (base, spread) in spreads.items():
        noise = np.random.default_rng([zlib.crc32(name.encode()), seed]).standard_normal(out[name].shape)
        drawn = base * np.exp(spread * noise) if base else spread * noise
        out[name] = jnp.asarray(drawn.astype(out[name].dtype))
    for name, factor in factors.items():
        out[name] = (out[name] * factor).astype(out[name].dtype)
    return out
```

```python
from contextlib import ExitStack

import concourse.bass as bass
from concourse import mybir

F32 = mybir.dt.float32
I32 = mybir.dt.int32
U32 = mybir.dt.uint32
ALU = mybir.AluOpType
ACT = mybir.ActivationFunctionType
AX = mybir.AxisListType

P = 128
BANK = 512
BATCH = 256
PATCH = 16
NODES = 207
HID = 64
D = 512
KD = D // P
TOK = BATCH * PATCH
NPAD = 208
CHUNKS = NPAD * PATCH // P
NODE_SPLIT = ((0, P), (P, NPAD - P))
M_START = (0, NODES - P)
OVERLAP = 2 * P - NODES
EPS = 1e-5

TB = 256
SUBS = TB // P
BLOCKS = TOK // TB
DG = 4
GROUPS = PATCH // DG
WINDOWS = 2

HEADS = 8
DH = 64
SLICE = 32
QUADS = 2
EXPERTS = 16
TOP = 2


def make_identity(nc, pool, ident, sem):
    nc.gpsimd.memset(ident[:], 0.0).then_inc(sem, 1)
    pool.wait_ge(sem, 1)
    nc.gpsimd.affine_select(out=ident[:], in_=ident[:], compare_op=ALU.not_equal, fill=1.0, base=0,
                            pattern=[[-1, P]], channel_multiplier=1).then_inc(sem, 1)


def fold_block(nc, adj, wp, w1, w2, wfold_dram, ident, adjT, w1big, w2pair, wfold):
    EG = 2
    NEG = PATCH // EG
    wp_rows = wp.rearrange("(m e) n -> m e n", e=PATCH)
    wfold_rows = wfold_dram.rearrange("(m e) n -> m e n", e=PATCH)
    with ExitStack() as ctx:
        def sb(name, shape, dt=F32):
            return ctx.enter_context(nc.sbuf_tensor(name, shape, dt))

        def sem(name):
            return ctx.enter_context(nc.semaphore(name))

        adj_rows = sb("adj_rows", [P, 2, NODES])
        adj_fold = sb("adj_fold", [P, WINDOWS, NPAD])
        wp_in = sb("wp_in", [P, 2, WINDOWS, EG, D])
        wfold_out = sb("wfold_out", [P, 2, 2, EG, D])
        ps_adj = ctx.enter_context(nc.psum_tensor("ps_adj", [P, 4, P], F32))
        ps_fold = ctx.enter_context(nc.psum_tensor("ps_fold", [P, 4, BANK], F32))

        adj_loaded = sem("adj_loaded")
        fold_cleared = sem("fold_cleared")
        fold_adj_loaded = sem("fold_adj_loaded")
        adj_fold_ready = sem("adj_fold_ready")
        ident_ready = sem("ident_ready")
        cleared = sem("cleared")
        small_loaded = sem("small_loaded")
        adj_turned = sem("adj_turned")
        adjT_copied = sem("adjT_copied")
        adjT_ready = sem("adjT_ready")
        wp_loaded = [sem(f"wp_loaded{s}") for s in range(2)]
        fold_done = sem("fold_done")
        fold_copied = sem("fold_copied")
        fold_stored = [sem(f"fold_stored{s}") for s in range(2)]
        wfold_loaded = sem("wfold_loaded")

        with nc.Block() as block:
            @block.sync
            def _(sp):
                for j, (n0, nn) in enumerate(((0, P), (P, NODES - P))):
                    sp.dma_start(adj_rows[0:nn, j, :], adj[n0:n0 + nn, :]).then_inc(adj_loaded, 16)
                sp.wait_ge(fold_cleared, 1)
                for c, m0 in enumerate(M_START):
                    sp.dma_start(adj_fold[:, c, 0:NODES], adj[m0:m0 + P, :]).then_inc(fold_adj_loaded, 16)
                for g in range(NEG):
                    if g >= 2:
                        sp.wait_ge(fold_done, 2 * EG * (g - 1))
                    for c, m0 in enumerate(M_START):
                        sp.dma_start(wp_in[:, g % 2, c], wp_rows[m0:m0 + P, g * EG:(g + 1) * EG, :]
                                     ).then_inc(wp_loaded[g % 2], 16)

            @block.gpsimd
            def _(pool):
                make_identity(nc, pool, ident, ident_ready)
                nc.gpsimd.memset(w1big[:], 0.0).then_inc(cleared, 1)
                nc.gpsimd.memset(w2pair[:], 0.0).then_inc(cleared, 1)
                pool.wait_ge(cleared, 2)
                for q in range(4):
                    for i in range(2):
                        pool.dma_start(w1big[32 * q + 16 * i:32 * q + 16 * i + 16, q, i * HID:(i + 1) * HID],
                                       w1).then_inc(small_loaded, 16)
                for i in range(2):
                    pool.dma_start(w2pair[i * HID:(i + 1) * HID, i * PATCH:(i + 1) * PATCH],
                                   w2).then_inc(small_loaded, 16)
                pool.wait_ge(small_loaded, 16 * 10)

            @block.scalar
            def _(act):
                for g in range(NEG):
                    act.wait_ge(fold_copied, 2 * EG * (g + 1))
                    for j, (n0, nn) in enumerate(NODE_SPLIT):
                        act.dma_start(wfold_rows[n0:n0 + nn, g * EG:(g + 1) * EG, :],
                                      wfold_out[0:nn, g % 2, j]).then_inc(fold_stored[g % 2], 16)
                act.wait_ge(fold_stored[0], 16 * NEG)
                act.wait_ge(fold_stored[1], 16 * NEG)
                act.dma_start(wfold[:], wfold_dram.rearrange("(c p) n -> p c n", p=P)).then_inc(wfold_loaded, 16)
                act.wait_ge(wfold_loaded, 16)

            @block.tensor
            def _(pe):
                pe.wait_ge(ident_ready, 2)
                pe.wait_ge(adj_loaded, 32)
                for c, m0 in enumerate(M_START):
                    for j, nn in enumerate((P, NODES - P)):
                        last = nc.tensor.transpose(ps_adj[:, 2 * c + j, 0:nn], adj_rows[0:nn, j, m0:m0 + P],
                                                   ident[0:nn, 0:nn])
                last.then_inc(adj_turned, 1)
                pe.wait_ge(adj_fold_ready, 1)
                for g in range(NEG):
                    pe.wait_ge(wp_loaded[g % 2], 32 * (g // 2 + 1))
                    for e in range(EG):
                        for j, (n0, nn) in enumerate(NODE_SPLIT):
                            n = 2 * (EG * g + e) + j
                            if n >= 4:
                                pe.wait_ge(fold_copied, n - 3)
                            for c in range(WINDOWS):
                                last = nc.tensor.matmul(ps_fold[0:nn, n % 4, :], adj_fold[:, c, n0:n0 + nn],
                                                        wp_in[:, g % 2, c, e, :], start=(c == 0),
                                                        stop=(c == WINDOWS - 1))
                            last.then_inc(fold_done, 1)

            @block.vector
            def _(dve):
                nc.vector.memset(adj_fold[:], 0.0).then_inc(fold_cleared, 1)
                nc.vector.memset(adjT[:], 0.0).then_inc(adjT_copied, 1)
                dve.wait_ge(adjT_copied, 1)
                dve.wait_ge(adj_turned, 1)
                for c in range(WINDOWS):
                    for j, nn in enumerate((P, NODES - P)):
                        last = nc.vector.tensor_copy(adjT[:, c, j * P:j * P + nn], ps_adj[:, 2 * c + j, 0:nn])
                        last.then_inc(adjT_copied, 1)
                dve.wait_ge(adjT_copied, 5)
                nc.vector.memset(adjT[0:OVERLAP, 1, :], 0.0).then_inc(adjT_ready, 1)
                dve.wait_ge(fold_adj_loaded, 32)
                nc.vector.memset(adj_fold[0:OVERLAP, 1, :], 0.0).then_inc(adj_fold_ready, 1)
                for g in range(NEG):
                    if g >= 2:
                        dve.wait_ge(fold_stored[g % 2], 32 * (g // 2))
                    for e in range(EG):
                        for j, (n0, nn) in enumerate(NODE_SPLIT):
                            n = 2 * (EG * g + e) + j
                            dve.wait_ge(fold_done, n + 1)
                            nc.vector.tensor_copy(wfold_out[0:nn, g % 2, j, e, :], ps_fold[0:nn, n % 4, :]
                                                  ).then_inc(fold_copied, 1)


def tokenizer_block(nc, x, y_dram, h_dram, ident, adjT, w1big, w2pair, wfold, stats):
    x_tok = x.rearrange("b (p s) f -> (b p) s f", s=PATCH)
    h_rows = h_dram.rearrange("(b s p) n -> b p s n", p=P, s=SUBS)
    PAIRS = CHUNKS // 2
    with ExitStack() as ctx:
        def sb(name, shape, dt=F32):
            return ctx.enter_context(nc.sbuf_tensor(name, shape, dt))

        def psum(name, shape):
            return ctx.enter_context(nc.psum_tensor(name, shape, F32))

        def sem(name):
            return ctx.enter_context(nc.semaphore(name))

        x_in = sb("x_in", [P, 2, SUBS, DG, NODES])
        xT = sb("xT", [P, 2, WINDOWS, DG, TB])
        y = sb("y", [P, 2, 2, DG, TB])
        y_turned = sb("y_turned", [P, 2, CHUNKS, TB])
        hidden = sb("hidden", [P, 2, 2, BANK])
        g_sb = sb("g_sb", [P, 2, 2, TB])
        h_out = sb("h_out", [P, 2, SUBS, D])

        ps_front = psum("ps_front", [P, 2, BANK])
        ps_hid = psum("ps_hid", [P, 2, BANK])
        ps_g = psum("ps_g", [P, 2, BANK])
        ps_h = psum("ps_h", [P, SUBS, BANK])

        x_loaded = [sem(f"x_loaded{s}") for s in range(2)]
        front_filled = sem("front_filled")
        front_copied = sem("front_copied")
        y_stored = [sem(f"y_stored{s}") for s in range(2)]
        y_loaded = sem("y_loaded")
        hid_filled = sem("hid_filled")
        gelu_done = sem("gelu_done")
        g_filled = sem("g_filled")
        g_copied = sem("g_copied")
        proj_done = sem("proj_done")
        h_copied = sem("h_copied")
        h_stored = sem("h_stored")
        h_free = sem("h_free")

        FILLS = 4 * WINDOWS

        with nc.Block() as block:
            @block.gpsimd
            def _(pool):
                def load_x(b, dg):
                    pool.wait_ge(front_filled, FILLS * (GROUPS * b + dg - 2) + 4)
                    pool_load(b, dg)

                def pool_load(b, dg):
                    for s in range(SUBS):
                        pool.dma_start(x_in[:, dg % 2, s],
                                       x_tok[bass.ds(b * TB + s * P, P), dg * DG:(dg + 1) * DG, :]
                                       ).then_inc(x_loaded[dg % 2], 16)

                pool_load(0, 0)
                pool_load(0, 1)
                load_x(0, 2)
                load_x(0, 3)
                with pool.Fori(1, BLOCKS) as b:
                    for dg in range(GROUPS):
                        load_x(b, dg)

            @block.sync
            def _(sp):
                def store_y(b):
                    for dg in range(GROUPS):
                        sp.wait_ge(front_copied, FILLS * (GROUPS * b + dg + 1))
                        for j, (n0, nn) in enumerate(NODE_SPLIT):
                            sp.dma_start(y_dram[b, n0:n0 + nn, dg * DG:(dg + 1) * DG, :],
                                         y[0:nn, dg % 2, j]).then_inc(y_stored[dg % 2], 16)
                    for s in range(2):
                        sp.wait_ge(y_stored[s], 64 * b + 64)

                def load_y(b, slot):
                    sp.dma_start(y_turned[:, slot],
                                 y_dram[b].rearrange("n s t -> (n s) t").rearrange("(c p) t -> p c t", p=P)
                                 ).then_inc(y_loaded, 16)

                def store_h(b, u):
                    sp.wait_ge(h_copied, b + 2)
                    sp.dma_start(h_rows[b], h_out[:, u]).then_inc(h_stored, 16)
                    sp.wait_ge(h_stored, 16 * b + 16)
                    sp.sem_inc(h_free, 1)

                store_y(0)
                load_y(0, 0)
                with sp.Fori(0, BLOCKS - 2, 2) as b:
                    for u in range(2):
                        store_y(b + u + 1)
                        load_y(b + u + 1, 1 - u)
                        store_h(b + u, u)
                store_y(BLOCKS - 1)
                load_y(BLOCKS - 1, 1)
                store_h(BLOCKS - 2, 0)
                store_h(BLOCKS - 1, 1)

            @block.tensor
            def _(pe):
                pe.sem_inc(g_filled, 2)
                pe.sem_inc(proj_done, 2)

                def turn_x(b, dg, first=False):
                    slot = dg % 2
                    pe.wait_ge(x_loaded[slot], 32 * (2 * b + dg // 2) + 32)
                    for k in range(4):
                        c, pair = k // 2, k % 2
                        if not (first and k < 2):
                            pe.wait_ge(front_copied, FILLS * (GROUPS * b + dg) + k - 1)
                        for e in range(2):
                            for s in range(SUBS):
                                last = nc.tensor.transpose(
                                    ps_front[:, k % 2, e * TB + s * P:e * TB + (s + 1) * P],
                                    x_in[:, slot, s, 2 * pair + e, M_START[c]:M_START[c] + P], ident[:])
                        last.then_inc(front_filled, 1)

                def adjacency(b, dg):
                    for k in range(4):
                        pair, j = k // 2, k % 2
                        n0, nn = NODE_SPLIT[j]
                        need = {0: 4, 1: 4, 2: 5, 3: 6}[k]
                        pe.wait_ge(front_copied, FILLS * (GROUPS * b + dg) + need)
                        for c in range(WINDOWS):
                            last = nc.tensor.matmul(ps_front[0:nn, k % 2, :], adjT[:, c, n0:n0 + nn],
                                                    xT[:, dg % 2, c, 2 * pair:2 * pair + 2, :],
                                                    start=(c == 0), stop=(c == WINDOWS - 1))
                        last.then_inc(front_filled, 1)

                def expand(b, u, k):
                    if k == 0:
                        pe.wait_ge(y_loaded, 16 * b + 16)
                    for half in range(2):
                        pe.wait_ge(gelu_done, 2 * CHUNKS * b + 2 * k + half + 1)
                        for i in range(2):
                            last = nc.tensor.matmul(ps_hid[:, half, i * TB:(i + 1) * TB], w1big[:, 2 * half + i, :],
                                                    y_turned[:, u, k, :], start=True, stop=True)
                        last.then_inc(hid_filled, 1)

                def contract(b, u, k):
                    bank = (CHUNKS // 2 * u + k // 2) % 2
                    pe.wait_ge(gelu_done, 2 * CHUNKS * b + 2 * k + 4)
                    if k % 2 == 0:
                        pe.wait_ge(g_copied, PAIRS * b + k // 2 + 1)
                    for q in range(4):
                        last = nc.tensor.matmul(ps_g[32 * q:32 * (q + 1), bank, (k % 2) * TB:(k % 2 + 1) * TB],
                                                w2pair[:], hidden[:, k % 2, q // 2, (q % 2) * TB:(q % 2 + 1) * TB],
                                                start=True, stop=True)
                    last.then_inc(g_filled, 1)

                def project(b, u, k):
                    slot = (CHUNKS // 2 * u + k // 2) % 2
                    if k % 2 == 0:
                        pe.wait_ge(g_copied, PAIRS * b + k // 2 + 3)
                    if k == 0:
                        pe.wait_ge(h_copied, b + 1)
                    for s in range(SUBS):
                        last = nc.tensor.matmul(ps_h[:, s, :], g_sb[:, slot, k % 2, s * P:(s + 1) * P],
                                                wfold[:, k, :], start=(k == 0), stop=(k == CHUNKS - 1))
                    if k % 2 == 1:
                        last.then_inc(proj_done, 1)

                def run_block(b, u, ahead):
                    for step in range(CHUNKS + 3):
                        if step < CHUNKS:
                            expand(b, u, step)
                        if ahead and step < 4 * GROUPS and step % 4 == 0:
                            turn_x(b + 1, step // 4)
                        if ahead and step < 4 * GROUPS and step % 4 == 2:
                            adjacency(b + 1, step // 4)
                        if 1 <= step <= CHUNKS:
                            contract(b, u, step - 1)
                        if step >= 3:
                            project(b, u, step - 3)

                for dg in range(GROUPS):
                    turn_x(0, dg, first=(dg == 0))
                    adjacency(0, dg)
                with pe.Fori(0, BLOCKS - 2, 2) as b:
                    run_block(b, 0, True)
                    run_block(b + 1, 1, True)
                run_block(BLOCKS - 2, 0, True)
                run_block(BLOCKS - 1, 1, False)

            @block.scalar
            def _(act):
                act.sem_inc(gelu_done, 2)

                def gelu_block(b):
                    for k in range(CHUNKS):
                        act.wait_ge(g_filled, CHUNKS * b + k + 1)
                        for half in range(2):
                            act.wait_ge(hid_filled, 2 * CHUNKS * b + 2 * k + half + 1)
                            nc.scalar.activation(hidden[:, k % 2, half], ps_hid[:, half, :], ACT.Gelu
                                                 ).then_inc(gelu_done, 1)

                with act.Fori(0, BLOCKS) as b:
                    gelu_block(b)

            @block.vector
            def _(dve):
                dve.sem_inc(g_copied, 2)
                dve.sem_inc(h_copied, 1)
                dve.sem_inc(h_free, 2)

                def copy_xT(b, dg):
                    for k in range(4):
                        dve.wait_ge(front_filled, FILLS * (GROUPS * b + dg) + k + 1)
                        nc.vector.tensor_copy(xT[:, dg % 2, k // 2, 2 * (k % 2):2 * (k % 2) + 2, :],
                                              ps_front[:, k % 2, :].rearrange("p (s t) -> p s t", s=2)
                                              ).then_inc(front_copied, 1)

                def copy_y(b, dg, first=False):
                    if not first:
                        dve.wait_ge(y_stored[dg % 2], 64 * b + 32 * (dg // 2))
                    for k in range(4):
                        pair, j = k // 2, k % 2
                        nn = NODE_SPLIT[j][1]
                        dve.wait_ge(front_filled, FILLS * (GROUPS * b + dg) + 4 + k + 1)
                        nc.vector.tensor_copy(y[0:nn, dg % 2, j, 2 * pair:2 * pair + 2, :],
                                              ps_front[0:nn, k % 2, :].rearrange("p (s t) -> p s t", s=2)
                                              ).then_inc(front_copied, 1)

                def copy_g(b, u, pair):
                    slot = (PAIRS * u + pair) % 2
                    dve.wait_ge(g_filled, CHUNKS * b + 2 * pair + 4)
                    dve.wait_ge(proj_done, PAIRS * b + pair + 1)
                    nc.vector.tensor_copy(g_sb[:, slot], ps_g[:, slot, :].rearrange("p (c t) -> p c t", c=2)
                                          ).then_inc(g_copied, 1)

                def copy_h(b, u):
                    dve.wait_ge(proj_done, PAIRS * (b + 1) + 2)
                    dve.wait_ge(h_free, b + 1)
                    for s in range(SUBS):
                        nc.vector.bn_stats(stats[:, bass.ds(b * SUBS + s, 1), :].squeeze(1), ps_h[:, s, :])
                    nc.vector.tensor_copy(h_out[:, u], ps_h[:]).then_inc(h_copied, 1)

                def run_block(b, u, ahead):
                    for step in range(CHUNKS + 1):
                        if ahead and step < 4 * GROUPS and step % 4 == 0:
                            copy_xT(b + 1, step // 4)
                        if ahead and step < 4 * GROUPS and step % 4 == 2:
                            copy_y(b + 1, step // 4)
                        if step >= 2 and step % 2 == 0:
                            copy_g(b, u, step // 2 - 1)
                    copy_h(b, u)

                for dg in range(GROUPS):
                    copy_xT(0, dg)
                    copy_y(0, dg, first=(dg < 2))
                with dve.Fori(0, BLOCKS - 2, 2) as b:
                    run_block(b, 0, True)
                    run_block(b + 1, 1, True)
                run_block(BLOCKS - 2, 0, True)
                run_block(BLOCKS - 1, 1, False)


class Chain:

    def __init__(self, eng, sem, base):
        self.eng, self.sem, self.base, self.n = eng, sem, base, 0

    def __call__(self, ins):
        self.n += 1
        ins.then_inc(self.sem, 1)
        self.eng.wait_ge(self.sem, self.base + self.n)


AB = 512
TILES = AB // P
ABLOCKS = TOK // AB
NTILES = TOK // P
IN_TILE = P // PATCH


def attention_block(nc, h_dram, W_in, b_in, Wq, Wk, Wv, W_out, b_out, ident, h, stats):
    QV = 2 * SLICE + 2 * DH
    with ExitStack() as ctx:
        def sb(name, shape, dt=F32):
            return ctx.enter_context(nc.sbuf_tensor(name, shape, dt))

        def psum(name, shape):
            return ctx.enter_context(nc.psum_tensor(name, shape, F32))

        def sem(name):
            return ctx.enter_context(nc.semaphore(name))

        w_in = sb("w_in", [P, KD, D])
        w_out = sb("w_out", [P, KD, D])
        wk_pair = sb("wk_pair", [P, 2 * SLICE])
        wqv_pair = sb("wqv_pair", [P, QV])
        b_in_row = sb("b_in_row", [KD, P])
        b_in_col = sb("b_in_col", [P, KD])
        b_out_all = sb("b_out_all", [P, D])
        same_batch = sb("same_batch", [P, 4, P])
        mean_var = sb("mean_var", [P, NTILES, 2])
        rstd = sb("rstd", [P, NTILES])
        hn = sb("hn", [P, TILES, D])
        hnT = sb("hnT", [P, KD, AB])
        xmT = sb("xmT", [P, KD, AB])
        k_exp = sb("k_exp", [P, 2, QUADS, AB])
        k_max = sb("k_max", [P, QUADS, AB // PATCH])
        k_inv = sb("k_inv", [P, 2, QUADS, AB // PATCH])
        qv = sb("qv", [P, 2, TILES, KD, QV])
        q_prob = sb("q_prob", [P, TILES, HEADS, SLICE])
        q_red = sb("q_red", [P, TILES, HEADS])
        qT_wide = sb("qT_wide", [P, 2, QUADS, 4, P])
        scores = sb("scores", [P, 2, QUADS, 4, P])
        oT = sb("oT", [P, 2, KD, P])

        ps_turn = psum("ps_turn", [P, 2, BANK])
        ps_proj = psum("ps_proj", [P, 2, BANK])
        ps_score = psum("ps_score", [P, QUADS, BANK])
        ps_oT = psum("ps_oT", [P, KD, P])
        ps_out = psum("ps_out", [P, D])

        h_loaded = [sem(f"h_loaded{i}") for i in range(2)]
        w_loaded = sem("w_loaded")
        cleared = sem("cleared")
        pair_loaded = sem("pair_loaded")
        masked_ones = sem("masked_ones")
        eps_ready = sem("eps_ready")
        stats_done = sem("stats_done")
        std_done = sem("std_done")
        setup = sem("setup")
        bias_turned = sem("bias_turned")
        bias_ready = sem("bias_ready")
        qT_cleared = sem("qT_cleared")
        normed = sem("normed")
        bias_added = sem("bias_added")
        turned = sem("turned")
        turn_copied = sem("turn_copied")
        proj_filled = sem("proj_filled")
        proj_copied = sem("proj_copied")
        k_centred = sem("k_centred")
        k_exped = sem("k_exped")
        k_ready = sem("k_ready")
        q_centred = sem("q_centred")
        q_exped = sem("q_exped")
        q_ready = sem("q_ready")
        soft = sem("soft")
        score_filled = sem("score_filled")
        score_masked = sem("score_masked")
        oT_filled = sem("oT_filled")
        oT_copied = sem("oT_copied")
        out_filled = sem("out_filled")
        out_added = sem("out_added")

        A_TURNS, B_TURNS = 6, 4
        TURNS = A_TURNS + B_TURNS
        PROJ = 3 * KD

        def turns_a(b):
            return TURNS * b - B_TURNS

        def turns_b(b):
            return TURNS * b + 2 * A_TURNS

        def turns_b_last(b):
            return TURNS * b + A_TURNS

        with nc.Block() as block:
            @block.sync
            def _(sp):
                for b in range(ABLOCKS):
                    sp.dma_start(h[:, b * TILES:(b + 1) * TILES, :],
                                 h_dram[b * AB:(b + 1) * AB, :].rearrange("(t p) n -> p t n", p=P)
                                 ).then_inc(h_loaded[0 if b == 0 else 1], 16)
                    if b == 0:
                        sp.dma_start(w_in[:], W_in.rearrange("(k p) n -> p k n", p=P)).then_inc(w_loaded, 16)
                        sp.dma_start(w_out[:], W_out.rearrange("(k p) n -> p k n", p=P)).then_inc(w_loaded, 16)
                        sp.dma_start(b_in_row[:], b_in.rearrange("(k p) -> k p", p=P)).then_inc(w_loaded, 16)
                        sp.dma_start(b_out_all[:], b_out.partition_broadcast(P)).then_inc(w_loaded, 16)

            @block.gpsimd
            def _(pool):
                nc.gpsimd.memset(wk_pair[:], 0.0).then_inc(cleared, 1)
                nc.gpsimd.memset(wqv_pair[:], 0.0).then_inc(cleared, 1)
                pool.wait_ge(cleared, 2)
                for i in range(2):
                    rows = slice(i * DH, (i + 1) * DH)
                    pool.dma_start(wk_pair[rows, i * SLICE:(i + 1) * SLICE], Wk).then_inc(pair_loaded, 16)
                    pool.dma_start(wqv_pair[rows, i * SLICE:(i + 1) * SLICE], Wq).then_inc(pair_loaded, 16)
                    pool.dma_start(wqv_pair[rows, 2 * SLICE + i * DH:2 * SLICE + (i + 1) * DH], Wv
                                   ).then_inc(pair_loaded, 16)
                nc.gpsimd.memset(same_batch[:], 1.0).then_inc(masked_ones, 1)
                for n, (step, base, mul) in enumerate(((-PATCH, 0, 1), (PATCH, PATCH - 1, -1))):
                    pool.wait_ge(masked_ones, n + 1)
                    v = same_batch[:].rearrange("p h (b s) -> p h b s", s=PATCH)
                    nc.gpsimd.affine_select(out=v, in_=v, compare_op=ALU.is_ge, fill=0.0, base=base,
                                            pattern=[[0, 4], [step, IN_TILE], [0, PATCH]],
                                            channel_multiplier=mul).then_inc(masked_ones, 1)
                pool.wait_ge(w_loaded, 64)
                with pool.Fori(0, ABLOCKS) as b:
                    pool.wait_ge(normed, b + 1)
                    rows = h[:, bass.ds(b * TILES, TILES), :]
                    nc.gpsimd.tensor_tensor(rows, rows, b_out_all[:].unsqueeze(1).broadcast_to([P, TILES, D]),
                                            ALU.add).then_inc(bias_added, 1)

            @block.tensor
            def _(pe):
                pe.sem_inc(oT_filled, 2)
                pe.sem_inc(out_filled, 2)
                pe.wait_ge(w_loaded, 64)
                nc.tensor.transpose(ps_out[:, 0:KD], b_in_row[:], ident[0:KD, 0:KD]).then_inc(bias_turned, 1)
                pe.wait_ge(pair_loaded, 96)
                pe.wait_ge(bias_ready, 1)

                def stage_a(b, turns, first=False):
                    pe.wait_ge(normed, b + 1)
                    for t in range(TILES):
                        if not (first and t < 2):
                            pe.wait_ge(turn_copied, turns + t - 1)
                        for k in range(KD):
                            last = nc.tensor.transpose(ps_turn[:, t % 2, k * P:(k + 1) * P],
                                                       hn[:, t, k * P:(k + 1) * P], ident[:])
                        last.then_inc(turned, 1)
                    pe.wait_ge(turn_copied, turns + TILES)
                    for i in range(KD):
                        if not (first and i < 2):
                            pe.wait_ge(proj_copied, PROJ * b + i - 1)
                        for k in range(KD):
                            last = nc.tensor.matmul(ps_proj[:, i % 2, :], w_in[:, k, i * P:(i + 1) * P],
                                                    hnT[:, k, :], start=(k == 0), stop=(k == KD - 1))
                        last.then_inc(proj_filled, 1)
                    pe.wait_ge(proj_copied, PROJ * b + KD)
                    for quad in range(QUADS):
                        for i in range(2):
                            last = nc.tensor.matmul(ps_turn[i * DH:(i + 1) * DH, quad, :], wk_pair[:],
                                                    xmT[:, 2 * quad + i, :], start=True, stop=True)
                        last.then_inc(turned, 1)
                    for t in range(TILES):
                        for half in range(2):
                            n = KD + 2 * t + half
                            pe.wait_ge(proj_copied, PROJ * b + n - 1)
                            for i in range(2):
                                last = nc.tensor.matmul(ps_proj[:, n % 2, i * QV:(i + 1) * QV],
                                                        xmT[:, 2 * half + i, t * P:(t + 1) * P], wqv_pair[:],
                                                        start=True, stop=True)
                            last.then_inc(proj_filled, 1)

                def stage_b(b, u, turns):
                    def turn_q(t):
                        if t == 0:
                            pe.wait_ge(q_ready, b + 1)
                        pe.wait_ge(turn_copied, turns + t - 1)
                        for quad in range(QUADS):
                            last = nc.tensor.transpose(
                                ps_turn[:, t % 2, quad * P:(quad + 1) * P],
                                q_prob[:, t, 4 * quad:4 * quad + 4, :].rearrange("p h s -> p (h s)"), ident[:])
                        last.then_inc(turned, 1)

                    def score(t):
                        if t == 0:
                            pe.wait_ge(k_ready, b + 1)
                        pe.wait_ge(turn_copied, turns + t + 1)
                        for quad in range(QUADS):
                            n = 2 * TILES * b + 2 * t + quad
                            pe.wait_ge(score_masked, n + 1)
                            nc.tensor.matmul(ps_score[:, quad, :], k_exp[:, u, quad, t * P:(t + 1) * P],
                                             qT_wide[:, t % 2, quad].rearrange("p h t -> p (h t)"),
                                             start=True, stop=True).then_inc(score_filled, 1)

                    def mix(t):
                        pe.wait_ge(score_masked, 2 * TILES * b + 2 * t + 4)
                        pe.wait_ge(oT_copied, TILES * b + t + 1)
                        for head in range(HEADS):
                            i, r = head // 2, head % 2
                            last = nc.tensor.matmul(
                                ps_oT[r * DH:(r + 1) * DH, i, :],
                                qv[:, u, t, i, 2 * SLICE + r * DH:2 * SLICE + (r + 1) * DH],
                                scores[:, t % 2, head // 4, head % 4, :], start=True, stop=True)
                        last.then_inc(oT_filled, 1)

                    def out(t):
                        pe.wait_ge(oT_copied, TILES * b + t + 2)
                        pe.wait_ge(out_added, TILES * b + t + 1)
                        for i in range(KD):
                            last = nc.tensor.matmul(ps_out[:], oT[:, t % 2, i, :], w_out[:, i, :],
                                                    start=(i == 0), stop=(i == KD - 1))
                        last.then_inc(out_filled, 1)

                    for step in range(TILES + 3):
                        if step < TILES:
                            turn_q(step)
                        if 1 <= step <= TILES:
                            score(step - 1)
                        if 2 <= step <= TILES + 1:
                            mix(step - 2)
                        if step >= 3:
                            out(step - 3)

                stage_a(0, 0, first=True)
                with pe.Fori(0, ABLOCKS // 2 - 1) as pair:
                    b = 2 * pair
                    for u in range(2):
                        stage_a(b + u + 1, turns_a(b + u + 1))
                        stage_b(b + u, u, turns_b(b + u))
                stage_a(ABLOCKS - 1, turns_a(ABLOCKS - 1))
                stage_b(ABLOCKS - 2, 0, turns_b(ABLOCKS - 2))
                stage_b(ABLOCKS - 1, 1, turns_b_last(ABLOCKS - 1))

            @block.scalar
            def _(act):
                act.sem_inc(oT_copied, 1)
                act.wait_ge(stats_done, 1)
                nc.scalar.activation(rstd[:], rstd[:], ACT.Sqrt).then_inc(std_done, 1)
                act.wait_ge(bias_ready, 1)

                def stage_a(b, first=False):
                    for i in range(KD):
                        act.wait_ge(proj_filled, PROJ * b + i + 1)
                        nc.scalar.activation(xmT[:, i, :], ps_proj[:, i % 2, :], ACT.Identity,
                                             bias=b_in_col[:, i:i + 1]).then_inc(proj_copied, 1)

                def exp_q(b):
                    act.wait_ge(q_centred, b + 1)
                    nc.scalar.activation(q_prob[:], q_prob[:], ACT.Exp).then_inc(q_exped, 1)

                def exp_k_copy_qv(b, u):
                    for quad in range(QUADS):
                        act.wait_ge(k_centred, 2 * b + quad + 1)
                        nc.scalar.activation(k_exp[:, u, quad, :], k_exp[:, u, quad, :], ACT.Exp
                                             ).then_inc(k_exped, 1)
                    for t in range(TILES):
                        for half in range(2):
                            n = KD + 2 * t + half
                            act.wait_ge(proj_filled, PROJ * b + n + 1)
                            nc.scalar.copy(qv[:, u, t, 2 * half:2 * half + 2, :],
                                           ps_proj[:, n % 2, 0:2 * QV].rearrange("p (i c) -> p i c", i=2)
                                           ).then_inc(proj_copied, 1)

                def stage_b(b):
                    for t in range(TILES):
                        n = TILES * b + t
                        act.wait_ge(oT_filled, n + 3)
                        act.wait_ge(out_filled, n + 1)
                        nc.scalar.copy(oT[:, t % 2], ps_oT[:]).then_inc(oT_copied, 1)

                stage_a(0)
                exp_k_copy_qv(0, 0)
                with act.Fori(0, ABLOCKS // 2 - 1) as pair:
                    b = 2 * pair
                    for u in range(2):
                        stage_a(b + u + 1)
                        exp_q(b + u)
                        exp_k_copy_qv(b + u + 1, 1 - u)
                        stage_b(b + u)
                stage_a(ABLOCKS - 1)
                exp_q(ABLOCKS - 2)
                exp_k_copy_qv(ABLOCKS - 1, 1)
                stage_b(ABLOCKS - 2)
                exp_q(ABLOCKS - 1)
                stage_b(ABLOCKS - 1)

            @block.vector
            def _(dve):
                dve.sem_inc(score_masked, 2)
                dve.sem_inc(out_added, 1)
                nc.vector.memset(qT_wide[:], 0.0).then_inc(qT_cleared, 1)
                for t in range(NTILES):
                    last = nc.vector.bn_aggr(mean_var[:, t, :], stats[:, t, :])
                last.then_inc(setup, 1)
                dve.wait_ge(setup, 1)
                nc.vector.tensor_scalar(rstd[:], mean_var[:, :, 1], EPS, None, ALU.add).then_inc(stats_done, 1)
                dve.wait_ge(bias_turned, 1)
                nc.vector.tensor_copy(b_in_col[:], ps_out[:, 0:KD]).then_inc(bias_ready, 1)
                dve.wait_ge(std_done, 1)
                nc.vector.reciprocal(rstd[:], rstd[:]).then_inc(setup, 1)
                dve.wait_ge(setup, 2)
                dve.wait_ge(qT_cleared, 1)

                def layernorm(b):
                    for t in range(TILES):
                        n = b * TILES + t
                        last = nc.vector.tensor_scalar(hn[:, t, :], h[:, bass.ds(n, 1), :].squeeze(1),
                                                       mean_var[:, bass.ds(n, 1), 0], rstd[:, bass.ds(n, 1)],
                                                       ALU.subtract, ALU.mult)
                    last.then_inc(normed, 1)

                def copy_hnT(b, turns):
                    for t in range(TILES):
                        dve.wait_ge(turned, turns + t + 1)
                        nc.vector.tensor_copy(hnT[:, :, t * P:(t + 1) * P],
                                              ps_turn[:, t % 2, :].rearrange("p (k t) -> p k t", k=KD)
                                              ).then_inc(turn_copied, 1)

                def centre_q(b, u, chain):
                    q = qv[:, u, :, :, 0:2 * SLICE].rearrange("p t i (h s) -> p (t i) h s", s=SLICE)
                    dve.wait_ge(proj_copied, PROJ * b + PROJ)
                    red = q_red[:].rearrange("p t (i h) -> p (t i) h", h=2)
                    chain(nc.vector.tensor_reduce(red, q, AX.X, ALU.max))
                    nc.vector.tensor_tensor(q_prob[:].rearrange("p t (i h) s -> p (t i) h s", h=2), q,
                                            red.unsqueeze(3).broadcast_to([P, TILES * KD, 2, SLICE]), ALU.subtract
                                            ).then_inc(q_centred, 1)

                def centre_k(b, u, turns, chain):
                    for quad in range(QUADS):
                        dve.wait_ge(turned, turns + TILES + quad + 1)
                        k = ps_turn[:, quad, :].rearrange("p (b s) -> p b s", s=PATCH)
                        chain(nc.vector.tensor_reduce(k_max[:, quad, :], k, AX.X, ALU.max))
                        nc.vector.tensor_tensor(k_exp[:, u, quad, :].rearrange("p (b s) -> p b s", s=PATCH), k,
                                                k_max[:, quad, :].unsqueeze(2).broadcast_to([P, AB // PATCH, PATCH]),
                                                ALU.subtract).then_inc(k_centred, 1)
                        dve.wait_ge(k_centred, 2 * b + quad + 1)
                        dve.sem_inc(turn_copied, 1)

                def norm_q(b, chain):
                    dve.wait_ge(q_exped, b + 1)
                    q = q_prob[:].rearrange("p t h s -> p (t h) s")
                    red = q_red[:].rearrange("p t h -> p (t h)")
                    chain(nc.vector.tensor_reduce(red, q, AX.X, ALU.add))
                    chain(nc.vector.reciprocal(red, red))
                    nc.vector.tensor_tensor(q, q, red.unsqueeze(2).broadcast_to([P, TILES * HEADS, SLICE]), ALU.mult
                                            ).then_inc(q_ready, 1)

                def norm_k(b, u, chain):
                    dve.wait_ge(k_exped, 2 * b + 2)
                    k = k_exp[:, u].rearrange("p q (b s) -> p (q b) s", s=PATCH)
                    inv = k_inv[:, u].rearrange("p q b -> p (q b)")
                    chain(nc.vector.tensor_reduce(inv, k, AX.X, ALU.add))
                    nc.vector.reciprocal(inv, inv).then_inc(k_ready, 1)

                def stage_b(b, u, turns):
                    def spread_q(t):
                        dve.wait_ge(turned, turns + t + 1)
                        for quad in range(QUADS):
                            for r in range(4):
                                rows = slice(32 * r, 32 * r + 32)
                                inv = k_inv[rows, u, quad, t * IN_TILE:(t + 1) * IN_TILE]
                                last = nc.vector.tensor_tensor(
                                    qT_wide[rows, t % 2, quad, r, :].rearrange("p (b s) -> p b s", s=PATCH),
                                    ps_turn[rows, t % 2, quad * P:(quad + 1) * P].rearrange("p (b s) -> p b s", s=PATCH),
                                    inv.unsqueeze(2).broadcast_to([32, IN_TILE, PATCH]), ALU.mult)
                        last.then_inc(turn_copied, 1)

                    def mask(t):
                        dve.wait_ge(oT_filled, TILES * b + t + 1)
                        for quad in range(QUADS):
                            dve.wait_ge(score_filled, 2 * TILES * b + 2 * t + quad + 1)
                            nc.vector.tensor_tensor(scores[:, t % 2, quad],
                                                    ps_score[:, quad, :].rearrange("p (h t) -> p h t", h=4),
                                                    same_batch[:], ALU.mult).then_inc(score_masked, 1)

                    def add_out(t):
                        n = TILES * b + t
                        if t == 0:
                            dve.wait_ge(bias_added, b + 1)
                        dve.wait_ge(out_filled, n + 3)
                        rows = h[:, bass.ds(n, 1), :].squeeze(1)
                        nc.vector.tensor_tensor(rows, ps_out[:], rows, ALU.add).then_inc(out_added, 1)
                        dve.wait_ge(out_added, n + 2)
                        nc.vector.bn_stats(stats[:, bass.ds(n, 1), :].squeeze(1), rows).then_inc(setup, 1)

                    dve.wait_ge(k_ready, b + 1)
                    for step in range(TILES + 3):
                        if step < TILES:
                            spread_q(step)
                        if 1 <= step <= TILES:
                            mask(step - 1)
                        if step >= 3:
                            add_out(step - 3)

                CHAIN = 6
                dve.wait_ge(h_loaded[0], 16)
                layernorm(0)
                copy_hnT(0, 0)
                dve.wait_ge(h_loaded[1], 16 * (ABLOCKS - 1))
                layernorm(1)
                chain = Chain(dve, soft, 0)
                centre_k(0, 0, 0, chain)
                norm_k(0, 0, chain)
                START = chain.n
                dve.wait_ge(masked_ones, 3)

                def both(b, u, ahead):
                    chain = Chain(dve, soft, CHAIN * b + START)
                    copy_hnT(b + 1, turns_a(b + 1))
                    centre_q(b, u, chain)
                    centre_k(b + 1, 1 - u, turns_a(b + 1), chain)
                    norm_q(b, chain)
                    norm_k(b + 1, 1 - u, chain)
                    if ahead:
                        layernorm(b + 2)
                    stage_b(b, u, turns_b(b))
                    assert chain.n == CHAIN

                with dve.Fori(0, ABLOCKS // 2 - 1) as pair:
                    b = 2 * pair
                    both(b, 0, True)
                    both(b + 1, 1, True)
                both(ABLOCKS - 2, 0, False)
                chain = Chain(dve, soft, CHAIN * (ABLOCKS - 1) + START)
                centre_q(ABLOCKS - 1, 1, chain)
                norm_q(ABLOCKS - 1, chain)
                stage_b(ABLOCKS - 1, 1, turns_b_last(ABLOCKS - 1))


def routing_block(nc, gate_w, ident, h, stats, row_dram, aff_dram, out_rows):
    with ExitStack() as ctx:
        def sb(name, shape, dt=F32):
            return ctx.enter_context(nc.sbuf_tensor(name, shape, dt))

        def psum(name, shape):
            return ctx.enter_context(nc.psum_tensor(name, shape, F32))

        def sem(name):
            return ctx.enter_context(nc.semaphore(name))

        gate = sb("gate", [P, KD, EXPERTS])
        mean_var = sb("mean_var2", [P, NTILES, 2])
        rstd = sb("rstd2", [P, NTILES])
        hn = sb("hn2", [P, 2, TILES, D])
        hnT = sb("hnT2", [P, 2, KD, P])
        affinity = sb("affinity", [P, NTILES, EXPERTS])
        red = sb("aff_red", [P, NTILES])
        ps_turn = psum("ps_turn2", [P, 2, KD, P])
        ps_logit = psum("ps_logit", [P, 2, BANK])

        gate_loaded = sem("gate_loaded")
        resid_stored = sem("resid_stored")
        setup = sem("setup2")
        var_ready = sem("var_ready")
        std_done = sem("std_done2")
        normed = sem("normed2")
        row_stored = sem("row_stored")
        row_free = sem("row_free")
        turned = sem("turned2")
        turn_copied = sem("turn_copied2")
        logit_done = sem("logit_done")
        logit_copied = sem("logit_copied")
        centred = sem("centred2")
        exped = sem("exped2")
        aff_ready = sem("aff_ready")
        aff_stored = sem("aff_stored")

        with nc.Block() as block:
            @block.sync
            def _(sp):
                sp.dma_start(gate[:], gate_w.rearrange("(k p) e -> p k e", p=P)).then_inc(gate_loaded, 16)
                rows = row_dram.rearrange("(b t p) n -> b p t n", p=P, t=TILES)

                def store_rows(b, u):
                    sp.wait_ge(normed, b + 1)
                    sp.dma_start(rows[b], hn[:, u]).then_inc(row_stored, 16)
                    sp.wait_ge(row_stored, 16 * b + 16)
                    sp.sem_inc(row_free, 1)

                with sp.Fori(0, ABLOCKS // 2) as pair:
                    for u in range(2):
                        store_rows(2 * pair + u, u)
                sp.dma_start(out_rows.rearrange("(t p) n -> p t n", p=P), h[:]).then_inc(resid_stored, 16)
                sp.wait_ge(aff_ready, 1)
                sp.dma_start(aff_dram.rearrange("(t p) e -> p t e", p=P), affinity[:]).then_inc(aff_stored, 16)
                sp.wait_ge(aff_stored, 16)
                sp.wait_ge(resid_stored, 16)

            @block.tensor
            def _(pe):
                pe.wait_ge(gate_loaded, 16)

                def turn(b, u, t):
                    if t == 0:
                        pe.wait_ge(normed, b + 1)
                    pe.wait_ge(turn_copied, TILES * b + t + 1)
                    for k in range(KD):
                        last = nc.tensor.transpose(ps_turn[:, t % 2, k, :], hn[:, u, t, k * P:(k + 1) * P], ident[:])
                    last.then_inc(turned, 1)

                def logits(b, t):
                    pe.wait_ge(turn_copied, TILES * b + t + 3)
                    pe.wait_ge(logit_copied, TILES * b + t + 1)
                    for k in range(KD):
                        last = nc.tensor.matmul(ps_logit[:, t % 2, 0:EXPERTS], hnT[:, t % 2, k, :], gate[:, k, :],
                                                start=(k == 0), stop=(k == KD - 1))
                    last.then_inc(logit_done, 1)

                with pe.Fori(0, ABLOCKS // 2) as pair:
                    for u in range(2):
                        for t in range(TILES + 1):
                            if t < TILES:
                                turn(2 * pair + u, u, t)
                            if t:
                                logits(2 * pair + u, t - 1)

            @block.scalar
            def _(act):
                act.sem_inc(turn_copied, 2)
                act.wait_ge(var_ready, 1)
                nc.scalar.activation(rstd[:], rstd[:], ACT.Sqrt).then_inc(std_done, 1)
                with act.Fori(0, ABLOCKS) as b:
                    for t in range(TILES):
                        act.wait_ge(turned, TILES * b + t + 1)
                        nc.scalar.copy(hnT[:, t % 2], ps_turn[:, t % 2]).then_inc(turn_copied, 1)
                act.wait_ge(centred, 1)
                nc.scalar.activation(affinity[:], affinity[:], ACT.Exp).then_inc(exped, 1)

            @block.vector
            def _(dve):
                dve.sem_inc(logit_copied, 2)
                dve.sem_inc(row_free, 2)
                for t in range(NTILES):
                    last = nc.vector.bn_aggr(mean_var[:, t, :], stats[:, t, :])
                last.then_inc(setup, 1)
                dve.wait_ge(setup, 1)
                nc.vector.tensor_scalar(rstd[:], mean_var[:, :, 1], EPS, None, ALU.add).then_inc(var_ready, 1)
                dve.wait_ge(std_done, 1)
                nc.vector.reciprocal(rstd[:], rstd[:]).then_inc(setup, 1)
                dve.wait_ge(setup, 2)

                def layernorm(b, u):
                    dve.wait_ge(row_free, b + 1)
                    for t in range(TILES):
                        n = b * TILES + t
                        last = nc.vector.tensor_scalar(hn[:, u, t, :], h[:, bass.ds(n, 1), :].squeeze(1),
                                                       mean_var[:, bass.ds(n, 1), 0], rstd[:, bass.ds(n, 1)],
                                                       ALU.subtract, ALU.mult)
                    last.then_inc(normed, 1)

                def copy_logits(b):
                    for t in range(TILES):
                        n = b * TILES + t
                        dve.wait_ge(logit_done, n + 1)
                        nc.vector.tensor_copy(affinity[:, bass.ds(n, 1), :].squeeze(1),
                                              ps_logit[:, t % 2, 0:EXPERTS]).then_inc(logit_copied, 1)

                layernorm(0, 0)
                with dve.Fori(0, ABLOCKS // 2 - 1) as pair:
                    layernorm(2 * pair + 1, 1)
                    copy_logits(2 * pair)
                    layernorm(2 * pair + 2, 0)
                    copy_logits(2 * pair + 1)
                layernorm(ABLOCKS - 1, 1)
                copy_logits(ABLOCKS - 2)
                copy_logits(ABLOCKS - 1)
                dve.wait_ge(logit_copied, NTILES + 2)
                wide = [P, NTILES, EXPERTS]
                chain = Chain(dve, setup, 2)
                chain(nc.vector.tensor_reduce(red[:], affinity[:], AX.X, ALU.max))
                nc.vector.tensor_tensor(affinity[:], affinity[:], red[:].unsqueeze(2).broadcast_to(wide),
                                        ALU.subtract).then_inc(centred, 1)
                dve.wait_ge(exped, 1)
                chain(nc.vector.tensor_reduce(red[:], affinity[:], AX.X, ALU.add))
                chain(nc.vector.reciprocal(red[:], red[:]))
                nc.vector.tensor_tensor(affinity[:], affinity[:], red[:].unsqueeze(2).broadcast_to(wide),
                                        ALU.mult).then_inc(aff_ready, 1)


HALVES = BATCH // P
PICKS = TOP * HALVES


def choice_block(nc, aff_dram, row_index, weight):
    with ExitStack() as ctx:
        def sb(name, shape, dt=F32):
            return ctx.enter_context(nc.sbuf_tensor(name, shape, dt))

        def sem(name):
            return ctx.enter_context(nc.semaphore(name))

        wide = [P, HALVES, EXPERTS, PATCH]
        a = sb("aff_in", [P, HALVES, PATCH, EXPERTS])
        by_expert = sb("by_expert", wide)
        best = sb("best", [P, HALVES, EXPERTS])
        place = sb("place", [P, HALVES, EXPERTS])
        hit = sb("hit", wide)
        countdown = sb("countdown", [P, PATCH])
        row_end = sb("row_end", [P, HALVES])
        row_float = sb("row_float", [P, EXPERTS, TOP, HALVES])
        loaded = sem("aff_loaded")
        ramps = sem("ramps")
        picked = sem("picked")

        with nc.Block() as block:
            @block.sync
            def _(sp):
                sp.dma_start(a[:], aff_dram.rearrange("(c p s) e -> p c s e", s=PATCH, p=P)).then_inc(loaded, 16)

            @block.gpsimd
            def _(pool):
                nc.gpsimd.iota(countdown[:], [[-1, PATCH]], base=PATCH, channel_multiplier=0,
                               allow_small_or_imprecise_dtypes=True).then_inc(ramps, 1)
                nc.gpsimd.iota(row_end[:], [[P * PATCH, HALVES]], base=PATCH, channel_multiplier=PATCH,
                               allow_small_or_imprecise_dtypes=True).then_inc(ramps, 1)

            @block.vector
            def _(dve):
                dve.wait_ge(loaded, 16)
                dve.wait_ge(ramps, 2)
                chain = Chain(dve, picked, 0)
                chain(nc.vector.tensor_copy(by_expert[:], a[:].rearrange("p c s e -> p c e s")))
                flat = "p c e s -> p (c e s)"
                for r in range(TOP):
                    chain(nc.vector.tensor_reduce(best[:], by_expert[:], AX.X, ALU.max))
                    chain(nc.vector.tensor_tensor(hit[:], by_expert[:], best[:].unsqueeze(3).broadcast_to(wide),
                                                  ALU.is_equal))
                    ramp = countdown[:].unsqueeze(1).unsqueeze(1).broadcast_to(wide)
                    chain(nc.vector.tensor_tensor(hit[:], hit[:], ramp, ALU.mult))
                    chain(nc.vector.tensor_reduce(place[:], hit[:], AX.X, ALU.max))
                    nc.vector.tensor_copy(weight[:, :, r, :], best[:].rearrange("p c e -> p e c"))
                    chain(nc.vector.tensor_tensor(row_float[:, :, r, :],
                                                  row_end[:].unsqueeze(1).broadcast_to([P, EXPERTS, HALVES]),
                                                  place[:].rearrange("p c e -> p e c"), ALU.subtract))
                    if r < TOP - 1:
                        chain(nc.vector.tensor_tensor(hit[:], ramp, place[:].unsqueeze(3).broadcast_to(wide),
                                                      ALU.is_equal))
                        chain(nc.vector.scalar_tensor_tensor(
                            by_expert[:].rearrange(flat), hit[:].rearrange(flat), -4.0,
                            by_expert[:].rearrange(flat), ALU.mult, ALU.add))
                chain(nc.vector.tensor_copy(row_index[:], row_float[:]))


def expert_block(nc, w1, b1, w2, b2, ident, row_index, weight, row_dram, out_rows):
    with ExitStack() as ctx:
        def sb(name, shape, dt=F32):
            return ctx.enter_context(nc.sbuf_tensor(name, shape, dt))

        def psum(name, shape):
            return ctx.enter_context(nc.psum_tensor(name, shape, F32))

        def sem(name):
            return ctx.enter_context(nc.semaphore(name))

        w1_sb = sb("w1_sb", [P, 2, KD, D])
        w2_sb = sb("w2_sb", [P, 2, KD, D])
        b2_sb = sb("b2_sb", [P, 2, D])
        b1_rows = sb("b1_rows", [EXPERTS * KD, P])
        b1_col = sb("b1_col", [P, EXPERTS, KD])
        index = sb("index", [P, 2, PICKS], I32)
        picked = sb("picked", [P, 2, PICKS, D])
        xT = sb("pickedT", [P, KD, PICKS * P])
        hiddenT = sb("hiddenT", [P, KD, PICKS * P])
        result = sb("result", [P, 2, PICKS, D])
        ps_turn = psum("ps_turn3", [P, 2, KD, P])
        ps_hid = psum("ps_hid3", [P, 2, PICKS * P])
        ps_out = psum("ps_out3", [P, 2, D])

        w_loaded = [sem(f"w_loaded{s}") for s in range(2)]
        b1_loaded = sem("b1_loaded")
        b1_turned = sem("b1_turned")
        b1_ready = sem("b1_ready")
        index_ready = sem("index_ready")
        gathered = [sem(f"gathered{s}") for s in range(2)]
        scattered = sem("scattered")
        turned = sem("turned3")
        turn_copied = sem("turn_copied3")
        hid_done = sem("hid_done")
        gelu_done = sem("gelu_done3")
        out_done = sem("out_done")
        out_copied = sem("out_copied")
        weighted = sem("weighted")
        waits_passed = sem("waits_passed")
        result_free = sem("result_free")

        with nc.Block() as block:
            @block.sync
            def _(sp):
                sp.dma_start(b1_rows[:], b1.rearrange("e (k p) -> (e k) p", p=P)).then_inc(b1_loaded, 16)
                b2_row = b2.rearrange("(e a) n -> e a n", a=1)

                def load(e, u):
                    sp.dma_start(w1_sb[:, u], w1[e].rearrange("(k p) n -> p k n", p=P)).then_inc(w_loaded[u], 16)
                    sp.dma_start(w2_sb[:, u], w2[e].rearrange("(k p) n -> p k n", p=P)).then_inc(w_loaded[u], 16)
                    sp.dma_start(b2_sb[:, u], b2_row[e].broadcast_to([P, D])).then_inc(w_loaded[u], 16)

                load(0, 0)
                load(1, 1)
                with sp.Fori(1, EXPERTS // 2) as pair:
                    for u in range(2):
                        sp.wait_ge(out_copied, PICKS * (2 * pair + u - 1) + 2)
                        load(2 * pair + u, u)

            @block.gpsimd
            def _(pool):
                def gather(e, u):
                    nc.gpsimd.tensor_copy(index[:, u], row_index[:, bass.ds(e, 1)].rearrange("p e r c -> p (e r c)")
                                          ).then_inc(index_ready, 1)
                    pool.wait_ge(index_ready, e + 1)
                    pool.sem_inc(waits_passed, 1)
                    for j in range(PICKS):
                        nc.gpsimd.indirect_dma_start(
                            picked[:, u, j, :], None, row_dram,
                            bass.IndirectOffsetOnAxis(ap=index[:, u, j:j + 1].bitcast(U32), axis=0)
                        ).then_inc(gathered[u], 16)

                def scatter(e, u):
                    for j in range(PICKS):
                        pool.wait_ge(weighted, PICKS * e + j + 1)
                        pool.sem_inc(waits_passed, 1)
                        nc.gpsimd.indirect_dma_start(
                            out_rows, bass.IndirectOffsetOnAxis(ap=index[:, u, j:j + 1].bitcast(U32), axis=0),
                            result[:, u, j, :], None, compute_op=ALU.add).then_inc(scattered, 16)

                def run(e, u, ahead):
                    scatter(e, u)
                    pool.wait_ge(scattered, 16 * PICKS * (e + 1))
                    pool.sem_inc(result_free, 1)
                    if ahead:
                        pool.wait_ge(turned, PICKS * (e + 1))
                        gather(e + 2, u)

                gather(0, 0)
                gather(1, 1)
                with pool.Fori(0, EXPERTS // 2 - 1) as pair:
                    for u in range(2):
                        run(2 * pair + u, u, True)
                run(EXPERTS - 2, 0, False)
                run(EXPERTS - 1, 1, False)

            @block.tensor
            def _(pe):
                pe.wait_ge(b1_loaded, 16)
                nc.tensor.transpose(ps_out[:, 0, 0:EXPERTS * KD], b1_rows[:], ident[0:EXPERTS * KD, 0:EXPERTS * KD]
                                    ).then_inc(b1_turned, 1)
                pe.wait_ge(b1_ready, 1)

                def turn(e, u):
                    pe.wait_ge(gathered[u], 8 * PICKS * (e - u) + 16 * PICKS)
                    for j in range(PICKS):
                        pe.wait_ge(turn_copied, PICKS * e + j + 1)
                        for k in range(KD):
                            last = nc.tensor.transpose(ps_turn[:, j % 2, k, :], picked[:, u, j, k * P:(k + 1) * P],
                                                       ident[:])
                        last.then_inc(turned, 1)

                def up(e, u):
                    pe.wait_ge(turn_copied, PICKS * e + PICKS + 2)
                    pe.wait_ge(w_loaded[u], 24 * (e - u) + 48)
                    for m in range(KD):
                        pe.wait_ge(gelu_done, KD * e + m + 1)
                        for k in range(KD):
                            last = nc.tensor.matmul(ps_hid[:, m % 2, :], w1_sb[:, u, k, m * P:(m + 1) * P],
                                                    xT[:, k, :], start=(k == 0), stop=(k == KD - 1))
                        last.then_inc(hid_done, 1)

                def down(e, u):
                    pe.wait_ge(gelu_done, KD * e + KD + 2)
                    for j in range(PICKS):
                        pe.wait_ge(out_copied, PICKS * e + j + 1)
                        for k in range(KD):
                            last = nc.tensor.matmul(ps_out[:, j % 2, :], hiddenT[:, k, j * P:(j + 1) * P],
                                                    w2_sb[:, u, k, :], start=(k == 0), stop=(k == KD - 1))
                        last.then_inc(out_done, 1)

                turn(0, 0)
                with pe.Fori(0, EXPERTS // 2 - 1) as pair:
                    for u in range(2):
                        up(2 * pair + u, u)
                        turn(2 * pair + u + 1, 1 - u)
                        down(2 * pair + u, u)
                up(EXPERTS - 2, 0)
                turn(EXPERTS - 1, 1)
                down(EXPERTS - 2, 0)
                up(EXPERTS - 1, 1)
                down(EXPERTS - 1, 1)

            @block.scalar
            def _(act):
                act.sem_inc(gelu_done, 2)
                act.wait_ge(b1_ready, 1)

                def weigh(e, u):
                    for j in range(PICKS):
                        act.wait_ge(out_copied, PICKS * e + j + 3)
                        scale = weight[:, bass.ds(e, 1)].rearrange("p e r c -> p (e r c)")[:, j:j + 1]
                        nc.scalar.activation(result[:, u, j, :], result[:, u, j, :], ACT.Copy, scale=scale
                                             ).then_inc(weighted, 1)

                def gelu(e):
                    for m in range(KD):
                        act.wait_ge(hid_done, KD * e + m + 1)
                        nc.scalar.activation(hiddenT[:, m, :], ps_hid[:, m % 2, :], ACT.Gelu_apprx_tanh,
                                             bias=b1_col[:, bass.ds(e, 1), m]).then_inc(gelu_done, 1)

                with act.Fori(0, EXPERTS // 2) as pair:
                    for u in range(2):
                        gelu(2 * pair + u)
                        weigh(2 * pair + u, u)

            @block.vector
            def _(dve):
                dve.sem_inc(turn_copied, 2)
                dve.sem_inc(out_copied, 2)
                dve.sem_inc(result_free, 2)
                dve.wait_ge(b1_turned, 1)
                nc.vector.tensor_copy(b1_col[:].rearrange("p e k -> p (e k)"), ps_out[:, 0, 0:EXPERTS * KD]
                                      ).then_inc(b1_ready, 1)

                def copy_turned(e):
                    for j in range(PICKS):
                        dve.wait_ge(turned, PICKS * e + j + 1)
                        nc.vector.tensor_copy(xT[:, :, j * P:(j + 1) * P], ps_turn[:, j % 2]).then_inc(turn_copied, 1)

                def copy_out(e, u):
                    dve.wait_ge(result_free, e + 1)
                    for j in range(PICKS):
                        dve.wait_ge(out_done, PICKS * e + j + 1)
                        nc.vector.tensor_tensor(result[:, u, j, :], ps_out[:, j % 2, :], b2_sb[:, u, :], ALU.add
                                                ).then_inc(out_copied, 1)

                copy_turned(0)
                copy_turned(1)
                copy_out(0, 0)
                with dve.Fori(0, EXPERTS // 2 - 1) as pair:
                    for u in range(2):
                        copy_turned(2 * pair + u + 2)
                        copy_out(2 * pair + u + 1, 1 - u)
                copy_out(EXPERTS - 1, 1)


def audio_tower(nc, x, adj, tok_w1, tok_w2, wp, W_in, b_in, Wq, Wk, Wv, W_out, b_out, gate_w, w1, b1, w2, b2, out):
    def scratch(name, shape):
        return nc.dram_tensor(name, shape, F32, kind="Internal").ap()

    wfold_dram = scratch("wfold_dram", [NPAD * PATCH, D])
    y_dram = scratch("y_dram", [BLOCKS, NPAD, PATCH, TB])
    h_dram = scratch("h_dram", [TOK, D])
    row_dram = scratch("row_dram", [TOK, D])
    aff_dram = scratch("aff_dram", [TOK, EXPERTS])
    out_rows = out.rearrange("b p n -> (b p) n")

    with ExitStack() as whole:
        def sb(ctx, name, shape, dt=F32):
            return ctx.enter_context(nc.sbuf_tensor(name, shape, dt))

        ident = sb(whole, "ident", [P, P])
        stats = sb(whole, "stats", [P, NTILES, 6])
        row_index = sb(whole, "row_index", [P, EXPERTS, TOP, HALVES], I32)
        weight = sb(whole, "weight", [P, EXPERTS, TOP, HALVES])
        with ExitStack() as ctx:
            adjT = sb(ctx, "adjT", [P, WINDOWS, NPAD])
            w1big = sb(ctx, "w1big", [P, 4, P])
            w2pair = sb(ctx, "w2pair", [P, 32])
            wfold = sb(ctx, "wfold", [P, CHUNKS, D])
            fold_block(nc, adj, wp, tok_w1, tok_w2, wfold_dram, ident, adjT, w1big, w2pair, wfold)
            tokenizer_block(nc, x, y_dram, h_dram, ident, adjT, w1big, w2pair, wfold, stats)
        with ExitStack() as ctx:
            h = sb(ctx, "h", [P, NTILES, D])
            attention_block(nc, h_dram, W_in, b_in, Wq, Wk, Wv, W_out, b_out, ident, h, stats)
            routing_block(nc, gate_w, ident, h, stats, row_dram, aff_dram, out_rows)
        choice_block(nc, aff_dram, row_index, weight)
        expert_block(nc, w1, b1, w2, b2, ident, row_index, weight, row_dram, out_rows)


_INS = ['x', 'L0_tok_adj', 'L0_tok_w1', 'L0_tok_w2', 'L0_tok_wp', 'L0_attn_W_in', 'L0_attn_b_in', 'L0_attn_Wq',
        'L0_attn_Wk', 'L0_attn_Wv', 'L0_attn_W_out', 'L0_attn_b_out', 'L0_ffn_gate_weight', 'L0_ffn_w1',
        'L0_ffn_b1', 'L0_ffn_w2', 'L0_ffn_b2']
_OUT = ((BATCH, PATCH, D), 'float32')


def kernel(**inputs):
    import numpy as _np
    import concourse.bacc as _bacc
    from concourse.bass_utils import run_bass_kernel_spmd as _run

    nc = _bacc.Bacc("TRN2", target_bir_lowering=False, num_devices=1)
    arrays, args = {}, []
    for name in _INS:
        a = _np.ascontiguousarray(inputs[name])
        arrays[f"in_{name}"] = a
        args.append(nc.dram_tensor(f"in_{name}", a.shape, mybir.dt.from_np(a.dtype), kind="ExternalInput").ap())
    out = nc.dram_tensor("out", _OUT[0], mybir.dt.from_np(_np.dtype(_OUT[1])), kind="ExternalOutput").ap()
    audio_tower(nc, *args, out)
    r = _run(nc, [arrays], core_ids=[0])
    return r.results[0]["out"]
```

```python
from contextlib import ExitStack

import concourse.bass as bass
from concourse import mybir

F32 = mybir.dt.float32
F32R = mybir.dt.float32r
I32 = mybir.dt.int32
U32 = mybir.dt.uint32
ALU = mybir.AluOpType
ACT = mybir.ActivationFunctionType
AX = mybir.AxisListType

P = 128
BANK = 512
BATCH = 256
PATCH = 16
NODES = 207
HID = 64
D = 512
KD = D // P
TOK = BATCH * PATCH
NPAD = 208
CHUNKS = NPAD * PATCH // P
NODE_SPLIT = ((0, P), (P, NPAD - P))
M_START = (0, NODES - P)
OVERLAP = 2 * P - NODES
EPS = 1e-5

TB = 256
SUBS = TB // P
BLOCKS = TOK // TB
DG = 2
GROUPS = PATCH // DG
WINDOWS = 2

PARTS = 2
PART_HIGH, PART_LOW = range(PARTS)
PRODUCTS = ((PART_HIGH, PART_HIGH), (PART_HIGH, PART_LOW), (PART_LOW, PART_HIGH))

HEADS = 8
DH = 64
SLICE = 32
QUADS = 2
EXPERTS = 16
TOP = 2


def make_identity(nc, pool, ident, sem):
    nc.gpsimd.memset(ident[:], 0.0).then_inc(sem, 1)
    pool.wait_ge(sem, 1)
    nc.gpsimd.affine_select(out=ident[:], in_=ident[:], compare_op=ALU.not_equal, fill=1.0, base=0,
                            pattern=[[-1, P]], channel_multiplier=1).then_inc(sem, 1)


def high(ap):
    return ap.bitcast(F32)


def fold_block(nc, adj, wp, w1, w2, wfold_dram, ident, adjT, w1pair, w2pair, wfold):
    EG = 2
    NEG = PATCH // EG
    wp_rows = wp.rearrange("(m e) n -> m e n", e=PATCH)
    wfold_rows = wfold_dram.rearrange("r (m e) n -> r m e n", e=PATCH)
    with ExitStack() as ctx:
        def sb(name, shape, dt=F32):
            return ctx.enter_context(nc.sbuf_tensor(name, shape, dt))

        def sem(name):
            return ctx.enter_context(nc.semaphore(name))

        adj_rows = sb("adj_rows", [P, 2, NODES])
        adj_fold = sb("adj_fold", [P, WINDOWS, NPAD])
        w1_wide = sb("w1_wide", [P, 2, P])
        wp_in = sb("wp_in", [P, 2, WINDOWS, EG, D])
        wfold_out = sb("wfold_out", [P, 2, 2, PARTS, EG, D], F32R)
        ps_adj = ctx.enter_context(nc.psum_tensor("ps_adj", [P, 4, P], F32))
        ps_fold = ctx.enter_context(nc.psum_tensor("ps_fold", [P, 4, BANK], F32))

        adj_loaded = sem("adj_loaded")
        fold_cleared = sem("fold_cleared")
        fold_adj_loaded = sem("fold_adj_loaded")
        adj_fold_ready = sem("adj_fold_ready")
        ident_ready = sem("ident_ready")
        cleared = sem("cleared")
        small_loaded = sem("small_loaded")
        adj_turned = sem("adj_turned")
        adjT_copied = sem("adjT_copied")
        w1_split = sem("w1_split")
        wp_loaded = [sem(f"wp_loaded{s}") for s in range(2)]
        fold_done = sem("fold_done")
        fold_high = sem("fold_high")
        fold_copied = sem("fold_copied")
        fold_stored = [sem(f"fold_stored{s}") for s in range(2)]
        wfold_loaded = sem("wfold_loaded")

        with nc.Block() as block:
            @block.sync
            def _(sp):
                def load_wp(g):
                    for c, m0 in enumerate(M_START):
                        sp.dma_start(wp_in[:, g % 2, c], wp_rows[m0:m0 + P, g * EG:(g + 1) * EG, :]
                                     ).then_inc(wp_loaded[g % 2], 16)

                for j, (n0, nn) in enumerate(((0, P), (P, NODES - P))):
                    sp.dma_start(adj_rows[0:nn, j, :], adj[n0:n0 + nn, :]).then_inc(adj_loaded, 16)
                sp.wait_ge(fold_cleared, 1)
                for c, m0 in enumerate(M_START):
                    sp.dma_start(adj_fold[:, c, 0:NODES], adj[m0:m0 + P, :]).then_inc(fold_adj_loaded, 16)
                load_wp(0)
                load_wp(1)
                for g in range(NEG):
                    sp.wait_ge(fold_copied, 2 * EG * (g + 1))
                    if g + 2 < NEG:
                        load_wp(g + 2)
                    for j, (n0, nn) in enumerate(NODE_SPLIT):
                        for r in range(PARTS):
                            sp.dma_start(wfold_rows[r, n0:n0 + nn, g * EG:(g + 1) * EG, :],
                                         high(wfold_out[0:nn, g % 2, j, r])).then_inc(fold_stored[g % 2], 16)
                for s in range(2):
                    sp.wait_ge(fold_stored[s], 16 * 2 * PARTS * NEG // 2)
                for r in range(PARTS):
                    sp.dma_start(high(wfold[:, r]), wfold_dram[r].rearrange("(c p) n -> p c n", p=P)
                                 ).then_inc(wfold_loaded, 16)
                sp.wait_ge(wfold_loaded, 16 * PARTS)

            @block.gpsimd
            def _(pool):
                make_identity(nc, pool, ident, ident_ready)
                nc.gpsimd.memset(w1_wide[:], 0.0).then_inc(cleared, 1)
                nc.gpsimd.memset(w2pair[:], 0.0).then_inc(cleared, 1)
                pool.wait_ge(cleared, 2)
                for i in range(2):
                    for half in range(2):
                        for n in range(2):
                            row = half * 64 + 32 * i + PATCH * n
                            pool.dma_start(w1_wide[row:row + PATCH, i, n * HID:(n + 1) * HID], w1
                                           ).then_inc(small_loaded, 16)
                for i in range(2):
                    pool.dma_start(w2pair[i * HID:(i + 1) * HID, i * PATCH:(i + 1) * PATCH],
                                   w2).then_inc(small_loaded, 16)

            @block.scalar
            def _(act):
                for g in range(NEG):
                    if g >= 2:
                        act.wait_ge(fold_stored[g % 2], 16 * 2 * PARTS * (g // 2))
                    for e in range(EG):
                        for j, (n0, nn) in enumerate(NODE_SPLIT):
                            n = 2 * (EG * g + e) + j
                            act.wait_ge(fold_done, n + 1)
                            nc.scalar.copy(wfold_out[0:nn, g % 2, j, PART_HIGH, e, :], ps_fold[0:nn, n % 4, :]
                                           ).then_inc(fold_high, 1)

            @block.tensor
            def _(pe):
                pe.wait_ge(ident_ready, 2)
                pe.wait_ge(adj_loaded, 32)
                for c, m0 in enumerate(M_START):
                    for j, nn in enumerate((P, NODES - P)):
                        last = nc.tensor.transpose(ps_adj[:, 2 * c + j, 0:nn], adj_rows[0:nn, j, m0:m0 + P],
                                                   ident[0:nn, 0:nn])
                last.then_inc(adj_turned, 1)
                pe.wait_ge(adj_fold_ready, 1)
                for g in range(NEG):
                    pe.wait_ge(wp_loaded[g % 2], 32 * (g // 2 + 1))
                    for e in range(EG):
                        for j, (n0, nn) in enumerate(NODE_SPLIT):
                            n = 2 * (EG * g + e) + j
                            if n >= 4:
                                pe.wait_ge(fold_copied, n - 3)
                            for c in range(WINDOWS):
                                last = nc.tensor.matmul(ps_fold[0:nn, n % 4, :], adj_fold[:, c, n0:n0 + nn],
                                                        wp_in[:, g % 2, c, e, :], start=(c == 0),
                                                        stop=(c == WINDOWS - 1))
                            last.then_inc(fold_done, 1)

            @block.vector
            def _(dve):
                nc.vector.memset(adj_fold[:], 0.0).then_inc(fold_cleared, 1)
                nc.vector.memset(high(adjT[:]), 0.0).then_inc(adjT_copied, 1)
                dve.wait_ge(fold_adj_loaded, 32)
                nc.vector.memset(adj_fold[0:OVERLAP, 1, :], 0.0).then_inc(adj_fold_ready, 1)
                dve.wait_ge(adjT_copied, 1)
                dve.wait_ge(adj_turned, 1)
                done = 1
                for part in range(PARTS):
                    for c in range(WINDOWS):
                        for j, nn in enumerate((P, NODES - P)):
                            cols = slice(j * P, j * P + nn)
                            if part == PART_HIGH:
                                last = nc.vector.tensor_copy(adjT[:, part, c, cols], ps_adj[:, 2 * c + j, 0:nn])
                            else:
                                last = nc.vector.tensor_tensor(adjT[:, part, c, cols], ps_adj[:, 2 * c + j, 0:nn],
                                                               high(adjT[:, PART_HIGH, c, cols]), ALU.subtract)
                            last.then_inc(adjT_copied, 1)
                            done += 1
                    dve.wait_ge(adjT_copied, done)
                nc.vector.memset(high(adjT[0:OVERLAP, :, 1, :]), 0.0)
                dve.wait_ge(small_loaded, 16 * 10)
                nc.vector.tensor_copy(w1pair[:, PART_HIGH], w1_wide[:]).then_inc(w1_split, 1)
                dve.wait_ge(w1_split, 1)
                nc.vector.tensor_tensor(w1pair[:, PART_LOW], w1_wide[:], high(w1pair[:, PART_HIGH]), ALU.subtract)
                for g in range(NEG):
                    for e in range(EG):
                        for j, (n0, nn) in enumerate(NODE_SPLIT):
                            n = 2 * (EG * g + e) + j
                            dve.wait_ge(fold_high, n + 1)
                            nc.vector.tensor_tensor(wfold_out[0:nn, g % 2, j, PART_LOW, e, :], ps_fold[0:nn, n % 4, :],
                                                    high(wfold_out[0:nn, g % 2, j, PART_HIGH, e, :]), ALU.subtract
                                                    ).then_inc(fold_copied, 1)


def tokenizer_block(nc, x, y_dram, h_dram, ident, adjT, w1pair, w2pair, wfold, stats):
    x_tok = x.rearrange("b (p s) f -> (b p) s f", s=PATCH)
    h_rows = h_dram.rearrange("(b s p) n -> b p s n", p=P, s=SUBS)
    PAIRS = CHUNKS // 2
    LOADS = ((0, 6), (6, 13), (13, 19), (19, CHUNKS))
    with ExitStack() as ctx:
        def sb(name, shape, dt=F32):
            return ctx.enter_context(nc.sbuf_tensor(name, shape, dt))

        def psum(name, shape):
            return ctx.enter_context(nc.psum_tensor(name, shape, F32))

        def sem(name):
            return ctx.enter_context(nc.semaphore(name))

        x_in = sb("x_in", [P, 2, SUBS, DG, NODES])
        xT = sb("xT", [P, 2, PARTS, WINDOWS, DG, TB], F32R)
        y = sb("y", [P, 2, 2, DG, TB])
        y_turned = sb("y_turned", [P, CHUNKS, TB])
        y_split = sb("y_split", [P, 2, 2, TB], F32R)
        hidden = sb("hidden", [P, 2, 2, BANK])
        g_sb = sb("g_sb", [P, 2, PARTS, 2, TB], F32R)
        h_out = sb("h_out", [P, 2, SUBS, D])

        ps_front = psum("ps_front", [P, 2, BANK])
        ps_hid = psum("ps_hid", [P, 2, BANK])
        ps_g = psum("ps_g", [P, 2, BANK])
        ps_h = psum("ps_h", [P, SUBS, BANK])

        x_loaded = [sem(f"x_loaded{s}") for s in range(2)]
        front_filled = sem("front_filled")
        x_high = sem("x_high")
        front_copied = sem("front_copied")
        y_stored = [sem(f"y_stored{s}") for s in range(2)]
        y_loaded = [sem(f"y_loaded{s}") for s in range(len(LOADS))]
        y_high = sem("y_high")
        y_low = sem("y_low")
        hid_filled = sem("hid_filled")
        gelu_done = sem("gelu_done")
        g_filled = sem("g_filled")
        g_high = sem("g_high")
        g_copied = sem("g_copied")
        proj_done = sem("proj_done")
        h_copied = sem("h_copied")
        h_stored = sem("h_stored")
        h_free = sem("h_free")

        FILLS = 2 * WINDOWS

        def part_of(k):
            return [lo <= k < hi for lo, hi in LOADS].index(True)

        with nc.Block() as block:
            @block.gpsimd
            def _(pool):
                def load_x(b, dg):
                    for s in range(SUBS):
                        pool.dma_start(x_in[:, dg % 2, s],
                                       x_tok[bass.ds(b * TB + s * P, P), dg * DG:(dg + 1) * DG, :]
                                       ).then_inc(x_loaded[dg % 2], 16)

                def load_x_next(b, dg):
                    pool.wait_ge(front_filled, FILLS * (GROUPS * b + dg - 2) + WINDOWS)
                    load_x(b, dg)

                load_x(0, 0)
                load_x(0, 1)
                for dg in range(2, GROUPS):
                    load_x_next(0, dg)
                with pool.Fori(1, BLOCKS) as b:
                    for dg in range(GROUPS):
                        load_x_next(b, dg)

            @block.sync
            def _(sp):
                def store_y(b):
                    for dg in range(GROUPS):
                        sp.wait_ge(front_copied, FILLS * (GROUPS * b + dg + 1))
                        for j, (n0, nn) in enumerate(NODE_SPLIT):
                            sp.dma_start(y_dram[b, n0:n0 + nn, dg * DG:(dg + 1) * DG, :],
                                         y[0:nn, dg % 2, j]).then_inc(y_stored[dg % 2], 16)
                    for s in range(2):
                        sp.wait_ge(y_stored[s], 16 * GROUPS * (b + 1))

                def load_y(b, first=False):
                    rows = y_dram[b].rearrange("n s t -> (n s) t").rearrange("(c p) t -> p c t", p=P)
                    for n, (lo, hi) in enumerate(LOADS):
                        if not first:
                            sp.wait_ge(y_low, CHUNKS * (b - 1) + hi)
                        sp.dma_start(y_turned[:, lo:hi], rows[:, lo:hi]).then_inc(y_loaded[n], 16)

                def store_h(b, u):
                    sp.wait_ge(h_copied, b + 2)
                    sp.dma_start(h_rows[b], h_out[:, u]).then_inc(h_stored, 16)
                    sp.wait_ge(h_stored, 16 * b + 16)
                    sp.sem_inc(h_free, 1)

                store_y(0)
                load_y(0, first=True)
                with sp.Fori(0, BLOCKS - 2, 2) as b:
                    for u in range(2):
                        store_y(b + u + 1)
                        load_y(b + u + 1)
                        store_h(b + u, u)
                store_y(BLOCKS - 1)
                load_y(BLOCKS - 1)
                store_h(BLOCKS - 2, 0)
                store_h(BLOCKS - 1, 1)

            @block.tensor
            def _(pe):
                pe.sem_inc(g_filled, 2)
                pe.sem_inc(proj_done, 2)

                def turn_x(b, dg, first=False):
                    slot = dg % 2
                    pe.wait_ge(x_loaded[slot], 16 * GROUPS * b + 32 * (dg // 2) + 32)
                    for c in range(WINDOWS):
                        if not first:
                            pe.wait_ge(front_copied, FILLS * (GROUPS * b + dg) + c - 1)
                        for e in range(DG):
                            for s in range(SUBS):
                                last = nc.tensor.transpose(
                                    ps_front[:, c, e * TB + s * P:e * TB + (s + 1) * P],
                                    x_in[:, slot, s, e, M_START[c]:M_START[c] + P], ident[:])
                        last.then_inc(front_filled, 1)

                def adjacency(b, dg):
                    pe.wait_ge(front_copied, FILLS * (GROUPS * b + dg) + WINDOWS)
                    for j, (n0, nn) in enumerate(NODE_SPLIT):
                        terms = [(c, a, v) for c in range(WINDOWS) for a, v in PRODUCTS]
                        for n, (c, a, v) in enumerate(terms):
                            last = nc.tensor.matmul(ps_front[0:nn, j, :], adjT[:, a, c, n0:n0 + nn],
                                                    xT[:, dg % 2, v, c], start=(n == 0), stop=(n == len(terms) - 1))
                        last.then_inc(front_filled, 1)

                def expand(b, k):
                    pe.wait_ge(y_low, CHUNKS * b + k + 1)
                    for half in range(2):
                        pe.wait_ge(gelu_done, 2 * CHUNKS * b + 2 * k + half + 1)
                        for i in range(2):
                            for part in range(PARTS):
                                last = nc.tensor.matmul(ps_hid[:, half, i * TB:(i + 1) * TB], w1pair[:, part, i, :],
                                                        y_split[:, k % 2, half, :], start=(part == 0),
                                                        stop=(part == PARTS - 1))
                        last.then_inc(hid_filled, 1)

                def contract(b, u, k):
                    bank = (PAIRS * u + k // 2) % 2
                    pe.wait_ge(gelu_done, 2 * CHUNKS * b + 2 * k + 4)
                    if k % 2 == 0:
                        pe.wait_ge(g_copied, PAIRS * b + k // 2 + 1)
                    for q in range(4):
                        last = nc.tensor.matmul(ps_g[32 * q:32 * (q + 1), bank, (k % 2) * TB:(k % 2 + 1) * TB],
                                                w2pair[:], hidden[:, k % 2, q // 2, (q % 2) * TB:(q % 2 + 1) * TB],
                                                start=True, stop=True)
                    last.then_inc(g_filled, 1)

                def project(b, u, k):
                    slot = (PAIRS * u + k // 2) % 2
                    if k % 2 == 0:
                        pe.wait_ge(g_copied, PAIRS * b + k // 2 + 3)
                    if k == 0:
                        pe.wait_ge(h_copied, b + 1)
                    for s in range(SUBS):
                        for n, (a, v) in enumerate(PRODUCTS):
                            last = nc.tensor.matmul(ps_h[:, s, :], g_sb[:, slot, a, k % 2, s * P:(s + 1) * P],
                                                    wfold[:, v, k, :], start=(k == 0 and n == 0),
                                                    stop=(k == CHUNKS - 1 and n == len(PRODUCTS) - 1))
                    if k % 2 == 1:
                        last.then_inc(proj_done, 1)

                def run_block(b, u, ahead):
                    for step in range(CHUNKS + 3):
                        if step < CHUNKS:
                            expand(b, step)
                        if ahead and step < 2 * GROUPS:
                            (adjacency if step % 2 else turn_x)(b + 1, step // 2)
                        if 1 <= step <= CHUNKS:
                            contract(b, u, step - 1)
                        if step >= 3:
                            project(b, u, step - 3)

                for dg in range(GROUPS):
                    turn_x(0, dg, first=(dg == 0))
                    adjacency(0, dg)
                with pe.Fori(0, BLOCKS - 2, 2) as b:
                    run_block(b, 0, True)
                    run_block(b + 1, 1, True)
                run_block(BLOCKS - 2, 0, True)
                run_block(BLOCKS - 1, 1, False)

            @block.scalar
            def _(act):
                act.sem_inc(gelu_done, 2)

                def x_part(b, dg):
                    for c in range(WINDOWS):
                        act.wait_ge(front_filled, FILLS * (GROUPS * b + dg) + c + 1)
                        nc.scalar.copy(xT[:, dg % 2, PART_HIGH, c],
                                       ps_front[:, c, :].rearrange("p (s t) -> p s t", s=DG)).then_inc(x_high, 1)

                def y_part(b, k):
                    if k in [lo for lo, _ in LOADS]:
                        act.wait_ge(y_loaded[part_of(k)], 16 * b + 16)
                    for half in range(2):
                        rows = slice(64 * half, 64 * half + 64)
                        last = nc.scalar.copy(y_split[rows, k % 2, half, :], y_turned[rows, k, :])
                    last.then_inc(y_high, 1)

                def gelu(b, k):
                    act.wait_ge(g_filled, CHUNKS * b + k + 1)
                    for half in range(2):
                        act.wait_ge(hid_filled, 2 * CHUNKS * b + 2 * k + half + 1)
                        nc.scalar.activation(hidden[:, k % 2, half], ps_hid[:, half, :], ACT.Gelu
                                             ).then_inc(gelu_done, 1)

                def g_part(b, u, pair):
                    slot = (PAIRS * u + pair) % 2
                    act.wait_ge(g_filled, CHUNKS * b + 2 * pair + 4)
                    act.wait_ge(proj_done, PAIRS * b + pair + 1)
                    nc.scalar.copy(g_sb[:, slot, PART_HIGH], ps_g[:, slot, :].rearrange("p (c t) -> p c t", c=2)
                                   ).then_inc(g_high, 1)

                def run_block(b, u, ahead):
                    for step in range(CHUNKS + 1):
                        if step + 1 < CHUNKS:
                            y_part(b, step + 1)
                        elif step + 1 == CHUNKS and ahead:
                            y_part(b + 1, 0)
                        if step < CHUNKS:
                            gelu(b, step)
                        if ahead and step < 2 * GROUPS and step % 2 == 0:
                            x_part(b + 1, step // 2)
                        if step >= 2 and step % 2 == 0:
                            g_part(b, u, step // 2 - 1)

                for dg in range(GROUPS):
                    x_part(0, dg)
                y_part(0, 0)
                with act.Fori(0, BLOCKS - 2, 2) as b:
                    run_block(b, 0, True)
                    run_block(b + 1, 1, True)
                run_block(BLOCKS - 2, 0, True)
                run_block(BLOCKS - 1, 1, False)

            @block.vector
            def _(dve):
                dve.sem_inc(g_copied, 2)
                dve.sem_inc(h_copied, 1)
                dve.sem_inc(h_free, 2)

                def x_part(b, dg):
                    for c in range(WINDOWS):
                        dve.wait_ge(x_high, WINDOWS * (GROUPS * b + dg) + c + 1)
                        nc.vector.tensor_tensor(xT[:, dg % 2, PART_LOW, c],
                                                ps_front[:, c, :].rearrange("p (s t) -> p s t", s=DG),
                                                high(xT[:, dg % 2, PART_HIGH, c]), ALU.subtract
                                                ).then_inc(front_copied, 1)

                def copy_y(b, dg, first=False):
                    if not first:
                        dve.wait_ge(y_stored[dg % 2], 16 * GROUPS * b + 32 * (dg // 2))
                    for j, (n0, nn) in enumerate(NODE_SPLIT):
                        dve.wait_ge(front_filled, FILLS * (GROUPS * b + dg) + WINDOWS + j + 1)
                        nc.vector.tensor_copy(y[0:nn, dg % 2, j],
                                              ps_front[0:nn, j, :].rearrange("p (s t) -> p s t", s=DG)
                                              ).then_inc(front_copied, 1)

                def y_part(b, k):
                    dve.wait_ge(y_high, CHUNKS * b + k + 1)
                    for half in range(2):
                        rows, other = slice(64 * half, 64 * half + 64), slice(64 - 64 * half, 128 - 64 * half)
                        last = nc.vector.tensor_tensor(y_split[other, k % 2, half, :], y_turned[rows, k, :],
                                                       high(y_split[rows, k % 2, half, :]), ALU.subtract)
                    last.then_inc(y_low, 1)

                def g_part(b, u, pair):
                    slot = (PAIRS * u + pair) % 2
                    dve.wait_ge(g_high, PAIRS * b + pair + 1)
                    nc.vector.tensor_tensor(g_sb[:, slot, PART_LOW], ps_g[:, slot, :].rearrange("p (c t) -> p c t", c=2),
                                            high(g_sb[:, slot, PART_HIGH]), ALU.subtract).then_inc(g_copied, 1)

                def copy_h(b, u):
                    dve.wait_ge(proj_done, PAIRS * (b + 1) + 2)
                    dve.wait_ge(h_free, b + 1)
                    for s in range(SUBS):
                        nc.vector.bn_stats(stats[:, bass.ds(b * SUBS + s, 1), :].squeeze(1), ps_h[:, s, :])
                    nc.vector.tensor_copy(h_out[:, u], ps_h[:]).then_inc(h_copied, 1)

                def run_block(b, u, ahead):
                    for step in range(CHUNKS + 1):
                        if step + 1 < CHUNKS:
                            y_part(b, step + 1)
                        elif step + 1 == CHUNKS and ahead:
                            y_part(b + 1, 0)
                        if ahead and step < 2 * GROUPS:
                            (copy_y if step % 2 else x_part)(b + 1, step // 2)
                        if step >= 2 and step % 2 == 0:
                            g_part(b, u, step // 2 - 1)
                    copy_h(b, u)

                for dg in range(GROUPS):
                    x_part(0, dg)
                    copy_y(0, dg, first=(dg < 2))
                y_part(0, 0)
                with dve.Fori(0, BLOCKS - 2, 2) as b:
                    run_block(b, 0, True)
                    run_block(b + 1, 1, True)
                run_block(BLOCKS - 2, 0, True)
                run_block(BLOCKS - 1, 1, False)


class Chain:

    def __init__(self, eng, sem, base):
        self.eng, self.sem, self.base, self.n = eng, sem, base, 0

    def __call__(self, ins):
        self.n += 1
        ins.then_inc(self.sem, 1)
        self.eng.wait_ge(self.sem, self.base + self.n)


AB = 512
TILES = AB // P
ABLOCKS = TOK // AB
NTILES = TOK // P
IN_TILE = P // PATCH


def attention_block(nc, h_dram, W_in, b_in, Wq, Wk, Wv, W_out, b_out, ident, h, stats):
    QV = 2 * SLICE + 2 * DH
    with ExitStack() as ctx:
        def sb(name, shape, dt=F32):
            return ctx.enter_context(nc.sbuf_tensor(name, shape, dt))

        def psum(name, shape):
            return ctx.enter_context(nc.psum_tensor(name, shape, F32))

        def sem(name):
            return ctx.enter_context(nc.semaphore(name))

        w_in = sb("w_in", [P, KD, D])
        w_out = sb("w_out", [P, KD, D])
        wk_pair = sb("wk_pair", [P, 2 * SLICE])
        wqv_pair = sb("wqv_pair", [P, QV])
        b_in_row = sb("b_in_row", [KD, P])
        b_in_col = sb("b_in_col", [P, KD])
        b_out_all = sb("b_out_all", [P, D])
        same_batch = sb("same_batch", [P, 4, P])
        mean_var = sb("mean_var", [P, NTILES, 2])
        rstd = sb("rstd", [P, NTILES])
        hn = sb("hn", [P, TILES, D])
        hnT = sb("hnT", [P, KD, AB])
        xmT = sb("xmT", [P, KD, AB])
        k_exp = sb("k_exp", [P, 2, QUADS, AB])
        k_max = sb("k_max", [P, QUADS, AB // PATCH])
        k_inv = sb("k_inv", [P, 2, QUADS, AB // PATCH])
        qv = sb("qv", [P, 2, TILES, KD, QV])
        q_prob = sb("q_prob", [P, TILES, HEADS, SLICE])
        q_red = sb("q_red", [P, TILES, HEADS])
        qT_wide = sb("qT_wide", [P, 2, QUADS, 4, P])
        scores = sb("scores", [P, 2, QUADS, 4, P])
        oT = sb("oT", [P, 2, KD, P])

        ps_turn = psum("ps_turn", [P, 2, BANK])
        ps_proj = psum("ps_proj", [P, 2, BANK])
        ps_score = psum("ps_score", [P, QUADS, BANK])
        ps_oT = psum("ps_oT", [P, KD, P])
        ps_out = psum("ps_out", [P, D])

        h_loaded = [sem(f"h_loaded{i}") for i in range(2)]
        w_loaded = sem("w_loaded")
        cleared = sem("cleared")
        pair_loaded = sem("pair_loaded")
        masked_ones = sem("masked_ones")
        eps_ready = sem("eps_ready")
        stats_done = sem("stats_done")
        std_done = sem("std_done")
        setup = sem("setup")
        bias_turned = sem("bias_turned")
        bias_ready = sem("bias_ready")
        qT_cleared = sem("qT_cleared")
        normed = sem("normed")
        bias_added = sem("bias_added")
        turned = sem("turned")
        turn_copied = sem("turn_copied")
        proj_filled = sem("proj_filled")
        proj_copied = sem("proj_copied")
        k_centred = sem("k_centred")
        k_exped = sem("k_exped")
        k_ready = sem("k_ready")
        q_centred = sem("q_centred")
        q_exped = sem("q_exped")
        q_ready = sem("q_ready")
        soft = sem("soft")
        score_filled = sem("score_filled")
        score_masked = sem("score_masked")
        oT_filled = sem("oT_filled")
        oT_copied = sem("oT_copied")
        out_filled = sem("out_filled")
        out_added = sem("out_added")

        A_TURNS, B_TURNS = 6, 4
        TURNS = A_TURNS + B_TURNS
        PROJ = 3 * KD

        def turns_a(b):
            return TURNS * b - B_TURNS

        def turns_b(b):
            return TURNS * b + 2 * A_TURNS

        def turns_b_last(b):
            return TURNS * b + A_TURNS

        with nc.Block() as block:
            @block.sync
            def _(sp):
                for b in range(ABLOCKS):
                    sp.dma_start(h[:, b * TILES:(b + 1) * TILES, :],
                                 h_dram[b * AB:(b + 1) * AB, :].rearrange("(t p) n -> p t n", p=P)
                                 ).then_inc(h_loaded[0 if b == 0 else 1], 16)
                    if b == 0:
                        sp.dma_start(w_in[:], W_in.rearrange("(k p) n -> p k n", p=P)).then_inc(w_loaded, 16)
                        sp.dma_start(w_out[:], W_out.rearrange("(k p) n -> p k n", p=P)).then_inc(w_loaded, 16)
                        sp.dma_start(b_in_row[:], b_in.rearrange("(k p) -> k p", p=P)).then_inc(w_loaded, 16)
                        sp.dma_start(b_out_all[:], b_out.partition_broadcast(P)).then_inc(w_loaded, 16)

            @block.gpsimd
            def _(pool):
                nc.gpsimd.memset(wk_pair[:], 0.0).then_inc(cleared, 1)
                nc.gpsimd.memset(wqv_pair[:], 0.0).then_inc(cleared, 1)
                pool.wait_ge(cleared, 2)
                for i in range(2):
                    rows = slice(i * DH, (i + 1) * DH)
                    pool.dma_start(wk_pair[rows, i * SLICE:(i + 1) * SLICE], Wk).then_inc(pair_loaded, 16)
                    pool.dma_start(wqv_pair[rows, i * SLICE:(i + 1) * SLICE], Wq).then_inc(pair_loaded, 16)
                    pool.dma_start(wqv_pair[rows, 2 * SLICE + i * DH:2 * SLICE + (i + 1) * DH], Wv
                                   ).then_inc(pair_loaded, 16)
                nc.gpsimd.memset(same_batch[:], 1.0).then_inc(masked_ones, 1)
                for n, (step, base, mul) in enumerate(((-PATCH, 0, 1), (PATCH, PATCH - 1, -1))):
                    pool.wait_ge(masked_ones, n + 1)
                    v = same_batch[:].rearrange("p h (b s) -> p h b s", s=PATCH)
                    nc.gpsimd.affine_select(out=v, in_=v, compare_op=ALU.is_ge, fill=0.0, base=base,
                                            pattern=[[0, 4], [step, IN_TILE], [0, PATCH]],
                                            channel_multiplier=mul).then_inc(masked_ones, 1)
                pool.wait_ge(w_loaded, 64)
                with pool.Fori(0, ABLOCKS) as b:
                    pool.wait_ge(normed, b + 1)
                    rows = h[:, bass.ds(b * TILES, TILES), :]
                    nc.gpsimd.tensor_tensor(rows, rows, b_out_all[:].unsqueeze(1).broadcast_to([P, TILES, D]),
                                            ALU.add).then_inc(bias_added, 1)

            @block.tensor
            def _(pe):
                pe.sem_inc(oT_filled, 2)
                pe.sem_inc(out_filled, 2)
                pe.wait_ge(w_loaded, 64)
                nc.tensor.transpose(ps_out[:, 0:KD], b_in_row[:], ident[0:KD, 0:KD]).then_inc(bias_turned, 1)
                pe.wait_ge(pair_loaded, 96)
                pe.wait_ge(bias_ready, 1)

                def stage_a(b, turns, first=False):
                    pe.wait_ge(normed, b + 1)
                    for t in range(TILES):
                        if not (first and t < 2):
                            pe.wait_ge(turn_copied, turns + t - 1)
                        for k in range(KD):
                            last = nc.tensor.transpose(ps_turn[:, t % 2, k * P:(k + 1) * P],
                                                       hn[:, t, k * P:(k + 1) * P], ident[:])
                        last.then_inc(turned, 1)
                    pe.wait_ge(turn_copied, turns + TILES)
                    for i in range(KD):
                        if not (first and i < 2):
                            pe.wait_ge(proj_copied, PROJ * b + i - 1)
                        for k in range(KD):
                            last = nc.tensor.matmul(ps_proj[:, i % 2, :], w_in[:, k, i * P:(i + 1) * P],
                                                    hnT[:, k, :], start=(k == 0), stop=(k == KD - 1))
                        last.then_inc(proj_filled, 1)
                    pe.wait_ge(proj_copied, PROJ * b + KD)
                    for quad in range(QUADS):
                        for i in range(2):
                            last = nc.tensor.matmul(ps_turn[i * DH:(i + 1) * DH, quad, :], wk_pair[:],
                                                    xmT[:, 2 * quad + i, :], start=True, stop=True)
                        last.then_inc(turned, 1)
                    for t in range(TILES):
                        for half in range(2):
                            n = KD + 2 * t + half
                            pe.wait_ge(proj_copied, PROJ * b + n - 1)
                            for i in range(2):
                                last = nc.tensor.matmul(ps_proj[:, n % 2, i * QV:(i + 1) * QV],
                                                        xmT[:, 2 * half + i, t * P:(t + 1) * P], wqv_pair[:],
                                                        start=True, stop=True)
                            last.then_inc(proj_filled, 1)

                def stage_b(b, u, turns):
                    def turn_q(t):
                        if t == 0:
                            pe.wait_ge(q_ready, b + 1)
                        pe.wait_ge(turn_copied, turns + t - 1)
                        for quad in range(QUADS):
                            last = nc.tensor.transpose(
                                ps_turn[:, t % 2, quad * P:(quad + 1) * P],
                                q_prob[:, t, 4 * quad:4 * quad + 4, :].rearrange("p h s -> p (h s)"), ident[:])
                        last.then_inc(turned, 1)

                    def score(t):
                        if t == 0:
                            pe.wait_ge(k_ready, b + 1)
                        pe.wait_ge(turn_copied, turns + t + 1)
                        for quad in range(QUADS):
                            n = 2 * TILES * b + 2 * t + quad
                            pe.wait_ge(score_masked, n + 1)
                            nc.tensor.matmul(ps_score[:, quad, :], k_exp[:, u, quad, t * P:(t + 1) * P],
                                             qT_wide[:, t % 2, quad].rearrange("p h t -> p (h t)"),
                                             start=True, stop=True).then_inc(score_filled, 1)

                    def mix(t):
                        pe.wait_ge(score_masked, 2 * TILES * b + 2 * t + 4)
                        pe.wait_ge(oT_copied, TILES * b + t + 1)
                        for head in range(HEADS):
                            i, r = head // 2, head % 2
                            last = nc.tensor.matmul(
                                ps_oT[r * DH:(r + 1) * DH, i, :],
                                qv[:, u, t, i, 2 * SLICE + r * DH:2 * SLICE + (r + 1) * DH],
                                scores[:, t % 2, head // 4, head % 4, :], start=True, stop=True)
                        last.then_inc(oT_filled, 1)

                    def out(t):
                        pe.wait_ge(oT_copied, TILES * b + t + 2)
                        pe.wait_ge(out_added, TILES * b + t + 1)
                        for i in range(KD):
                            last = nc.tensor.matmul(ps_out[:], oT[:, t % 2, i, :], w_out[:, i, :],
                                                    start=(i == 0), stop=(i == KD - 1))
                        last.then_inc(out_filled, 1)

                    for step in range(TILES + 3):
                        if step < TILES:
                            turn_q(step)
                        if 1 <= step <= TILES:
                            score(step - 1)
                        if 2 <= step <= TILES + 1:
                            mix(step - 2)
                        if step >= 3:
                            out(step - 3)

                stage_a(0, 0, first=True)
                with pe.Fori(0, ABLOCKS // 2 - 1) as pair:
                    b = 2 * pair
                    for u in range(2):
                        stage_a(b + u + 1, turns_a(b + u + 1))
                        stage_b(b + u, u, turns_b(b + u))
                stage_a(ABLOCKS - 1, turns_a(ABLOCKS - 1))
                stage_b(ABLOCKS - 2, 0, turns_b(ABLOCKS - 2))
                stage_b(ABLOCKS - 1, 1, turns_b_last(ABLOCKS - 1))

            @block.scalar
            def _(act):
                act.sem_inc(oT_copied, 1)
                act.wait_ge(stats_done, 1)
                nc.scalar.activation(rstd[:], rstd[:], ACT.Sqrt).then_inc(std_done, 1)
                act.wait_ge(bias_ready, 1)

                def stage_a(b, first=False):
                    for i in range(KD):
                        act.wait_ge(proj_filled, PROJ * b + i + 1)
                        nc.scalar.activation(xmT[:, i, :], ps_proj[:, i % 2, :], ACT.Identity,
                                             bias=b_in_col[:, i:i + 1]).then_inc(proj_copied, 1)

                def exp_q(b):
                    act.wait_ge(q_centred, b + 1)
                    nc.scalar.activation(q_prob[:], q_prob[:], ACT.Exp).then_inc(q_exped, 1)

                def exp_k_copy_qv(b, u):
                    for quad in range(QUADS):
                        act.wait_ge(k_centred, 2 * b + quad + 1)
                        nc.scalar.activation(k_exp[:, u, quad, :], k_exp[:, u, quad, :], ACT.Exp
                                             ).then_inc(k_exped, 1)
                    for t in range(TILES):
                        for half in range(2):
                            n = KD + 2 * t + half
                            act.wait_ge(proj_filled, PROJ * b + n + 1)
                            nc.scalar.copy(qv[:, u, t, 2 * half:2 * half + 2, :],
                                           ps_proj[:, n % 2, 0:2 * QV].rearrange("p (i c) -> p i c", i=2)
                                           ).then_inc(proj_copied, 1)

                def stage_b(b):
                    for t in range(TILES):
                        n = TILES * b + t
                        act.wait_ge(oT_filled, n + 3)
                        act.wait_ge(out_filled, n + 1)
                        nc.scalar.copy(oT[:, t % 2], ps_oT[:]).then_inc(oT_copied, 1)

                stage_a(0)
                exp_k_copy_qv(0, 0)
                with act.Fori(0, ABLOCKS // 2 - 1) as pair:
                    b = 2 * pair
                    for u in range(2):
                        stage_a(b + u + 1)
                        exp_q(b + u)
                        exp_k_copy_qv(b + u + 1, 1 - u)
                        stage_b(b + u)
                stage_a(ABLOCKS - 1)
                exp_q(ABLOCKS - 2)
                exp_k_copy_qv(ABLOCKS - 1, 1)
                stage_b(ABLOCKS - 2)
                exp_q(ABLOCKS - 1)
                stage_b(ABLOCKS - 1)

            @block.vector
            def _(dve):
                dve.sem_inc(score_masked, 2)
                dve.sem_inc(out_added, 1)
                nc.vector.memset(qT_wide[:], 0.0).then_inc(qT_cleared, 1)
                for t in range(NTILES):
                    last = nc.vector.bn_aggr(mean_var[:, t, :], stats[:, t, :])
                last.then_inc(setup, 1)
                dve.wait_ge(setup, 1)
                nc.vector.tensor_scalar(rstd[:], mean_var[:, :, 1], EPS, None, ALU.add).then_inc(stats_done, 1)
                dve.wait_ge(bias_turned, 1)
                nc.vector.tensor_copy(b_in_col[:], ps_out[:, 0:KD]).then_inc(bias_ready, 1)
                dve.wait_ge(std_done, 1)
                nc.vector.reciprocal(rstd[:], rstd[:]).then_inc(setup, 1)
                dve.wait_ge(setup, 2)
                dve.wait_ge(qT_cleared, 1)

                def layernorm(b):
                    for t in range(TILES):
                        n = b * TILES + t
                        last = nc.vector.tensor_scalar(hn[:, t, :], h[:, bass.ds(n, 1), :].squeeze(1),
                                                       mean_var[:, bass.ds(n, 1), 0], rstd[:, bass.ds(n, 1)],
                                                       ALU.subtract, ALU.mult)
                    last.then_inc(normed, 1)

                def copy_hnT(b, turns):
                    for t in range(TILES):
                        dve.wait_ge(turned, turns + t + 1)
                        nc.vector.tensor_copy(hnT[:, :, t * P:(t + 1) * P],
                                              ps_turn[:, t % 2, :].rearrange("p (k t) -> p k t", k=KD)
                                              ).then_inc(turn_copied, 1)

                def centre_q(b, u, chain):
                    q = qv[:, u, :, :, 0:2 * SLICE].rearrange("p t i (h s) -> p (t i) h s", s=SLICE)
                    dve.wait_ge(proj_copied, PROJ * b + PROJ)
                    red = q_red[:].rearrange("p t (i h) -> p (t i) h", h=2)
                    chain(nc.vector.tensor_reduce(red, q, AX.X, ALU.max))
                    nc.vector.tensor_tensor(q_prob[:].rearrange("p t (i h) s -> p (t i) h s", h=2), q,
                                            red.unsqueeze(3).broadcast_to([P, TILES * KD, 2, SLICE]), ALU.subtract
                                            ).then_inc(q_centred, 1)

                def centre_k(b, u, turns, chain):
                    for quad in range(QUADS):
                        dve.wait_ge(turned, turns + TILES + quad + 1)
                        k = ps_turn[:, quad, :].rearrange("p (b s) -> p b s", s=PATCH)
                        chain(nc.vector.tensor_reduce(k_max[:, quad, :], k, AX.X, ALU.max))
                        nc.vector.tensor_tensor(k_exp[:, u, quad, :].rearrange("p (b s) -> p b s", s=PATCH), k,
                                                k_max[:, quad, :].unsqueeze(2).broadcast_to([P, AB // PATCH, PATCH]),
                                                ALU.subtract).then_inc(k_centred, 1)
                        dve.wait_ge(k_centred, 2 * b + quad + 1)
                        dve.sem_inc(turn_copied, 1)

                def norm_q(b, chain):
                    dve.wait_ge(q_exped, b + 1)
                    q = q_prob[:].rearrange("p t h s -> p (t h) s")
                    red = q_red[:].rearrange("p t h -> p (t h)")
                    chain(nc.vector.tensor_reduce(red, q, AX.X, ALU.add))
                    chain(nc.vector.reciprocal(red, red))
                    nc.vector.tensor_tensor(q, q, red.unsqueeze(2).broadcast_to([P, TILES * HEADS, SLICE]), ALU.mult
                                            ).then_inc(q_ready, 1)

                def norm_k(b, u, chain):
                    dve.wait_ge(k_exped, 2 * b + 2)
                    k = k_exp[:, u].rearrange("p q (b s) -> p (q b) s", s=PATCH)
                    inv = k_inv[:, u].rearrange("p q b -> p (q b)")
                    chain(nc.vector.tensor_reduce(inv, k, AX.X, ALU.add))
                    nc.vector.reciprocal(inv, inv).then_inc(k_ready, 1)

                def stage_b(b, u, turns):
                    def spread_q(t):
                        dve.wait_ge(turned, turns + t + 1)
                        for quad in range(QUADS):
                            for r in range(4):
                                rows = slice(32 * r, 32 * r + 32)
                                inv = k_inv[rows, u, quad, t * IN_TILE:(t + 1) * IN_TILE]
                                last = nc.vector.tensor_tensor(
                                    qT_wide[rows, t % 2, quad, r, :].rearrange("p (b s) -> p b s", s=PATCH),
                                    ps_turn[rows, t % 2, quad * P:(quad + 1) * P].rearrange("p (b s) -> p b s", s=PATCH),
                                    inv.unsqueeze(2).broadcast_to([32, IN_TILE, PATCH]), ALU.mult)
                        last.then_inc(turn_copied, 1)

                    def mask(t):
                        dve.wait_ge(oT_filled, TILES * b + t + 1)
                        for quad in range(QUADS):
                            dve.wait_ge(score_filled, 2 * TILES * b + 2 * t + quad + 1)
                            nc.vector.tensor_tensor(scores[:, t % 2, quad],
                                                    ps_score[:, quad, :].rearrange("p (h t) -> p h t", h=4),
                                                    same_batch[:], ALU.mult).then_inc(score_masked, 1)

                    def add_out(t):
                        n = TILES * b + t
                        if t == 0:
                            dve.wait_ge(bias_added, b + 1)
                        dve.wait_ge(out_filled, n + 3)
                        rows = h[:, bass.ds(n, 1), :].squeeze(1)
                        nc.vector.tensor_tensor(rows, ps_out[:], rows, ALU.add).then_inc(out_added, 1)
                        dve.wait_ge(out_added, n + 2)
                        nc.vector.bn_stats(stats[:, bass.ds(n, 1), :].squeeze(1), rows).then_inc(setup, 1)

                    dve.wait_ge(k_ready, b + 1)
                    for step in range(TILES + 3):
                        if step < TILES:
                            spread_q(step)
                        if 1 <= step <= TILES:
                            mask(step - 1)
                        if step >= 3:
                            add_out(step - 3)

                CHAIN = 6
                dve.wait_ge(h_loaded[0], 16)
                layernorm(0)
                copy_hnT(0, 0)
                dve.wait_ge(h_loaded[1], 16 * (ABLOCKS - 1))
                layernorm(1)
                chain = Chain(dve, soft, 0)
                centre_k(0, 0, 0, chain)
                norm_k(0, 0, chain)
                START = chain.n
                dve.wait_ge(masked_ones, 3)

                def both(b, u, ahead):
                    chain = Chain(dve, soft, CHAIN * b + START)
                    copy_hnT(b + 1, turns_a(b + 1))
                    centre_q(b, u, chain)
                    centre_k(b + 1, 1 - u, turns_a(b + 1), chain)
                    norm_q(b, chain)
                    norm_k(b + 1, 1 - u, chain)
                    if ahead:
                        layernorm(b + 2)
                    stage_b(b, u, turns_b(b))
                    assert chain.n == CHAIN

                with dve.Fori(0, ABLOCKS // 2 - 1) as pair:
                    b = 2 * pair
                    both(b, 0, True)
                    both(b + 1, 1, True)
                both(ABLOCKS - 2, 0, False)
                chain = Chain(dve, soft, CHAIN * (ABLOCKS - 1) + START)
                centre_q(ABLOCKS - 1, 1, chain)
                norm_q(ABLOCKS - 1, chain)
                stage_b(ABLOCKS - 1, 1, turns_b_last(ABLOCKS - 1))


def routing_block(nc, gate_w, ident, h, stats, row_dram, aff_dram, out_rows):
    with ExitStack() as ctx:
        def sb(name, shape, dt=F32):
            return ctx.enter_context(nc.sbuf_tensor(name, shape, dt))

        def psum(name, shape):
            return ctx.enter_context(nc.psum_tensor(name, shape, F32))

        def sem(name):
            return ctx.enter_context(nc.semaphore(name))

        gate = sb("gate", [P, KD, EXPERTS])
        mean_var = sb("mean_var2", [P, NTILES, 2])
        rstd = sb("rstd2", [P, NTILES])
        hn = sb("hn2", [P, 2, TILES, D])
        hnT = sb("hnT2", [P, 2, KD, P])
        affinity = sb("affinity", [P, NTILES, EXPERTS])
        red = sb("aff_red", [P, NTILES])
        ps_turn = psum("ps_turn2", [P, 2, KD, P])
        ps_logit = psum("ps_logit", [P, 2, BANK])

        gate_loaded = sem("gate_loaded")
        resid_stored = sem("resid_stored")
        setup = sem("setup2")
        var_ready = sem("var_ready")
        std_done = sem("std_done2")
        normed = sem("normed2")
        row_stored = sem("row_stored")
        row_free = sem("row_free")
        turned = sem("turned2")
        turn_copied = sem("turn_copied2")
        logit_done = sem("logit_done")
        logit_copied = sem("logit_copied")
        centred = sem("centred2")
        exped = sem("exped2")
        aff_ready = sem("aff_ready")
        aff_stored = sem("aff_stored")

        with nc.Block() as block:
            @block.sync
            def _(sp):
                sp.dma_start(gate[:], gate_w.rearrange("(k p) e -> p k e", p=P)).then_inc(gate_loaded, 16)
                rows = row_dram.rearrange("(b t p) n -> b p t n", p=P, t=TILES)

                def store_rows(b, u):
                    sp.wait_ge(normed, b + 1)
                    sp.dma_start(rows[b], hn[:, u]).then_inc(row_stored, 16)
                    sp.wait_ge(row_stored, 16 * b + 16)
                    sp.sem_inc(row_free, 1)

                with sp.Fori(0, ABLOCKS // 2) as pair:
                    for u in range(2):
                        store_rows(2 * pair + u, u)
                sp.dma_start(out_rows.rearrange("(t p) n -> p t n", p=P), h[:]).then_inc(resid_stored, 16)
                sp.wait_ge(aff_ready, 1)
                sp.dma_start(aff_dram.rearrange("(t p) e -> p t e", p=P), affinity[:]).then_inc(aff_stored, 16)
                sp.wait_ge(aff_stored, 16)
                sp.wait_ge(resid_stored, 16)

            @block.tensor
            def _(pe):
                pe.wait_ge(gate_loaded, 16)

                def turn(b, u, t):
                    if t == 0:
                        pe.wait_ge(normed, b + 1)
                    pe.wait_ge(turn_copied, TILES * b + t + 1)
                    for k in range(KD):
                        last = nc.tensor.transpose(ps_turn[:, t % 2, k, :], hn[:, u, t, k * P:(k + 1) * P], ident[:])
                    last.then_inc(turned, 1)

                def logits(b, t):
                    pe.wait_ge(turn_copied, TILES * b + t + 3)
                    pe.wait_ge(logit_copied, TILES * b + t + 1)
                    for k in range(KD):
                        last = nc.tensor.matmul(ps_logit[:, t % 2, 0:EXPERTS], hnT[:, t % 2, k, :], gate[:, k, :],
                                                start=(k == 0), stop=(k == KD - 1))
                    last.then_inc(logit_done, 1)

                with pe.Fori(0, ABLOCKS // 2) as pair:
                    for u in range(2):
                        for t in range(TILES + 1):
                            if t < TILES:
                                turn(2 * pair + u, u, t)
                            if t:
                                logits(2 * pair + u, t - 1)

            @block.scalar
            def _(act):
                act.sem_inc(turn_copied, 2)
                act.wait_ge(var_ready, 1)
                nc.scalar.activation(rstd[:], rstd[:], ACT.Sqrt).then_inc(std_done, 1)
                with act.Fori(0, ABLOCKS) as b:
                    for t in range(TILES):
                        act.wait_ge(turned, TILES * b + t + 1)
                        nc.scalar.copy(hnT[:, t % 2], ps_turn[:, t % 2]).then_inc(turn_copied, 1)
                act.wait_ge(centred, 1)
                nc.scalar.activation(affinity[:], affinity[:], ACT.Exp).then_inc(exped, 1)

            @block.vector
            def _(dve):
                dve.sem_inc(logit_copied, 2)
                dve.sem_inc(row_free, 2)
                for t in range(NTILES):
                    last = nc.vector.bn_aggr(mean_var[:, t, :], stats[:, t, :])
                last.then_inc(setup, 1)
                dve.wait_ge(setup, 1)
                nc.vector.tensor_scalar(rstd[:], mean_var[:, :, 1], EPS, None, ALU.add).then_inc(var_ready, 1)
                dve.wait_ge(std_done, 1)
                nc.vector.reciprocal(rstd[:], rstd[:]).then_inc(setup, 1)
                dve.wait_ge(setup, 2)

                def layernorm(b, u):
                    dve.wait_ge(row_free, b + 1)
                    for t in range(TILES):
                        n = b * TILES + t
                        last = nc.vector.tensor_scalar(hn[:, u, t, :], h[:, bass.ds(n, 1), :].squeeze(1),
                                                       mean_var[:, bass.ds(n, 1), 0], rstd[:, bass.ds(n, 1)],
                                                       ALU.subtract, ALU.mult)
                    last.then_inc(normed, 1)

                def copy_logits(b):
                    for t in range(TILES):
                        n = b * TILES + t
                        dve.wait_ge(logit_done, n + 1)
                        nc.vector.tensor_copy(affinity[:, bass.ds(n, 1), :].squeeze(1),
                                              ps_logit[:, t % 2, 0:EXPERTS]).then_inc(logit_copied, 1)

                layernorm(0, 0)
                with dve.Fori(0, ABLOCKS // 2 - 1) as pair:
                    layernorm(2 * pair + 1, 1)
                    copy_logits(2 * pair)
                    layernorm(2 * pair + 2, 0)
                    copy_logits(2 * pair + 1)
                layernorm(ABLOCKS - 1, 1)
                copy_logits(ABLOCKS - 2)
                copy_logits(ABLOCKS - 1)
                dve.wait_ge(logit_copied, NTILES + 2)
                wide = [P, NTILES, EXPERTS]
                chain = Chain(dve, setup, 2)
                chain(nc.vector.tensor_reduce(red[:], affinity[:], AX.X, ALU.max))
                nc.vector.tensor_tensor(affinity[:], affinity[:], red[:].unsqueeze(2).broadcast_to(wide),
                                        ALU.subtract).then_inc(centred, 1)
                dve.wait_ge(exped, 1)
                chain(nc.vector.tensor_reduce(red[:], affinity[:], AX.X, ALU.add))
                chain(nc.vector.reciprocal(red[:], red[:]))
                nc.vector.tensor_tensor(affinity[:], affinity[:], red[:].unsqueeze(2).broadcast_to(wide),
                                        ALU.mult).then_inc(aff_ready, 1)


HALVES = BATCH // P
PICKS = TOP * HALVES


def choice_block(nc, aff_dram, row_index, weight):
    with ExitStack() as ctx:
        def sb(name, shape, dt=F32):
            return ctx.enter_context(nc.sbuf_tensor(name, shape, dt))

        def sem(name):
            return ctx.enter_context(nc.semaphore(name))

        wide = [P, HALVES, EXPERTS, PATCH]
        a = sb("aff_in", [P, HALVES, PATCH, EXPERTS])
        by_expert = sb("by_expert", wide)
        best = sb("best", [P, HALVES, EXPERTS])
        place = sb("place", [P, HALVES, EXPERTS])
        hit = sb("hit", wide)
        countdown = sb("countdown", [P, PATCH])
        row_end = sb("row_end", [P, HALVES])
        row_float = sb("row_float", [P, EXPERTS, TOP, HALVES])
        loaded = sem("aff_loaded")
        ramps = sem("ramps")
        picked = sem("picked")

        with nc.Block() as block:
            @block.sync
            def _(sp):
                sp.dma_start(a[:], aff_dram.rearrange("(c p s) e -> p c s e", s=PATCH, p=P)).then_inc(loaded, 16)

            @block.gpsimd
            def _(pool):
                nc.gpsimd.iota(countdown[:], [[-1, PATCH]], base=PATCH, channel_multiplier=0,
                               allow_small_or_imprecise_dtypes=True).then_inc(ramps, 1)
                nc.gpsimd.iota(row_end[:], [[P * PATCH, HALVES]], base=PATCH, channel_multiplier=PATCH,
                               allow_small_or_imprecise_dtypes=True).then_inc(ramps, 1)

            @block.vector
            def _(dve):
                dve.wait_ge(loaded, 16)
                dve.wait_ge(ramps, 2)
                chain = Chain(dve, picked, 0)
                chain(nc.vector.tensor_copy(by_expert[:], a[:].rearrange("p c s e -> p c e s")))
                flat = "p c e s -> p (c e s)"
                for r in range(TOP):
                    chain(nc.vector.tensor_reduce(best[:], by_expert[:], AX.X, ALU.max))
                    chain(nc.vector.tensor_tensor(hit[:], by_expert[:], best[:].unsqueeze(3).broadcast_to(wide),
                                                  ALU.is_equal))
                    ramp = countdown[:].unsqueeze(1).unsqueeze(1).broadcast_to(wide)
                    chain(nc.vector.tensor_tensor(hit[:], hit[:], ramp, ALU.mult))
                    chain(nc.vector.tensor_reduce(place[:], hit[:], AX.X, ALU.max))
                    nc.vector.tensor_copy(weight[:, :, r, :], best[:].rearrange("p c e -> p e c"))
                    chain(nc.vector.tensor_tensor(row_float[:, :, r, :],
                                                  row_end[:].unsqueeze(1).broadcast_to([P, EXPERTS, HALVES]),
                                                  place[:].rearrange("p c e -> p e c"), ALU.subtract))
                    if r < TOP - 1:
                        chain(nc.vector.tensor_tensor(hit[:], ramp, place[:].unsqueeze(3).broadcast_to(wide),
                                                      ALU.is_equal))
                        chain(nc.vector.scalar_tensor_tensor(
                            by_expert[:].rearrange(flat), hit[:].rearrange(flat), -4.0,
                            by_expert[:].rearrange(flat), ALU.mult, ALU.add))
                chain(nc.vector.tensor_copy(row_index[:], row_float[:]))


def expert_block(nc, w1, b1, w2, b2, ident, row_index, weight, row_dram, out_rows):
    with ExitStack() as ctx:
        def sb(name, shape, dt=F32):
            return ctx.enter_context(nc.sbuf_tensor(name, shape, dt))

        def psum(name, shape):
            return ctx.enter_context(nc.psum_tensor(name, shape, F32))

        def sem(name):
            return ctx.enter_context(nc.semaphore(name))

        w1_sb = sb("w1_sb", [P, 2, KD, D])
        w2_sb = sb("w2_sb", [P, 2, KD, D])
        b2_sb = sb("b2_sb", [P, 2, D])
        b1_rows = sb("b1_rows", [EXPERTS * KD, P])
        b1_col = sb("b1_col", [P, EXPERTS, KD])
        index = sb("index", [P, 2, PICKS], I32)
        picked = sb("picked", [P, 2, PICKS, D])
        xT = sb("pickedT", [P, KD, PICKS * P])
        hiddenT = sb("hiddenT", [P, KD, PICKS * P])
        result = sb("result", [P, 2, PICKS, D])
        ps_turn = psum("ps_turn3", [P, 2, KD, P])
        ps_hid = psum("ps_hid3", [P, 2, PICKS * P])
        ps_out = psum("ps_out3", [P, 2, D])

        w_loaded = [sem(f"w_loaded{s}") for s in range(2)]
        b1_loaded = sem("b1_loaded")
        b1_turned = sem("b1_turned")
        b1_ready = sem("b1_ready")
        index_ready = sem("index_ready")
        gathered = [sem(f"gathered{s}") for s in range(2)]
        scattered = sem("scattered")
        turned = sem("turned3")
        turn_copied = sem("turn_copied3")
        hid_done = sem("hid_done")
        gelu_done = sem("gelu_done3")
        out_done = sem("out_done")
        out_copied = sem("out_copied")
        weighted = sem("weighted")
        waits_passed = sem("waits_passed")
        result_free = sem("result_free")

        with nc.Block() as block:
            @block.sync
            def _(sp):
                sp.dma_start(b1_rows[:], b1.rearrange("e (k p) -> (e k) p", p=P)).then_inc(b1_loaded, 16)
                b2_row = b2.rearrange("(e a) n -> e a n", a=1)

                def load(e, u):
                    sp.dma_start(w1_sb[:, u], w1[e].rearrange("(k p) n -> p k n", p=P)).then_inc(w_loaded[u], 16)
                    sp.dma_start(w2_sb[:, u], w2[e].rearrange("(k p) n -> p k n", p=P)).then_inc(w_loaded[u], 16)
                    sp.dma_start(b2_sb[:, u], b2_row[e].broadcast_to([P, D])).then_inc(w_loaded[u], 16)

                load(0, 0)
                load(1, 1)
                with sp.Fori(1, EXPERTS // 2) as pair:
                    for u in range(2):
                        sp.wait_ge(out_copied, PICKS * (2 * pair + u - 1) + 2)
                        load(2 * pair + u, u)

            @block.gpsimd
            def _(pool):
                def gather(e, u):
                    nc.gpsimd.tensor_copy(index[:, u], row_index[:, bass.ds(e, 1)].rearrange("p e r c -> p (e r c)")
                                          ).then_inc(index_ready, 1)
                    pool.wait_ge(index_ready, e + 1)
                    pool.sem_inc(waits_passed, 1)
                    for j in range(PICKS):
                        nc.gpsimd.indirect_dma_start(
                            picked[:, u, j, :], None, row_dram,
                            bass.IndirectOffsetOnAxis(ap=index[:, u, j:j + 1].bitcast(U32), axis=0)
                        ).then_inc(gathered[u], 16)

                def scatter(e, u):
                    for j in range(PICKS):
                        pool.wait_ge(weighted, PICKS * e + j + 1)
                        pool.sem_inc(waits_passed, 1)
                        nc.gpsimd.indirect_dma_start(
                            out_rows, bass.IndirectOffsetOnAxis(ap=index[:, u, j:j + 1].bitcast(U32), axis=0),
                            result[:, u, j, :], None, compute_op=ALU.add).then_inc(scattered, 16)

                def run(e, u, ahead):
                    scatter(e, u)
                    pool.wait_ge(scattered, 16 * PICKS * (e + 1))
                    pool.sem_inc(result_free, 1)
                    if ahead:
                        pool.wait_ge(turned, PICKS * (e + 1))
                        gather(e + 2, u)

                gather(0, 0)
                gather(1, 1)
                with pool.Fori(0, EXPERTS // 2 - 1) as pair:
                    for u in range(2):
                        run(2 * pair + u, u, True)
                run(EXPERTS - 2, 0, False)
                run(EXPERTS - 1, 1, False)

            @block.tensor
            def _(pe):
                pe.wait_ge(b1_loaded, 16)
                nc.tensor.transpose(ps_out[:, 0, 0:EXPERTS * KD], b1_rows[:], ident[0:EXPERTS * KD, 0:EXPERTS * KD]
                                    ).then_inc(b1_turned, 1)
                pe.wait_ge(b1_ready, 1)

                def turn(e, u):
                    pe.wait_ge(gathered[u], 8 * PICKS * (e - u) + 16 * PICKS)
                    for j in range(PICKS):
                        pe.wait_ge(turn_copied, PICKS * e + j + 1)
                        for k in range(KD):
                            last = nc.tensor.transpose(ps_turn[:, j % 2, k, :], picked[:, u, j, k * P:(k + 1) * P],
                                                       ident[:])
                        last.then_inc(turned, 1)

                def up(e, u):
                    pe.wait_ge(turn_copied, PICKS * e + PICKS + 2)
                    pe.wait_ge(w_loaded[u], 24 * (e - u) + 48)
                    for m in range(KD):
                        pe.wait_ge(gelu_done, KD * e + m + 1)
                        for k in range(KD):
                            last = nc.tensor.matmul(ps_hid[:, m % 2, :], w1_sb[:, u, k, m * P:(m + 1) * P],
                                                    xT[:, k, :], start=(k == 0), stop=(k == KD - 1))
                        last.then_inc(hid_done, 1)

                def down(e, u):
                    pe.wait_ge(gelu_done, KD * e + KD + 2)
                    for j in range(PICKS):
                        pe.wait_ge(out_copied, PICKS * e + j + 1)
                        for k in range(KD):
                            last = nc.tensor.matmul(ps_out[:, j % 2, :], hiddenT[:, k, j * P:(j + 1) * P],
                                                    w2_sb[:, u, k, :], start=(k == 0), stop=(k == KD - 1))
                        last.then_inc(out_done, 1)

                turn(0, 0)
                with pe.Fori(0, EXPERTS // 2 - 1) as pair:
                    for u in range(2):
                        up(2 * pair + u, u)
                        turn(2 * pair + u + 1, 1 - u)
                        down(2 * pair + u, u)
                up(EXPERTS - 2, 0)
                turn(EXPERTS - 1, 1)
                down(EXPERTS - 2, 0)
                up(EXPERTS - 1, 1)
                down(EXPERTS - 1, 1)

            @block.scalar
            def _(act):
                act.sem_inc(gelu_done, 2)
                act.wait_ge(b1_ready, 1)

                def weigh(e, u):
                    for j in range(PICKS):
                        act.wait_ge(out_copied, PICKS * e + j + 3)
                        scale = weight[:, bass.ds(e, 1)].rearrange("p e r c -> p (e r c)")[:, j:j + 1]
                        nc.scalar.activation(result[:, u, j, :], result[:, u, j, :], ACT.Copy, scale=scale
                                             ).then_inc(weighted, 1)

                def gelu(e):
                    for m in range(KD):
                        act.wait_ge(hid_done, KD * e + m + 1)
                        nc.scalar.activation(hiddenT[:, m, :], ps_hid[:, m % 2, :], ACT.Gelu_apprx_tanh,
                                             bias=b1_col[:, bass.ds(e, 1), m]).then_inc(gelu_done, 1)

                with act.Fori(0, EXPERTS // 2) as pair:
                    for u in range(2):
                        gelu(2 * pair + u)
                        weigh(2 * pair + u, u)

            @block.vector
            def _(dve):
                dve.sem_inc(turn_copied, 2)
                dve.sem_inc(out_copied, 2)
                dve.sem_inc(result_free, 2)
                dve.wait_ge(b1_turned, 1)
                nc.vector.tensor_copy(b1_col[:].rearrange("p e k -> p (e k)"), ps_out[:, 0, 0:EXPERTS * KD]
                                      ).then_inc(b1_ready, 1)

                def copy_turned(e):
                    for j in range(PICKS):
                        dve.wait_ge(turned, PICKS * e + j + 1)
                        nc.vector.tensor_copy(xT[:, :, j * P:(j + 1) * P], ps_turn[:, j % 2]).then_inc(turn_copied, 1)

                def copy_out(e, u):
                    dve.wait_ge(result_free, e + 1)
                    for j in range(PICKS):
                        dve.wait_ge(out_done, PICKS * e + j + 1)
                        nc.vector.tensor_tensor(result[:, u, j, :], ps_out[:, j % 2, :], b2_sb[:, u, :], ALU.add
                                                ).then_inc(out_copied, 1)

                copy_turned(0)
                copy_turned(1)
                copy_out(0, 0)
                with dve.Fori(0, EXPERTS // 2 - 1) as pair:
                    for u in range(2):
                        copy_turned(2 * pair + u + 2)
                        copy_out(2 * pair + u + 1, 1 - u)
                copy_out(EXPERTS - 1, 1)


def audio_tower(nc, x, adj, tok_w1, tok_w2, wp, W_in, b_in, Wq, Wk, Wv, W_out, b_out, gate_w, w1, b1, w2, b2, out):
    def scratch(name, shape):
        return nc.dram_tensor(name, shape, F32, kind="Internal").ap()

    wfold_dram = scratch("wfold_dram", [PARTS, NPAD * PATCH, D])
    y_dram = scratch("y_dram", [BLOCKS, NPAD, PATCH, TB])
    h_dram = scratch("h_dram", [TOK, D])
    row_dram = scratch("row_dram", [TOK, D])
    aff_dram = scratch("aff_dram", [TOK, EXPERTS])
    out_rows = out.rearrange("b p n -> (b p) n")

    with ExitStack() as whole:
        def sb(ctx, name, shape, dt=F32):
            return ctx.enter_context(nc.sbuf_tensor(name, shape, dt))

        ident = sb(whole, "ident", [P, P])
        stats = sb(whole, "stats", [P, NTILES, 6])
        row_index = sb(whole, "row_index", [P, EXPERTS, TOP, HALVES], I32)
        weight = sb(whole, "weight", [P, EXPERTS, TOP, HALVES])
        with ExitStack() as ctx:
            adjT = sb(ctx, "adjT", [P, PARTS, WINDOWS, NPAD], F32R)
            w1pair = sb(ctx, "w1pair", [P, PARTS, 2, P], F32R)
            w2pair = sb(ctx, "w2pair", [P, 32])
            wfold = sb(ctx, "wfold", [P, PARTS, CHUNKS, D], F32R)
            fold_block(nc, adj, wp, tok_w1, tok_w2, wfold_dram, ident, adjT, w1pair, w2pair, wfold)
            tokenizer_block(nc, x, y_dram, h_dram, ident, adjT, w1pair, w2pair, wfold, stats)
        with ExitStack() as ctx:
            h = sb(ctx, "h", [P, NTILES, D])
            attention_block(nc, h_dram, W_in, b_in, Wq, Wk, Wv, W_out, b_out, ident, h, stats)
            routing_block(nc, gate_w, ident, h, stats, row_dram, aff_dram, out_rows)
        choice_block(nc, aff_dram, row_index, weight)
        expert_block(nc, w1, b1, w2, b2, ident, row_index, weight, row_dram, out_rows)


_INS = ['x', 'L0_tok_adj', 'L0_tok_w1', 'L0_tok_w2', 'L0_tok_wp', 'L0_attn_W_in', 'L0_attn_b_in', 'L0_attn_Wq',
        'L0_attn_Wk', 'L0_attn_Wv', 'L0_attn_W_out', 'L0_attn_b_out', 'L0_ffn_gate_weight', 'L0_ffn_w1',
        'L0_ffn_b1', 'L0_ffn_w2', 'L0_ffn_b2']
_OUT = ((BATCH, PATCH, D), 'float32')


def kernel(**inputs):
    import numpy as _np
    import concourse.bacc as _bacc
    from concourse.bass_utils import run_bass_kernel_spmd as _run

    nc = _bacc.Bacc("TRN2", target_bir_lowering=False, num_devices=1)
    arrays, args = {}, []
    for name in _INS:
        a = _np.ascontiguousarray(inputs[name])
        arrays[f"in_{name}"] = a
        args.append(nc.dram_tensor(f"in_{name}", a.shape, mybir.dt.from_np(a.dtype), kind="ExternalInput").ap())
    out = nc.dram_tensor("out", _OUT[0], mybir.dt.from_np(_np.dtype(_OUT[1])), kind="ExternalOutput").ap()
    audio_tower(nc, *args, out)
    r = _run(nc, [arrays], core_ids=[0])
    return r.results[0]["out"]
```

```python
from contextlib import ExitStack

import concourse.bass as bass
from concourse import mybir

F32 = mybir.dt.float32
F32R = mybir.dt.float32r
I32 = mybir.dt.int32
U32 = mybir.dt.uint32
ALU = mybir.AluOpType
ACT = mybir.ActivationFunctionType
AX = mybir.AxisListType

P = 128
BANK = 512
BATCH = 256
PATCH = 16
NODES = 207
HID = 64
D = 512
KD = D // P
TOK = BATCH * PATCH
NPAD = 208
CHUNKS = NPAD * PATCH // P
NODE_SPLIT = ((0, P), (P, NPAD - P))
M_START = (0, NODES - P)
OVERLAP = 2 * P - NODES
EPS = 1e-5

TB = 256
SUBS = TB // P
BLOCKS = TOK // TB
DG = 2
GROUPS = PATCH // DG
WINDOWS = 2

PARTS = 2
PART_HIGH, PART_LOW = range(PARTS)
PRODUCTS = ((PART_HIGH, PART_HIGH), (PART_HIGH, PART_LOW), (PART_LOW, PART_HIGH))

HEADS = 8
DH = 64
SLICE = 32
QUADS = 2
EXPERTS = 16
TOP = 2
HALVES = BATCH // P
PICKS = TOP * HALVES


def make_identity(nc, pool, ident, sem):
    nc.gpsimd.memset(ident[:], 0.0).then_inc(sem, 1)
    pool.wait_ge(sem, 1)
    nc.gpsimd.affine_select(out=ident[:], in_=ident[:], compare_op=ALU.not_equal, fill=1.0, base=0,
                            pattern=[[-1, P]], channel_multiplier=1).then_inc(sem, 1)


def high(ap):
    return ap.bitcast(F32)


class Front:

    FILLS = 2 * WINDOWS

    def __init__(self, nc, ctx, x, y_dram, ident):
        def sb(name, shape, dt=F32):
            return ctx.enter_context(nc.sbuf_tensor(name, shape, dt))

        def sem(name):
            return ctx.enter_context(nc.semaphore(name))

        self.nc, self.y_dram, self.ident = nc, y_dram, ident
        self.x_tok = x.rearrange("b (p s) f -> (b p) s f", s=PATCH)
        self.x_in = sb("x_in", [P, 2, SUBS, DG, NODES])
        self.xT = sb("xT", [P, 2, PARTS, WINDOWS, DG, TB], F32R)
        self.y = sb("y", [P, 2, 2, DG, TB])
        self.adjT = sb("adjT", [P, PARTS, WINDOWS, NPAD], F32R)
        self.ps_front = ctx.enter_context(nc.psum_tensor("ps_front", [P, 2, BANK], F32))
        self.x_loaded = [sem(f"x_loaded{s}") for s in range(2)]
        self.front_filled = sem("front_filled")
        self.x_high = sem("x_high")
        self.front_copied = sem("front_copied")
        self.y_stored = [sem(f"y_stored{s}") for s in range(2)]

    def load_x(self, pool, b, dg):
        for s in range(SUBS):
            pool.dma_start(self.x_in[:, dg % 2, s],
                           self.x_tok[bass.ds(b * TB + s * P, P), dg * DG:(dg + 1) * DG, :]
                           ).then_inc(self.x_loaded[dg % 2], 16)

    def load_x_next(self, pool, b, dg):
        pool.wait_ge(self.front_filled, self.FILLS * (GROUPS * b + dg - 2) + WINDOWS)
        self.load_x(pool, b, dg)

    def turn_x(self, pe, b, dg, first=False):
        slot = dg % 2
        pe.wait_ge(self.x_loaded[slot], 16 * GROUPS * b + 32 * (dg // 2) + 32)
        for c in range(WINDOWS):
            if not first:
                pe.wait_ge(self.front_copied, self.FILLS * (GROUPS * b + dg) + c - 1)
            for e in range(DG):
                for s in range(SUBS):
                    last = self.nc.tensor.transpose(
                        self.ps_front[:, c, e * TB + s * P:e * TB + (s + 1) * P],
                        self.x_in[:, slot, s, e, M_START[c]:M_START[c] + P], self.ident[:])
            last.then_inc(self.front_filled, 1)

    def adjacency(self, pe, b, dg):
        pe.wait_ge(self.front_copied, self.FILLS * (GROUPS * b + dg) + WINDOWS)
        for j, (n0, nn) in enumerate(NODE_SPLIT):
            terms = [(c, a, v) for c in range(WINDOWS) for a, v in PRODUCTS]
            for n, (c, a, v) in enumerate(terms):
                last = self.nc.tensor.matmul(self.ps_front[0:nn, j, :], self.adjT[:, a, c, n0:n0 + nn],
                                             self.xT[:, dg % 2, v, c], start=(n == 0), stop=(n == len(terms) - 1))
            last.then_inc(self.front_filled, 1)

    def x_high_part(self, act, b, dg):
        for c in range(WINDOWS):
            act.wait_ge(self.front_filled, self.FILLS * (GROUPS * b + dg) + c + 1)
            self.nc.scalar.copy(self.xT[:, dg % 2, PART_HIGH, c],
                                self.ps_front[:, c, :].rearrange("p (s t) -> p s t", s=DG)).then_inc(self.x_high, 1)

    def x_low_part(self, dve, b, dg):
        for c in range(WINDOWS):
            dve.wait_ge(self.x_high, WINDOWS * (GROUPS * b + dg) + c + 1)
            self.nc.vector.tensor_tensor(self.xT[:, dg % 2, PART_LOW, c],
                                         self.ps_front[:, c, :].rearrange("p (s t) -> p s t", s=DG),
                                         high(self.xT[:, dg % 2, PART_HIGH, c]), ALU.subtract
                                         ).then_inc(self.front_copied, 1)

    def copy_y(self, dve, b, dg, first=False):
        if not first:
            dve.wait_ge(self.y_stored[dg % 2], 16 * GROUPS * b + 32 * (dg // 2))
        for j, (n0, nn) in enumerate(NODE_SPLIT):
            dve.wait_ge(self.front_filled, self.FILLS * (GROUPS * b + dg) + WINDOWS + j + 1)
            self.nc.vector.tensor_copy(self.y[0:nn, dg % 2, j],
                                       self.ps_front[0:nn, j, :].rearrange("p (s t) -> p s t", s=DG)
                                       ).then_inc(self.front_copied, 1)

    def store_y(self, sp, b, dg):
        sp.wait_ge(self.front_copied, self.FILLS * (GROUPS * b + dg + 1))
        for j, (n0, nn) in enumerate(NODE_SPLIT):
            sp.dma_start(self.y_dram[b, n0:n0 + nn, dg * DG:(dg + 1) * DG, :],
                         self.y[0:nn, dg % 2, j]).then_inc(self.y_stored[dg % 2], 16)

    def y_whole(self, sp, b):
        for s in range(2):
            sp.wait_ge(self.y_stored[s], 16 * GROUPS * (b + 1))


def fold_block(nc, adj, wp, w1, w2, wfold_dram, ident, w1pair, w2pair, front):
    adjT = front.adjT
    EG = 2
    NEG = PATCH // EG
    wp_rows = wp.rearrange("(m e) n -> m e n", e=PATCH)
    wfold_rows = wfold_dram.rearrange("r (m e) n -> r m e n", e=PATCH)
    with ExitStack() as ctx:
        def sb(name, shape, dt=F32):
            return ctx.enter_context(nc.sbuf_tensor(name, shape, dt))

        def sem(name):
            return ctx.enter_context(nc.semaphore(name))

        adj_rows = sb("adj_rows", [P, 2, NODES])
        adj_fold = sb("adj_fold", [P, WINDOWS, NPAD])
        w1_wide = sb("w1_wide", [P, 2, P])
        wp_in = sb("wp_in", [P, 2, WINDOWS, EG, D])
        wfold_out = sb("wfold_out", [P, 2, 2, PARTS, EG, D], F32R)
        ps_adj = ctx.enter_context(nc.psum_tensor("ps_adj", [P, 4, P], F32))
        ps_fold = ctx.enter_context(nc.psum_tensor("ps_fold", [P, 4, BANK], F32))

        adj_loaded = sem("adj_loaded")
        fold_cleared = sem("fold_cleared")
        fold_adj_loaded = sem("fold_adj_loaded")
        adj_fold_ready = sem("adj_fold_ready")
        ident_ready = sem("ident_ready")
        cleared = sem("cleared")
        small_loaded = sem("small_loaded")
        adj_turned = sem("adj_turned")
        adjT_copied = sem("adjT_copied")
        adjT_whole = sem("adjT_whole")
        w1_split = sem("w1_split")
        wp_loaded = [sem(f"wp_loaded{s}") for s in range(2)]
        fold_done = sem("fold_done")
        fold_high = sem("fold_high")
        fold_copied = sem("fold_copied")
        fold_stored = [sem(f"fold_stored{s}") for s in range(2)]

        with nc.Block() as block:
            @block.sync
            def _(sp):
                def load_wp(g):
                    for c, m0 in enumerate(M_START):
                        sp.dma_start(wp_in[:, g % 2, c], wp_rows[m0:m0 + P, g * EG:(g + 1) * EG, :]
                                     ).then_inc(wp_loaded[g % 2], 16)

                for j, (n0, nn) in enumerate(((0, P), (P, NODES - P))):
                    sp.dma_start(adj_rows[0:nn, j, :], adj[n0:n0 + nn, :]).then_inc(adj_loaded, 16)
                sp.wait_ge(fold_cleared, 1)
                for c, m0 in enumerate(M_START):
                    sp.dma_start(adj_fold[:, c, 0:NODES], adj[m0:m0 + P, :]).then_inc(fold_adj_loaded, 16)
                load_wp(0)
                load_wp(1)
                for g in range(NEG):
                    sp.wait_ge(fold_copied, 2 * EG * (g + 1))
                    if g + 2 < NEG:
                        load_wp(g + 2)
                    for j, (n0, nn) in enumerate(NODE_SPLIT):
                        for r in range(PARTS):
                            sp.dma_start(wfold_rows[r, n0:n0 + nn, g * EG:(g + 1) * EG, :],
                                         high(wfold_out[0:nn, g % 2, j, r])).then_inc(fold_stored[g % 2], 16)
                    front.store_y(sp, 0, g)
                front.y_whole(sp, 0)
                for s in range(2):
                    sp.wait_ge(fold_stored[s], 16 * 2 * PARTS * NEG // 2)

            @block.gpsimd
            def _(pool):
                make_identity(nc, pool, ident, ident_ready)
                front.load_x(pool, 0, 0)
                front.load_x(pool, 0, 1)
                nc.gpsimd.memset(w1_wide[:], 0.0).then_inc(cleared, 1)
                nc.gpsimd.memset(w2pair[:], 0.0).then_inc(cleared, 1)
                pool.wait_ge(cleared, 2)
                for i in range(2):
                    for half in range(2):
                        for n in range(2):
                            row = half * 64 + 32 * i + PATCH * n
                            pool.dma_start(w1_wide[row:row + PATCH, i, n * HID:(n + 1) * HID], w1
                                           ).then_inc(small_loaded, 16)
                for i in range(2):
                    pool.dma_start(w2pair[i * HID:(i + 1) * HID, i * PATCH:(i + 1) * PATCH],
                                   w2).then_inc(small_loaded, 16)
                for dg in range(2, GROUPS + 2):
                    front.load_x_next(pool, dg // GROUPS, dg % GROUPS)

            @block.scalar
            def _(act):
                for g in range(NEG):
                    if g >= 2:
                        act.wait_ge(fold_stored[g % 2], 16 * 2 * PARTS * (g // 2))
                    for e in range(EG):
                        for j, (n0, nn) in enumerate(NODE_SPLIT):
                            n = 2 * (EG * g + e) + j
                            act.wait_ge(fold_done, n + 1)
                            nc.scalar.copy(wfold_out[0:nn, g % 2, j, PART_HIGH, e, :], ps_fold[0:nn, n % 4, :]
                                           ).then_inc(fold_high, 1)
                        if e == 0:
                            front.x_high_part(act, 0, g)

            @block.tensor
            def _(pe):
                pe.wait_ge(ident_ready, 2)
                pe.wait_ge(adj_loaded, 32)
                for c, m0 in enumerate(M_START):
                    for j, nn in enumerate((P, NODES - P)):
                        last = nc.tensor.transpose(ps_adj[:, 2 * c + j, 0:nn], adj_rows[0:nn, j, m0:m0 + P],
                                                   ident[0:nn, 0:nn])
                last.then_inc(adj_turned, 1)
                pe.wait_ge(adj_fold_ready, 1)
                for g in range(NEG):
                    pe.wait_ge(wp_loaded[g % 2], 32 * (g // 2 + 1))
                    for e in range(EG):
                        for j, (n0, nn) in enumerate(NODE_SPLIT):
                            n = 2 * (EG * g + e) + j
                            if n >= 4:
                                pe.wait_ge(fold_copied, n - 3)
                            for c in range(WINDOWS):
                                last = nc.tensor.matmul(ps_fold[0:nn, n % 4, :], adj_fold[:, c, n0:n0 + nn],
                                                        wp_in[:, g % 2, c, e, :], start=(c == 0),
                                                        stop=(c == WINDOWS - 1))
                            last.then_inc(fold_done, 1)
                        if e == 0:
                            front.turn_x(pe, 0, g, first=(g == 0))
                    if g == 0:
                        pe.wait_ge(adjT_whole, 1)
                    front.adjacency(pe, 0, g)

            @block.vector
            def _(dve):
                nc.vector.memset(adj_fold[:], 0.0).then_inc(fold_cleared, 1)
                nc.vector.memset(high(adjT[:]), 0.0).then_inc(adjT_copied, 1)
                dve.wait_ge(fold_adj_loaded, 32)
                nc.vector.memset(adj_fold[0:OVERLAP, 1, :], 0.0).then_inc(adj_fold_ready, 1)
                dve.wait_ge(adjT_copied, 1)
                dve.wait_ge(adj_turned, 1)
                done = 1
                for part in range(PARTS):
                    for c in range(WINDOWS):
                        for j, nn in enumerate((P, NODES - P)):
                            cols = slice(j * P, j * P + nn)
                            if part == PART_HIGH:
                                last = nc.vector.tensor_copy(adjT[:, part, c, cols], ps_adj[:, 2 * c + j, 0:nn])
                            else:
                                last = nc.vector.tensor_tensor(adjT[:, part, c, cols], ps_adj[:, 2 * c + j, 0:nn],
                                                               high(adjT[:, PART_HIGH, c, cols]), ALU.subtract)
                            last.then_inc(adjT_copied, 1)
                            done += 1
                    dve.wait_ge(adjT_copied, done)
                nc.vector.memset(high(adjT[0:OVERLAP, :, 1, :]), 0.0).then_inc(adjT_whole, 1)
                dve.wait_ge(small_loaded, 16 * 10)
                nc.vector.tensor_copy(w1pair[:, PART_HIGH], w1_wide[:]).then_inc(w1_split, 1)
                dve.wait_ge(w1_split, 1)
                nc.vector.tensor_tensor(w1pair[:, PART_LOW], w1_wide[:], high(w1pair[:, PART_HIGH]), ALU.subtract)
                for g in range(NEG):
                    for e in range(EG):
                        for j, (n0, nn) in enumerate(NODE_SPLIT):
                            n = 2 * (EG * g + e) + j
                            dve.wait_ge(fold_high, n + 1)
                            nc.vector.tensor_tensor(wfold_out[0:nn, g % 2, j, PART_LOW, e, :], ps_fold[0:nn, n % 4, :],
                                                    high(wfold_out[0:nn, g % 2, j, PART_HIGH, e, :]), ALU.subtract
                                                    ).then_inc(fold_copied, 1)
                        if e == 0:
                            front.x_low_part(dve, 0, g)
                    front.copy_y(dve, 0, g, first=(g < 2))


def tokenizer_block(nc, front, y_dram, wfold_dram, h_dram, w1pair, w2pair, wfold, stats):
    h_rows = h_dram.rearrange("(b s p) n -> b p s n", p=P, s=SUBS)
    PAIRS = CHUNKS // 2
    LOADS = ((0, 6), (6, 13), (13, 19), (19, CHUNKS))
    with ExitStack() as ctx:
        def sb(name, shape, dt=F32):
            return ctx.enter_context(nc.sbuf_tensor(name, shape, dt))

        def psum(name, shape):
            return ctx.enter_context(nc.psum_tensor(name, shape, F32))

        def sem(name):
            return ctx.enter_context(nc.semaphore(name))

        y_turned = sb("y_turned", [P, CHUNKS, TB])
        y_split = sb("y_split", [P, 2, 2, TB], F32R)
        hidden = sb("hidden", [P, 2, 2, BANK])
        g_sb = sb("g_sb", [P, 2, PARTS, 2, TB], F32R)
        h_out = sb("h_out", [P, 2, SUBS, D])

        ps_hid = psum("ps_hid", [P, 2, BANK])
        ps_g = psum("ps_g", [P, 2, BANK])
        ps_h = psum("ps_h", [P, SUBS, BANK])

        wfold_loaded = [sem(f"wfold_loaded{s}") for s in range(len(LOADS))]
        y_loaded = [sem(f"y_loaded{s}") for s in range(len(LOADS))]
        y_high = sem("y_high")
        y_low = sem("y_low")
        hid_filled = sem("hid_filled")
        gelu_done = sem("gelu_done")
        g_filled = sem("g_filled")
        g_high = sem("g_high")
        g_copied = sem("g_copied")
        proj_done = sem("proj_done")
        h_copied = sem("h_copied")
        h_stored = sem("h_stored")
        h_free = sem("h_free")

        def part_of(k):
            return [lo <= k < hi for lo, hi in LOADS].index(True)

        def load_wfold(eng, n):
            lo, hi = LOADS[n]
            for r in range(PARTS):
                eng.dma_start(high(wfold[:, r, lo:hi]), wfold_dram[r].rearrange("(c p) n -> p c n", p=P)[:, lo:hi]
                              ).then_inc(wfold_loaded[n], 16)

        with nc.Block() as block:
            @block.gpsimd
            def _(pool):
                for dg in range(2, GROUPS):
                    front.load_x_next(pool, 1, dg)
                    if dg % 2:
                        load_wfold(pool, dg // 2)
                with pool.Fori(2, BLOCKS) as b:
                    for dg in range(GROUPS):
                        front.load_x_next(pool, b, dg)

            @block.sync
            def _(sp):
                def store_y(b):
                    for dg in range(GROUPS):
                        front.store_y(sp, b, dg)
                    front.y_whole(sp, b)

                def load_y(b, first=False):
                    rows = y_dram[b].rearrange("n s t -> (n s) t").rearrange("(c p) t -> p c t", p=P)
                    for n, (lo, hi) in enumerate(LOADS):
                        if not first:
                            sp.wait_ge(y_low, CHUNKS * (b - 1) + hi)
                        sp.dma_start(y_turned[:, lo:hi], rows[:, lo:hi]).then_inc(y_loaded[n], 16)
                        if first and n == 0:
                            load_wfold(sp, n)

                def store_h(b, u):
                    sp.wait_ge(h_copied, b + 2)
                    sp.dma_start(h_rows[b], h_out[:, u]).then_inc(h_stored, 16)
                    sp.wait_ge(h_stored, 16 * b + 16)
                    sp.sem_inc(h_free, 1)

                load_y(0, first=True)
                with sp.Fori(0, BLOCKS - 2, 2) as b:
                    for u in range(2):
                        store_y(b + u + 1)
                        load_y(b + u + 1)
                        store_h(b + u, u)
                store_y(BLOCKS - 1)
                load_y(BLOCKS - 1)
                store_h(BLOCKS - 2, 0)
                store_h(BLOCKS - 1, 1)

            @block.tensor
            def _(pe):
                pe.sem_inc(g_filled, 2)
                pe.sem_inc(proj_done, 2)

                def expand(b, k):
                    pe.wait_ge(y_low, CHUNKS * b + k + 1)
                    for half in range(2):
                        pe.wait_ge(gelu_done, 2 * CHUNKS * b + 2 * k + half + 1)
                        for i in range(2):
                            for part in range(PARTS):
                                last = nc.tensor.matmul(ps_hid[:, half, i * TB:(i + 1) * TB], w1pair[:, part, i, :],
                                                        y_split[:, k % 2, half, :], start=(part == 0),
                                                        stop=(part == PARTS - 1))
                        last.then_inc(hid_filled, 1)

                def contract(b, u, k):
                    bank = (PAIRS * u + k // 2) % 2
                    pe.wait_ge(gelu_done, 2 * CHUNKS * b + 2 * k + 4)
                    if k % 2 == 0:
                        pe.wait_ge(g_copied, PAIRS * b + k // 2 + 1)
                    for q in range(4):
                        last = nc.tensor.matmul(ps_g[32 * q:32 * (q + 1), bank, (k % 2) * TB:(k % 2 + 1) * TB],
                                                w2pair[:], hidden[:, k % 2, q // 2, (q % 2) * TB:(q % 2 + 1) * TB],
                                                start=True, stop=True)
                    last.then_inc(g_filled, 1)

                def project(b, u, k):
                    slot = (PAIRS * u + k // 2) % 2
                    if k % 2 == 0:
                        pe.wait_ge(g_copied, PAIRS * b + k // 2 + 3)
                    if k in [lo for lo, _ in LOADS]:
                        pe.wait_ge(wfold_loaded[part_of(k)], 16 * PARTS)
                    if k == 0:
                        pe.wait_ge(h_copied, b + 1)
                    for s in range(SUBS):
                        for n, (a, v) in enumerate(PRODUCTS):
                            last = nc.tensor.matmul(ps_h[:, s, :], g_sb[:, slot, a, k % 2, s * P:(s + 1) * P],
                                                    wfold[:, v, k, :], start=(k == 0 and n == 0),
                                                    stop=(k == CHUNKS - 1 and n == len(PRODUCTS) - 1))
                    if k % 2 == 1:
                        last.then_inc(proj_done, 1)

                def run_block(b, u, ahead):
                    for step in range(CHUNKS + 3):
                        if step < CHUNKS:
                            expand(b, step)
                        if ahead and step < 2 * GROUPS:
                            (front.adjacency if step % 2 else front.turn_x)(pe, b + 1, step // 2)
                        if 1 <= step <= CHUNKS:
                            contract(b, u, step - 1)
                        if step >= 3:
                            project(b, u, step - 3)

                with pe.Fori(0, BLOCKS - 2, 2) as b:
                    run_block(b, 0, True)
                    run_block(b + 1, 1, True)
                run_block(BLOCKS - 2, 0, True)
                run_block(BLOCKS - 1, 1, False)

            @block.scalar
            def _(act):
                act.sem_inc(gelu_done, 2)

                def y_part(b, k):
                    if k in [lo for lo, _ in LOADS]:
                        act.wait_ge(y_loaded[part_of(k)], 16 * b + 16)
                    for half in range(2):
                        rows = slice(64 * half, 64 * half + 64)
                        last = nc.scalar.copy(y_split[rows, k % 2, half, :], y_turned[rows, k, :])
                    last.then_inc(y_high, 1)

                def gelu(b, k):
                    act.wait_ge(g_filled, CHUNKS * b + k + 1)
                    for half in range(2):
                        act.wait_ge(hid_filled, 2 * CHUNKS * b + 2 * k + half + 1)
                        nc.scalar.activation(hidden[:, k % 2, half], ps_hid[:, half, :], ACT.Gelu
                                             ).then_inc(gelu_done, 1)

                def g_part(b, u, pair):
                    slot = (PAIRS * u + pair) % 2
                    act.wait_ge(g_filled, CHUNKS * b + 2 * pair + 4)
                    act.wait_ge(proj_done, PAIRS * b + pair + 1)
                    nc.scalar.copy(g_sb[:, slot, PART_HIGH], ps_g[:, slot, :].rearrange("p (c t) -> p c t", c=2)
                                   ).then_inc(g_high, 1)

                def run_block(b, u, ahead):
                    for step in range(CHUNKS + 1):
                        if step + 1 < CHUNKS:
                            y_part(b, step + 1)
                        elif step + 1 == CHUNKS and ahead:
                            y_part(b + 1, 0)
                        if step < CHUNKS:
                            gelu(b, step)
                        if ahead and step < 2 * GROUPS and step % 2 == 0:
                            front.x_high_part(act, b + 1, step // 2)
                        if step >= 2 and step % 2 == 0:
                            g_part(b, u, step // 2 - 1)

                y_part(0, 0)
                with act.Fori(0, BLOCKS - 2, 2) as b:
                    run_block(b, 0, True)
                    run_block(b + 1, 1, True)
                run_block(BLOCKS - 2, 0, True)
                run_block(BLOCKS - 1, 1, False)

            @block.vector
            def _(dve):
                dve.sem_inc(g_copied, 2)
                dve.sem_inc(h_copied, 1)
                dve.sem_inc(h_free, 2)

                def y_part(b, k):
                    dve.wait_ge(y_high, CHUNKS * b + k + 1)
                    for half in range(2):
                        rows, other = slice(64 * half, 64 * half + 64), slice(64 - 64 * half, 128 - 64 * half)
                        last = nc.vector.tensor_tensor(y_split[other, k % 2, half, :], y_turned[rows, k, :],
                                                       high(y_split[rows, k % 2, half, :]), ALU.subtract)
                    last.then_inc(y_low, 1)

                def g_part(b, u, pair):
                    slot = (PAIRS * u + pair) % 2
                    dve.wait_ge(g_high, PAIRS * b + pair + 1)
                    nc.vector.tensor_tensor(g_sb[:, slot, PART_LOW], ps_g[:, slot, :].rearrange("p (c t) -> p c t", c=2),
                                            high(g_sb[:, slot, PART_HIGH]), ALU.subtract).then_inc(g_copied, 1)

                def copy_h(b, u):
                    dve.wait_ge(proj_done, PAIRS * (b + 1) + 2)
                    dve.wait_ge(h_free, b + 1)
                    for s in range(SUBS):
                        nc.vector.bn_stats(stats[:, bass.ds(b * SUBS + s, 1), :].squeeze(1), ps_h[:, s, :])
                    nc.vector.tensor_copy(h_out[:, u], ps_h[:]).then_inc(h_copied, 1)

                def run_block(b, u, ahead):
                    for step in range(CHUNKS + 1):
                        if step + 1 < CHUNKS:
                            y_part(b, step + 1)
                        elif step + 1 == CHUNKS and ahead:
                            y_part(b + 1, 0)
                        if ahead and step < 2 * GROUPS:
                            (front.copy_y if step % 2 else front.x_low_part)(dve, b + 1, step // 2)
                        if step >= 2 and step % 2 == 0:
                            g_part(b, u, step // 2 - 1)
                    copy_h(b, u)

                y_part(0, 0)
                with dve.Fori(0, BLOCKS - 2, 2) as b:
                    run_block(b, 0, True)
                    run_block(b + 1, 1, True)
                run_block(BLOCKS - 2, 0, True)
                run_block(BLOCKS - 1, 1, False)


class Chain:

    def __init__(self, eng, sem, base):
        self.eng, self.sem, self.base, self.n = eng, sem, base, 0

    def __call__(self, ins):
        self.n += 1
        ins.then_inc(self.sem, 1)
        self.eng.wait_ge(self.sem, self.base + self.n)


AB = 512
TILES = AB // P
ABLOCKS = TOK // AB
NTILES = TOK // P
IN_TILE = P // PATCH


def attention_block(nc, h_dram, W_in, b_in, Wq, Wk, Wv, W_out, b_out, ident, h, stats, out_rows):
    QV = 2 * SLICE + 2 * DH
    with ExitStack() as ctx:
        def sb(name, shape, dt=F32):
            return ctx.enter_context(nc.sbuf_tensor(name, shape, dt))

        def psum(name, shape):
            return ctx.enter_context(nc.psum_tensor(name, shape, F32))

        def sem(name):
            return ctx.enter_context(nc.semaphore(name))

        w_in = sb("w_in", [P, PARTS, KD, D], F32R)
        w_out = sb("w_out", [P, PARTS, KD, D], F32R)
        wk_pair = sb("wk_pair", [P, 2 * SLICE])
        wqv_pair = sb("wqv_pair", [P, QV])
        b_in_row = sb("b_in_row", [KD, P])
        b_in_col = sb("b_in_col", [P, KD])
        b_out_all = sb("b_out_all", [P, D])
        same_batch = sb("same_batch", [P, 4, P])
        mean_var = sb("mean_var", [P, NTILES, 2])
        rstd = sb("rstd", [P, NTILES])
        hn = sb("hn", [P, TILES, D])
        hnT = sb("hnT", [P, PARTS, KD, AB], F32R)
        xmT = sb("xmT", [P, KD, AB])
        k_exp = sb("k_exp", [P, 2, QUADS, AB])
        k_max = sb("k_max", [P, QUADS, AB // PATCH])
        k_inv = sb("k_inv", [P, 2, QUADS, AB // PATCH])
        qv = sb("qv", [P, 2, TILES, KD, QV])
        q_prob = sb("q_prob", [P, TILES, HEADS, SLICE])
        q_red = sb("q_red", [P, TILES, HEADS])
        qT_wide = sb("qT_wide", [P, 2, QUADS, 4, P])
        scores = sb("scores", [P, 2, QUADS, 4, P])
        oT = sb("oT", [P, 2, PARTS, KD, P], F32R)

        ps_turn = psum("ps_turn", [P, 2, BANK])
        ps_proj = psum("ps_proj", [P, 2, BANK])
        ps_score = psum("ps_score", [P, QUADS, BANK])
        ps_oT = psum("ps_oT", [P, KD, P])
        ps_out = psum("ps_out", [P, D])

        h_loaded = [sem(f"h_loaded{i}") for i in range(3)]
        w_in_loaded = sem("w_in_loaded")
        w_in_high = sem("w_in_high")
        w_in_low = sem("w_in_low")
        hnT_high = sem("hnT_high")
        w_out_loaded = sem("w_out_loaded")
        w_out_high = sem("w_out_high")
        w_out_low = sem("w_out_low")
        oT_high = sem("oT_high")
        h_stored = sem("h_stored2")
        w_loaded = sem("w_loaded")
        cleared = sem("cleared")
        pair_loaded = sem("pair_loaded")
        masked_ones = sem("masked_ones")
        eps_ready = sem("eps_ready")
        stats_done = sem("stats_done")
        std_done = sem("std_done")
        setup = sem("setup")
        bias_turned = sem("bias_turned")
        bias_ready = sem("bias_ready")
        qT_cleared = sem("qT_cleared")
        normed = sem("normed")
        bias_added = sem("bias_added")
        turned = sem("turned")
        turn_copied = sem("turn_copied")
        proj_filled = sem("proj_filled")
        proj_copied = sem("proj_copied")
        k_centred = sem("k_centred")
        k_exped = sem("k_exped")
        k_ready = sem("k_ready")
        q_centred = sem("q_centred")
        q_exped = sem("q_exped")
        q_ready = sem("q_ready")
        soft = sem("soft")
        score_filled = sem("score_filled")
        score_masked = sem("score_masked")
        oT_filled = sem("oT_filled")
        oT_copied = sem("oT_copied")
        out_filled = sem("out_filled")
        out_added = sem("out_added")

        w_raw = qv[:, 1].rearrange("p t k c -> p (t k c)")[:, 0:KD * D].rearrange("p (k n) -> p k n", k=KD)

        w_out_raw = scores[:].rearrange("p u q h t -> p (u q h t)").rearrange("p (k n) -> p k n", k=KD)

        A_TURNS, B_TURNS = 6, 4
        TURNS = A_TURNS + B_TURNS
        PROJ = 3 * KD

        def turns_a(b):
            return TURNS * b - B_TURNS

        def turns_b(b):
            return TURNS * b + 2 * A_TURNS

        def turns_b_last(b):
            return TURNS * b + A_TURNS

        TURN_STEPS = {TILES: (0,), TILES + 1: (1, 2), TILES + 2: (3,)}

        with nc.Block() as block:
            @block.sync
            def _(sp):
                sp.dma_start(b_in_row[:], b_in.rearrange("(k p) -> k p", p=P)).then_inc(w_loaded, 16)
                sp.dma_start(b_out_all[:], b_out.partition_broadcast(P)).then_inc(w_loaded, 16)
                for b in range(ABLOCKS):
                    if b == 1:
                        sp.wait_ge(pair_loaded, 96)
                    sp.dma_start(h[:, b * TILES:(b + 1) * TILES, :],
                                 h_dram[b * AB:(b + 1) * AB, :].rearrange("(t p) n -> p t n", p=P)
                                 ).then_inc(h_loaded[min(b, 2)], 16)
                    if b == 0:
                        sp.dma_start(w_raw, W_in.rearrange("(k p) n -> p k n", p=P)).then_inc(w_in_loaded, 16)
                        sp.dma_start(w_out_raw, W_out.rearrange("(k p) n -> p k n", p=P)).then_inc(w_out_loaded, 16)
                out_blocks = out_rows.rearrange("(b t p) n -> b p t n", p=P, t=TILES)
                with sp.Fori(0, ABLOCKS) as b:
                    sp.wait_ge(out_added, TILES * b + TILES + 1)
                    sp.dma_start(out_blocks[b], h[:, bass.ds(b * TILES, TILES), :]).then_inc(h_stored, 16)
                sp.wait_ge(h_stored, 16 * ABLOCKS)

            @block.gpsimd
            def _(pool):
                nc.gpsimd.memset(wk_pair[:], 0.0).then_inc(cleared, 1)
                nc.gpsimd.memset(wqv_pair[:], 0.0).then_inc(cleared, 1)
                pool.wait_ge(cleared, 2)
                for i in range(2):
                    rows = slice(i * DH, (i + 1) * DH)
                    pool.dma_start(wk_pair[rows, i * SLICE:(i + 1) * SLICE], Wk).then_inc(pair_loaded, 16)
                    pool.dma_start(wqv_pair[rows, i * SLICE:(i + 1) * SLICE], Wq).then_inc(pair_loaded, 16)
                    pool.dma_start(wqv_pair[rows, 2 * SLICE + i * DH:2 * SLICE + (i + 1) * DH], Wv
                                   ).then_inc(pair_loaded, 16)
                nc.gpsimd.memset(same_batch[:], 1.0).then_inc(masked_ones, 1)
                for n, (step, base, mul) in enumerate(((-PATCH, 0, 1), (PATCH, PATCH - 1, -1))):
                    pool.wait_ge(masked_ones, n + 1)
                    v = same_batch[:].rearrange("p h (b s) -> p h b s", s=PATCH)
                    nc.gpsimd.affine_select(out=v, in_=v, compare_op=ALU.is_ge, fill=0.0, base=base,
                                            pattern=[[0, 4], [step, IN_TILE], [0, PATCH]],
                                            channel_multiplier=mul).then_inc(masked_ones, 1)
                pool.wait_ge(w_loaded, 32)
                with pool.Fori(0, ABLOCKS) as b:
                    pool.wait_ge(normed, b + 1)
                    rows = h[:, bass.ds(b * TILES, TILES), :]
                    nc.gpsimd.tensor_tensor(rows, rows, b_out_all[:].unsqueeze(1).broadcast_to([P, TILES, D]),
                                            ALU.add).then_inc(bias_added, 1)

            @block.tensor
            def _(pe):
                pe.sem_inc(oT_filled, 2)
                pe.sem_inc(out_filled, 2)
                pe.wait_ge(w_loaded, 32)
                nc.tensor.transpose(ps_out[:, 0:KD], b_in_row[:], ident[0:KD, 0:KD]).then_inc(bias_turned, 1)
                pe.wait_ge(bias_ready, 1)

                def turn_q(b, turns, t):
                    if t == 0:
                        pe.wait_ge(q_ready, b + 1)
                    pe.wait_ge(turn_copied, turns + t - 1)
                    for quad in range(QUADS):
                        last = nc.tensor.transpose(
                            ps_turn[:, t % 2, quad * P:(quad + 1) * P],
                            q_prob[:, t, 4 * quad:4 * quad + 4, :].rearrange("p h s -> p (h s)"), ident[:])
                    last.then_inc(turned, 1)

                def turn_rows(b, turns, t, first=False):
                    if t == 0:
                        pe.wait_ge(normed, b + 1)
                    if not (first and t < 2):
                        pe.wait_ge(turn_copied, turns + t - 1)
                    for k in range(KD):
                        last = nc.tensor.transpose(ps_turn[:, t % 2, k * P:(k + 1) * P],
                                                   hn[:, t, k * P:(k + 1) * P], ident[:])
                    last.then_inc(turned, 1)

                def stage_a(b, turns, first=False):
                    pe.wait_ge(turn_copied, turns + TILES)
                    if first:
                        pe.wait_ge(w_in_low, 1)
                    terms = [(k, a, v) for k in range(KD) for a, v in PRODUCTS]
                    for i in range(KD):
                        if not (first and i < 2):
                            pe.wait_ge(proj_copied, PROJ * b + i - 1)
                        for n, (k, a, v) in enumerate(terms):
                            last = nc.tensor.matmul(ps_proj[:, i % 2, :], w_in[:, a, k, i * P:(i + 1) * P],
                                                    hnT[:, v, k, :], start=(n == 0), stop=(n == len(terms) - 1))
                        last.then_inc(proj_filled, 1)
                    pe.wait_ge(proj_copied, PROJ * b + KD)
                    if first:
                        pe.wait_ge(pair_loaded, 96)
                    for quad in range(QUADS):
                        for i in range(2):
                            last = nc.tensor.matmul(ps_turn[i * DH:(i + 1) * DH, quad, :], wk_pair[:],
                                                    xmT[:, 2 * quad + i, :], start=True, stop=True)
                        last.then_inc(turned, 1)
                    for t in range(TILES):
                        for half in range(2):
                            n = KD + 2 * t + half
                            pe.wait_ge(proj_copied, PROJ * b + n - 1)
                            for i in range(2):
                                last = nc.tensor.matmul(ps_proj[:, n % 2, i * QV:(i + 1) * QV],
                                                        xmT[:, 2 * half + i, t * P:(t + 1) * P], wqv_pair[:],
                                                        start=True, stop=True)
                            last.then_inc(proj_filled, 1)
                        if not first and t < 2:
                            turn_q(b - 1, turns + A_TURNS, t)

                def stage_b(b, u, turns, last_block=False, ahead=False):
                    def score(t):
                        if t == 0:
                            pe.wait_ge(k_ready, b + 1)
                        pe.wait_ge(turn_copied, turns + t + 1)
                        for quad in range(QUADS):
                            n = 2 * TILES * b + 2 * t + quad
                            pe.wait_ge(score_masked, n + 1)
                            nc.tensor.matmul(ps_score[:, quad, :], k_exp[:, u, quad, t * P:(t + 1) * P],
                                             qT_wide[:, t % 2, quad].rearrange("p h t -> p (h t)"),
                                             start=True, stop=True).then_inc(score_filled, 1)

                    def mix(t):
                        pe.wait_ge(score_masked, 2 * TILES * b + 2 * t + 4)
                        pe.wait_ge(oT_copied, TILES * b + t + 1)
                        for head in range(HEADS):
                            i, r = head // 2, head % 2
                            last = nc.tensor.matmul(
                                ps_oT[r * DH:(r + 1) * DH, i, :],
                                qv[:, u, t, i, 2 * SLICE + r * DH:2 * SLICE + (r + 1) * DH],
                                scores[:, t % 2, head // 4, head % 4, :], start=True, stop=True)
                        last.then_inc(oT_filled, 1)

                    def out(t):
                        pe.wait_ge(oT_copied, TILES * b + t + 2)
                        pe.wait_ge(out_added, TILES * b + t + 1)
                        terms = [(i, a, v) for i in range(KD) for a, v in PRODUCTS]
                        for n, (i, a, v) in enumerate(terms):
                            last = nc.tensor.matmul(ps_out[:], oT[:, t % 2, a, i, :], w_out[:, v, i, :],
                                                    start=(n == 0), stop=(n == len(terms) - 1))
                        last.then_inc(out_filled, 1)

                    for step in range(TILES + 3):
                        if step < TILES and (last_block or step >= 2):
                            turn_q(b, turns, step)
                        if 1 <= step <= TILES:
                            score(step - 1)
                        if 2 <= step <= TILES + 1:
                            mix(step - 2)
                        if ahead:
                            for t in TURN_STEPS.get(step, ()):
                                turn_rows(b + 2, turns_a(b + 2), t)
                        if step >= 3:
                            out(step - 3)

                for t in range(TILES):
                    turn_rows(0, 0, t, first=True)
                stage_a(0, 0, first=True)
                for t in range(TILES):
                    turn_rows(1, turns_a(1), t)
                pe.wait_ge(w_out_low, 1)
                with pe.Fori(0, ABLOCKS // 2 - 1) as pair:
                    b = 2 * pair
                    for u in range(2):
                        stage_a(b + u + 1, turns_a(b + u + 1))
                        stage_b(b + u, u, turns_b(b + u), ahead=True)
                stage_a(ABLOCKS - 1, turns_a(ABLOCKS - 1))
                stage_b(ABLOCKS - 2, 0, turns_b(ABLOCKS - 2))
                stage_b(ABLOCKS - 1, 1, turns_b_last(ABLOCKS - 1), last_block=True)

            @block.scalar
            def _(act):
                act.sem_inc(oT_copied, 1)
                act.wait_ge(stats_done, 1)
                nc.scalar.activation(rstd[:], rstd[:], ACT.Sqrt).then_inc(std_done, 1)
                act.wait_ge(w_in_loaded, 16)
                nc.scalar.copy(w_in[:, PART_HIGH], w_raw).then_inc(w_in_high, 1)

                def turned_high(b, turns, t):
                    act.wait_ge(turned, turns + t + 1)
                    nc.scalar.copy(hnT[:, PART_HIGH, :, t * P:(t + 1) * P],
                                   ps_turn[:, t % 2, :].rearrange("p (k t) -> p k t", k=KD)).then_inc(hnT_high, 1)

                def x_mid(b):
                    for i in range(KD):
                        act.wait_ge(proj_filled, PROJ * b + i + 1)
                        nc.scalar.activation(xmT[:, i, :], ps_proj[:, i % 2, :], ACT.Identity,
                                             bias=b_in_col[:, i:i + 1]).then_inc(proj_copied, 1)

                def exp_q(b):
                    act.wait_ge(q_centred, b + 1)
                    nc.scalar.activation(q_prob[:], q_prob[:], ACT.Exp).then_inc(q_exped, 1)

                def exp_k_copy_qv(b, u):
                    for quad in range(QUADS):
                        act.wait_ge(k_centred, 2 * b + quad + 1)
                        nc.scalar.activation(k_exp[:, u, quad, :], k_exp[:, u, quad, :], ACT.Exp
                                             ).then_inc(k_exped, 1)
                    for t in range(TILES):
                        for half in range(2):
                            n = KD + 2 * t + half
                            act.wait_ge(proj_filled, PROJ * b + n + 1)
                            nc.scalar.copy(qv[:, u, t, 2 * half:2 * half + 2, :],
                                           ps_proj[:, n % 2, 0:2 * QV].rearrange("p (i c) -> p i c", i=2)
                                           ).then_inc(proj_copied, 1)

                def stage_b(b, ahead=False):
                    for step in range(2, TILES + 3):
                        if step < TILES + 2:
                            n, slot = TILES * b + step - 2, step % 2
                            act.wait_ge(oT_filled, n + 3)
                            act.wait_ge(out_filled, n + 1)
                            nc.scalar.copy(oT[:, slot, PART_HIGH], ps_oT[:]).then_inc(oT_high, 1)
                        if ahead:
                            for t in TURN_STEPS.get(step, ()):
                                turned_high(b + 2, turns_a(b + 2), t)

                for t in range(TILES):
                    turned_high(0, 0, t)
                act.wait_ge(w_out_loaded, 16)
                nc.scalar.copy(w_out[:, PART_HIGH], w_out_raw).then_inc(w_out_high, 1)
                act.wait_ge(bias_ready, 1)
                x_mid(0)
                exp_k_copy_qv(0, 0)
                for t in range(TILES):
                    turned_high(1, turns_a(1), t)
                with act.Fori(0, ABLOCKS // 2 - 1) as pair:
                    b = 2 * pair
                    for u in range(2):
                        exp_q(b + u)
                        x_mid(b + u + 1)
                        exp_k_copy_qv(b + u + 1, 1 - u)
                        stage_b(b + u, ahead=True)
                exp_q(ABLOCKS - 2)
                x_mid(ABLOCKS - 1)
                exp_k_copy_qv(ABLOCKS - 1, 1)
                stage_b(ABLOCKS - 2)
                exp_q(ABLOCKS - 1)
                stage_b(ABLOCKS - 1)

            @block.vector
            def _(dve):
                dve.sem_inc(score_masked, 2)
                dve.sem_inc(out_added, 1)
                for t in range(NTILES):
                    last = nc.vector.bn_aggr(mean_var[:, t, :], stats[:, t, :])
                last.then_inc(setup, 1)
                dve.wait_ge(setup, 1)
                nc.vector.tensor_scalar(rstd[:], mean_var[:, :, 1], EPS, None, ALU.add).then_inc(stats_done, 1)
                nc.vector.memset(qT_wide[:], 0.0).then_inc(qT_cleared, 1)
                dve.wait_ge(std_done, 1)
                nc.vector.reciprocal(rstd[:], rstd[:]).then_inc(setup, 1)
                dve.wait_ge(setup, 2)
                dve.wait_ge(qT_cleared, 1)

                def layernorm(b):
                    for t in range(TILES):
                        n = b * TILES + t
                        last = nc.vector.tensor_scalar(hn[:, t, :], h[:, bass.ds(n, 1), :].squeeze(1),
                                                       mean_var[:, bass.ds(n, 1), 0], rstd[:, bass.ds(n, 1)],
                                                       ALU.subtract, ALU.mult)
                    last.then_inc(normed, 1)

                def split_hnT(b, t):
                    dve.wait_ge(hnT_high, TILES * b + t + 1)
                    cols = slice(t * P, (t + 1) * P)
                    nc.vector.tensor_tensor(hnT[:, PART_LOW, :, cols],
                                            ps_turn[:, t % 2, :].rearrange("p (k t) -> p k t", k=KD),
                                            high(hnT[:, PART_HIGH, :, cols]), ALU.subtract
                                            ).then_inc(turn_copied, 1)

                def centre_q(b, u, chain):
                    q = qv[:, u, :, :, 0:2 * SLICE].rearrange("p t i (h s) -> p (t i) h s", s=SLICE)
                    dve.wait_ge(proj_copied, PROJ * b + PROJ)
                    red = q_red[:].rearrange("p t (i h) -> p (t i) h", h=2)
                    chain(nc.vector.tensor_reduce(red, q, AX.X, ALU.max))
                    nc.vector.tensor_tensor(q_prob[:].rearrange("p t (i h) s -> p (t i) h s", h=2), q,
                                            red.unsqueeze(3).broadcast_to([P, TILES * KD, 2, SLICE]), ALU.subtract
                                            ).then_inc(q_centred, 1)

                def centre_k(b, u, turns, chain):
                    for quad in range(QUADS):
                        dve.wait_ge(turned, turns + TILES + quad + 1)
                        k = ps_turn[:, quad, :].rearrange("p (b s) -> p b s", s=PATCH)
                        chain(nc.vector.tensor_reduce(k_max[:, quad, :], k, AX.X, ALU.max))
                        nc.vector.tensor_tensor(k_exp[:, u, quad, :].rearrange("p (b s) -> p b s", s=PATCH), k,
                                                k_max[:, quad, :].unsqueeze(2).broadcast_to([P, AB // PATCH, PATCH]),
                                                ALU.subtract).then_inc(k_centred, 1)
                        dve.wait_ge(k_centred, 2 * b + quad + 1)
                        dve.sem_inc(turn_copied, 1)

                def norm_q(b, chain):
                    dve.wait_ge(q_exped, b + 1)
                    q = q_prob[:].rearrange("p t h s -> p (t h) s")
                    red = q_red[:].rearrange("p t h -> p (t h)")
                    chain(nc.vector.tensor_reduce(red, q, AX.X, ALU.add))
                    chain(nc.vector.reciprocal(red, red))
                    nc.vector.tensor_tensor(q, q, red.unsqueeze(2).broadcast_to([P, TILES * HEADS, SLICE]), ALU.mult
                                            ).then_inc(q_ready, 1)

                def norm_k(b, u, chain):
                    dve.wait_ge(k_exped, 2 * b + 2)
                    k = k_exp[:, u].rearrange("p q (b s) -> p (q b) s", s=PATCH)
                    inv = k_inv[:, u].rearrange("p q b -> p (q b)")
                    chain(nc.vector.tensor_reduce(inv, k, AX.X, ALU.add))
                    nc.vector.reciprocal(inv, inv).then_inc(k_ready, 1)

                def stage_b(b, u, turns, ahead=False):
                    def spread_q(t):
                        dve.wait_ge(turned, turns + t + 1)
                        for quad in range(QUADS):
                            for r in range(4):
                                rows = slice(32 * r, 32 * r + 32)
                                inv = k_inv[rows, u, quad, t * IN_TILE:(t + 1) * IN_TILE]
                                last = nc.vector.tensor_tensor(
                                    qT_wide[rows, t % 2, quad, r, :].rearrange("p (b s) -> p b s", s=PATCH),
                                    ps_turn[rows, t % 2, quad * P:(quad + 1) * P].rearrange("p (b s) -> p b s", s=PATCH),
                                    inv.unsqueeze(2).broadcast_to([32, IN_TILE, PATCH]), ALU.mult)
                        last.then_inc(turn_copied, 1)

                    def mask(t):
                        dve.wait_ge(oT_filled, TILES * b + t + 1)
                        for quad in range(QUADS):
                            dve.wait_ge(score_filled, 2 * TILES * b + 2 * t + quad + 1)
                            nc.vector.tensor_tensor(scores[:, t % 2, quad],
                                                    ps_score[:, quad, :].rearrange("p (h t) -> p h t", h=4),
                                                    same_batch[:], ALU.mult).then_inc(score_masked, 1)

                    def split_oT(t):
                        dve.wait_ge(oT_high, TILES * b + t + 1)
                        nc.vector.tensor_tensor(oT[:, t % 2, PART_LOW], ps_oT[:], high(oT[:, t % 2, PART_HIGH]),
                                                ALU.subtract).then_inc(oT_copied, 1)

                    def add_out(t):
                        n = TILES * b + t
                        if t == 0:
                            dve.wait_ge(bias_added, b + 1)
                        dve.wait_ge(out_filled, n + 3)
                        rows = h[:, bass.ds(n, 1), :].squeeze(1)
                        nc.vector.tensor_tensor(rows, ps_out[:], rows, ALU.add).then_inc(out_added, 1)
                        dve.wait_ge(out_added, n + 2)
                        nc.vector.bn_stats(stats[:, bass.ds(n, 1), :].squeeze(1), rows).then_inc(setup, 1)

                    dve.wait_ge(k_ready, b + 1)
                    for step in range(TILES + 3):
                        if step < TILES:
                            spread_q(step)
                        if 1 <= step <= TILES:
                            mask(step - 1)
                        if 2 <= step <= TILES + 1:
                            split_oT(step - 2)
                        if ahead:
                            for t in TURN_STEPS.get(step, ()):
                                split_hnT(b + 2, t)
                        if step >= 3:
                            add_out(step - 3)

                CHAIN = 6
                dve.wait_ge(h_loaded[0], 16)
                layernorm(0)
                dve.wait_ge(bias_turned, 1)
                nc.vector.tensor_copy(b_in_col[:], ps_out[:, 0:KD]).then_inc(bias_ready, 1)
                dve.wait_ge(w_in_high, 1)
                nc.vector.tensor_tensor(w_in[:, PART_LOW], w_raw, high(w_in[:, PART_HIGH]), ALU.subtract
                                        ).then_inc(w_in_low, 1)
                for t in range(TILES):
                    split_hnT(0, t)
                dve.wait_ge(h_loaded[1], 16)
                layernorm(1)
                dve.wait_ge(w_out_high, 1)
                nc.vector.tensor_tensor(w_out[:, PART_LOW], w_out_raw, high(w_out[:, PART_HIGH]), ALU.subtract
                                        ).then_inc(w_out_low, 1)
                chain = Chain(dve, soft, 0)
                centre_k(0, 0, 0, chain)
                norm_k(0, 0, chain)
                for t in range(TILES):
                    split_hnT(1, t)
                START = chain.n
                dve.wait_ge(w_out_low, 1)
                dve.wait_ge(masked_ones, 3)
                dve.wait_ge(h_loaded[2], 16 * (ABLOCKS - 2))

                def both(b, u, ahead):
                    chain = Chain(dve, soft, CHAIN * b + START)
                    centre_q(b, u, chain)
                    norm_q(b, chain)
                    if ahead:
                        layernorm(b + 2)
                    centre_k(b + 1, 1 - u, turns_a(b + 1), chain)
                    norm_k(b + 1, 1 - u, chain)
                    stage_b(b, u, turns_b(b), ahead)
                    assert chain.n == CHAIN

                with dve.Fori(0, ABLOCKS // 2 - 1) as pair:
                    b = 2 * pair
                    both(b, 0, True)
                    both(b + 1, 1, True)
                both(ABLOCKS - 2, 0, False)
                chain = Chain(dve, soft, CHAIN * (ABLOCKS - 1) + START)
                centre_q(ABLOCKS - 1, 1, chain)
                norm_q(ABLOCKS - 1, chain)
                stage_b(ABLOCKS - 1, 1, turns_b_last(ABLOCKS - 1))


def routing_block(nc, gate_w, ident, h, stats, row_dram, affinity):
    with ExitStack() as ctx:
        def sb(name, shape, dt=F32):
            return ctx.enter_context(nc.sbuf_tensor(name, shape, dt))

        def psum(name, shape):
            return ctx.enter_context(nc.psum_tensor(name, shape, F32))

        def sem(name):
            return ctx.enter_context(nc.semaphore(name))

        gate = sb("gate", [P, KD, EXPERTS])
        mean_var = sb("mean_var2", [P, NTILES, 2])
        rstd = sb("rstd2", [P, NTILES])
        hn = sb("hn2", [P, 2, TILES, D])
        hnT = sb("hnT2", [P, 2, KD, AB])
        logitT = sb("logitT", [EXPERTS, TOK])
        red = sb("aff_red", [P, HALVES * PATCH])
        ps_turn = psum("ps_turn2", [P, 2, KD, P])
        ps_logit = psum("ps_logit", [EXPERTS, 2, BANK])
        ps_aff = psum("ps_aff", [P, HALVES, PATCH, EXPERTS])

        gate_loaded = sem("gate_loaded")
        setup = sem("setup2")
        var_ready = sem("var_ready")
        std_done = sem("std_done2")
        normed = sem("normed2")
        row_stored = sem("row_stored")
        row_free = sem("row_free")
        turned = sem("turned2")
        turn_copied = sem("turn_copied2")
        logit_done = sem("logit_done")
        logit_copied = sem("logit_copied")
        logit_turned = sem("logit_turned")
        centred = sem("centred2")
        exped = sem("exped2")

        with nc.Block() as block:
            @block.sync
            def _(sp):
                sp.dma_start(gate[:], gate_w.rearrange("(k p) e -> p k e", p=P)).then_inc(gate_loaded, 16)
                rows = row_dram.rearrange("(b t p) n -> b p t n", p=P, t=TILES)

                def store_rows(b, u):
                    sp.wait_ge(normed, b + 1)
                    sp.dma_start(rows[b], hn[:, u]).then_inc(row_stored, 16)
                    sp.wait_ge(row_stored, 16 * b + 16)
                    sp.sem_inc(row_free, 1)

                with sp.Fori(0, ABLOCKS // 2) as pair:
                    for u in range(2):
                        store_rows(2 * pair + u, u)

            @block.tensor
            def _(pe):
                pe.wait_ge(gate_loaded, 16)

                def turn(b, u, t):
                    if t == 0:
                        pe.wait_ge(normed, b + 1)
                    pe.wait_ge(turn_copied, TILES * b + t + 1)
                    for k in range(KD):
                        last = nc.tensor.transpose(ps_turn[:, t % 2, k, :], hn[:, u, t, k * P:(k + 1) * P], ident[:])
                    last.then_inc(turned, 1)

                def logits(b, u):
                    pe.wait_ge(turn_copied, TILES * b + TILES + 2)
                    pe.wait_ge(logit_copied, b + 1)
                    for k in range(KD):
                        last = nc.tensor.matmul(ps_logit[:, u, :], gate[:, k, :], hnT[:, u, k, :],
                                                start=(k == 0), stop=(k == KD - 1))
                    last.then_inc(logit_done, 1)

                def turn_block(b, u):
                    for t in range(TILES):
                        turn(b, u, t)

                turn_block(0, 0)
                with pe.Fori(0, ABLOCKS // 2 - 1) as pair:
                    turn_block(2 * pair + 1, 1)
                    logits(2 * pair, 0)
                    turn_block(2 * pair + 2, 0)
                    logits(2 * pair + 1, 1)
                turn_block(ABLOCKS - 1, 1)
                logits(ABLOCKS - 2, 0)
                logits(ABLOCKS - 1, 1)
                pe.wait_ge(logit_copied, ABLOCKS + 2)
                by_token = logitT[:].rearrange("e (c p s) -> e c s p", p=P, s=PATCH)
                for c in range(HALVES):
                    for s in range(PATCH):
                        last = nc.tensor.transpose(ps_aff[:, c, s, :], by_token[:, c, s, :],
                                                   ident[0:EXPERTS, 0:EXPERTS])
                last.then_inc(logit_turned, 1)

            @block.scalar
            def _(act):
                act.sem_inc(turn_copied, 2)
                act.wait_ge(var_ready, 1)
                nc.scalar.activation(rstd[:], rstd[:], ACT.Sqrt).then_inc(std_done, 1)
                with act.Fori(0, ABLOCKS // 2) as pair:
                    for u in range(2):
                        for t in range(TILES):
                            act.wait_ge(turned, TILES * (2 * pair + u) + t + 1)
                            nc.scalar.copy(hnT[:, u, :, t * P:(t + 1) * P], ps_turn[:, t % 2]).then_inc(turn_copied, 1)
                act.wait_ge(centred, 1)
                nc.scalar.activation(affinity[:], affinity[:], ACT.Exp).then_inc(exped, 1)

            @block.vector
            def _(dve):
                dve.sem_inc(logit_copied, 2)
                dve.sem_inc(row_free, 2)
                for t in range(NTILES):
                    last = nc.vector.bn_aggr(mean_var[:, t, :], stats[:, t, :])
                last.then_inc(setup, 1)
                dve.wait_ge(setup, 1)
                nc.vector.tensor_scalar(rstd[:], mean_var[:, :, 1], EPS, None, ALU.add).then_inc(var_ready, 1)
                dve.wait_ge(std_done, 1)
                nc.vector.reciprocal(rstd[:], rstd[:]).then_inc(setup, 1)
                dve.wait_ge(setup, 2)

                def layernorm(b, u, first=False):
                    if not first:
                        dve.wait_ge(turned, TILES * (b - 1))
                    dve.wait_ge(row_free, b + 1)
                    for t in range(TILES):
                        n = b * TILES + t
                        last = nc.vector.tensor_scalar(hn[:, u, t, :], h[:, bass.ds(n, 1), :].squeeze(1),
                                                       mean_var[:, bass.ds(n, 1), 0], rstd[:, bass.ds(n, 1)],
                                                       ALU.subtract, ALU.mult)
                    last.then_inc(normed, 1)

                def copy_logits(b, u):
                    dve.wait_ge(logit_done, b + 1)
                    nc.vector.tensor_copy(logitT[:, bass.ds(b * AB, AB)], ps_logit[:, u, :]).then_inc(logit_copied, 1)

                layernorm(0, 0, first=True)
                layernorm(1, 1, first=True)
                with dve.Fori(0, ABLOCKS // 2 - 1) as pair:
                    for u in range(2):
                        layernorm(2 * pair + u + 2, u)
                        copy_logits(2 * pair + u, u)
                copy_logits(ABLOCKS - 2, 0)
                copy_logits(ABLOCKS - 1, 1)
                dve.wait_ge(logit_turned, 1)
                wide = [P, HALVES * PATCH, EXPERTS]
                aff = affinity[:].rearrange("p c s e -> p (c s) e")
                logits = ps_aff[:].rearrange("p c s e -> p (c s) e")
                chain = Chain(dve, setup, 2)
                chain(nc.vector.tensor_reduce(red[:], logits, AX.X, ALU.max))
                nc.vector.tensor_tensor(aff, logits, red[:].unsqueeze(2).broadcast_to(wide),
                                        ALU.subtract).then_inc(centred, 1)
                dve.wait_ge(exped, 1)
                chain(nc.vector.tensor_reduce(red[:], aff, AX.X, ALU.add))
                chain(nc.vector.reciprocal(red[:], red[:]))
                nc.vector.tensor_tensor(aff, aff, red[:].unsqueeze(2).broadcast_to(wide), ALU.mult)


def choice_block(nc, affinity, row_index, weight):
    with ExitStack() as ctx:
        def sb(name, shape, dt=F32):
            return ctx.enter_context(nc.sbuf_tensor(name, shape, dt))

        def sem(name):
            return ctx.enter_context(nc.semaphore(name))

        wide = [P, HALVES, EXPERTS, PATCH]
        by_expert = sb("by_expert", wide)
        best = sb("best", [P, HALVES, EXPERTS])
        place = sb("place", [P, HALVES, EXPERTS])
        hit = sb("hit", wide)
        countdown = sb("countdown", [P, PATCH])
        row_end = sb("row_end", [P, HALVES])
        row_float = sb("row_float", [P, EXPERTS, TOP, HALVES])
        ramps = sem("ramps")
        picked = sem("picked")

        with nc.Block() as block:
            @block.gpsimd
            def _(pool):
                nc.gpsimd.iota(countdown[:], [[-1, PATCH]], base=PATCH, channel_multiplier=0,
                               allow_small_or_imprecise_dtypes=True).then_inc(ramps, 1)
                nc.gpsimd.iota(row_end[:], [[P * PATCH, HALVES]], base=PATCH, channel_multiplier=PATCH,
                               allow_small_or_imprecise_dtypes=True).then_inc(ramps, 1)

            @block.vector
            def _(dve):
                dve.wait_ge(ramps, 2)
                chain = Chain(dve, picked, 0)
                chain(nc.vector.tensor_copy(by_expert[:], affinity[:].rearrange("p c s e -> p c e s")))
                flat = "p c e s -> p (c e s)"
                for r in range(TOP):
                    chain(nc.vector.tensor_reduce(best[:], by_expert[:], AX.X, ALU.max))
                    chain(nc.vector.tensor_tensor(hit[:], by_expert[:], best[:].unsqueeze(3).broadcast_to(wide),
                                                  ALU.is_equal))
                    ramp = countdown[:].unsqueeze(1).unsqueeze(1).broadcast_to(wide)
                    chain(nc.vector.tensor_tensor(hit[:], hit[:], ramp, ALU.mult))
                    chain(nc.vector.tensor_reduce(place[:], hit[:], AX.X, ALU.max))
                    nc.vector.tensor_copy(weight[:, :, r, :], best[:].rearrange("p c e -> p e c"))
                    chain(nc.vector.tensor_tensor(row_float[:, :, r, :],
                                                  row_end[:].unsqueeze(1).broadcast_to([P, EXPERTS, HALVES]),
                                                  place[:].rearrange("p c e -> p e c"), ALU.subtract))
                    if r < TOP - 1:
                        chain(nc.vector.tensor_tensor(hit[:], ramp, place[:].unsqueeze(3).broadcast_to(wide),
                                                      ALU.is_equal))
                        chain(nc.vector.scalar_tensor_tensor(
                            by_expert[:].rearrange(flat), hit[:].rearrange(flat), -4.0,
                            by_expert[:].rearrange(flat), ALU.mult, ALU.add))
                chain(nc.vector.tensor_copy(row_index[:], row_float[:]))


def expert_block(nc, w1, b1, w2, b2, ident, row_index, weight, row_dram, out_rows):
    with ExitStack() as ctx:
        def sb(name, shape, dt=F32):
            return ctx.enter_context(nc.sbuf_tensor(name, shape, dt))

        def psum(name, shape):
            return ctx.enter_context(nc.psum_tensor(name, shape, F32))

        def sem(name):
            return ctx.enter_context(nc.semaphore(name))

        w1_in = sb("w1_in", [P, KD, D])
        w2_in = sb("w2_in", [P, KD, D])
        w1_sb = sb("w1_sb", [P, 2, PARTS, KD, D], F32R)
        w2_sb = sb("w2_sb", [P, 2, PARTS, KD, D], F32R)
        b2_sb = sb("b2_sb", [P, 2, D])
        b1_rows = sb("b1_rows", [EXPERTS * KD, P])
        b1_col = sb("b1_col", [P, EXPERTS, KD])
        picked = sb("picked", [P, 2, PICKS, D])
        xT = sb("pickedT", [P, 2, PARTS, KD, PICKS * P], F32R)
        hidden = sb("hidden3", [P, KD, PICKS * P])
        hiddenT = sb("hiddenT", [P, PARTS, KD, PICKS * P], F32R)
        result = sb("result", [P, 2, PICKS, D])
        ps_turn = psum("ps_turn3", [P, 2, KD, P])
        ps_hid = psum("ps_hid3", [P, 2, PICKS * P])
        ps_out = psum("ps_out3", [P, 2, D])

        w1_loaded = sem("w1_loaded")
        w2_loaded = sem("w2_loaded")
        b1_loaded = sem("b1_loaded")
        b1_turned = sem("b1_turned")
        b1_ready = sem("b1_ready")
        gathered = [sem(f"gathered{s}") for s in range(2)]
        scattered = sem("scattered")
        w1_high = sem("w1_high")
        w1_low = sem("w1_low")
        w2_high = sem("w2_high")
        w2_low = sem("w2_low")
        x_high = sem("x_high3")
        h_high = sem("h_high")
        h_low = sem("h_low")
        turned = sem("turned3")
        turn_copied = sem("turn_copied3")
        hid_done = sem("hid_done")
        gelu_done = sem("gelu_done3")
        out_done = sem("out_done")
        out_copied = sem("out_copied")
        weighted = sem("weighted")
        result_free = sem("result_free")

        WEIGHTS_UP = ((), (0,), (1,), (2,))
        WEIGHTS_DOWN = ((3, 4), (5,), (6,), (7,))

        with nc.Block() as block:
            @block.sync
            def _(sp):
                sp.dma_start(b1_rows[:], b1.rearrange("e (k p) -> (e k) p", p=P)).then_inc(b1_loaded, 16)
                b2_row = b2.rearrange("(e a) n -> e a n", a=1)

                def load(e, u, first=False):
                    if not first:
                        sp.wait_ge(w1_low, KD * e)
                    sp.dma_start(w1_in[:], w1[e].rearrange("(k p) n -> p k n", p=P)).then_inc(w1_loaded, 16)
                    if not first:
                        sp.wait_ge(w2_low, KD * e)
                    sp.dma_start(w2_in[:], w2[e].rearrange("(k p) n -> p k n", p=P)).then_inc(w2_loaded, 16)
                    if not first:
                        sp.wait_ge(out_copied, PICKS * (e - 1) + 2)
                    sp.dma_start(b2_sb[:, u], b2_row[e].broadcast_to([P, D])).then_inc(w2_loaded, 16)

                load(0, 0, first=True)
                load(1, 1)
                with sp.Fori(1, EXPERTS // 2) as pair:
                    for u in range(2):
                        load(2 * pair + u, u)

            @block.gpsimd
            def _(pool):
                for e in range(-2, EXPERTS):
                    if e + 2 < EXPERTS:
                        if e >= 0:
                            pool.wait_ge(turned, PICKS * (e + 1))
                        for r in range(TOP):
                            for c in range(HALVES):
                                nc.gpsimd.indirect_dma_start(
                                    picked[:, e % 2, HALVES * r + c, :], None, row_dram,
                                    bass.IndirectOffsetOnAxis(ap=row_index[:, e + 2, r, c:c + 1].bitcast(U32), axis=0)
                                ).then_inc(gathered[e % 2], 16)
                    if e >= 1:
                        pool.wait_ge(scattered, 16 * PICKS * e)
                        pool.sem_inc(result_free, 1)
                    if e >= 0:
                        for r in range(TOP):
                            for c in range(HALVES):
                                j = HALVES * r + c
                                pool.wait_ge(weighted, PICKS * e + j + 1)
                                nc.gpsimd.indirect_dma_start(
                                    out_rows,
                                    bass.IndirectOffsetOnAxis(ap=row_index[:, e, r, c:c + 1].bitcast(U32), axis=0),
                                    result[:, e % 2, j, :], None, compute_op=ALU.add).then_inc(scattered, 16)
                pool.wait_ge(scattered, 16 * PICKS * EXPERTS)

            @block.tensor
            def _(pe):
                pe.wait_ge(b1_loaded, 16)
                nc.tensor.transpose(ps_out[:, 0, 0:EXPERTS * KD], b1_rows[:], ident[0:EXPERTS * KD, 0:EXPERTS * KD]
                                    ).then_inc(b1_turned, 1)
                pe.wait_ge(b1_ready, 1)

                terms = [(k, a, v) for k in range(KD) for a, v in PRODUCTS]

                def turn(e, u, j):
                    if j == 0:
                        pe.wait_ge(gathered[u], 8 * PICKS * (e - u) + 16 * PICKS)
                    pe.wait_ge(turn_copied, PICKS * e + j + 1)
                    for k in range(KD):
                        last = nc.tensor.transpose(ps_turn[:, j % 2, k, :], picked[:, u, j, k * P:(k + 1) * P],
                                                   ident[:])
                    last.then_inc(turned, 1)

                def up(e, u, ahead):
                    pe.wait_ge(turn_copied, PICKS * e + PICKS + 2)
                    pe.wait_ge(w1_low, KD * e + KD)
                    for m in range(KD):
                        pe.wait_ge(gelu_done, KD * e + m + 1)
                        for n, (k, a, v) in enumerate(terms):
                            last = nc.tensor.matmul(ps_hid[:, m % 2, :], w1_sb[:, u, a, k, m * P:(m + 1) * P],
                                                    xT[:, u, v, k, :], start=(n == 0), stop=(n == len(terms) - 1))
                        last.then_inc(hid_done, 1)
                        if ahead:
                            turn(e + 1, 1 - u, m)

                def down(e, u):
                    pe.wait_ge(w2_low, KD * e + KD)
                    for j in range(PICKS):
                        pe.wait_ge(out_copied, PICKS * e + j + 1)
                        for n, (k, a, v) in enumerate(terms):
                            if j == 0 and n % len(PRODUCTS) == 0:
                                pe.wait_ge(h_low, KD * e + k + 1)
                            last = nc.tensor.matmul(ps_out[:, j % 2, :], hiddenT[:, a, k, j * P:(j + 1) * P],
                                                    w2_sb[:, u, v, k, :], start=(n == 0), stop=(n == len(terms) - 1))
                        last.then_inc(out_done, 1)

                for j in range(PICKS):
                    turn(0, 0, j)
                with pe.Fori(0, EXPERTS // 2 - 1) as pair:
                    for u in range(2):
                        up(2 * pair + u, u, True)
                        down(2 * pair + u, u)
                up(EXPERTS - 2, 0, True)
                down(EXPERTS - 2, 0)
                up(EXPERTS - 1, 1, False)
                down(EXPERTS - 1, 1)

            @block.scalar
            def _(act):
                act.sem_inc(gelu_done, 2)
                act.wait_ge(b1_ready, 1)

                def split_w(e, u, n):
                    w_in, w_sb, loaded, done, per = ((w1_in, w1_sb, w1_loaded, w1_high, 16),
                                                     (w2_in, w2_sb, w2_loaded, w2_high, 32))[n // KD]
                    if n % KD == 0:
                        act.wait_ge(loaded, per * e + per)
                    nc.scalar.copy(w_sb[:, u, PART_HIGH, n % KD, :], w_in[:, n % KD, :]).then_inc(done, 1)

                def split_x(e, u, j):
                    act.wait_ge(turned, PICKS * e + j + 1)
                    nc.scalar.copy(xT[:, u, PART_HIGH, :, j * P:(j + 1) * P], ps_turn[:, j % 2]).then_inc(x_high, 1)

                def gelu(e, m):
                    act.wait_ge(hid_done, KD * e + m + 1)
                    nc.scalar.activation(hidden[:, m, :], ps_hid[:, m % 2, :], ACT.Gelu_apprx_tanh,
                                         bias=b1_col[:, bass.ds(e, 1), m]).then_inc(gelu_done, 1)
                    act.wait_ge(gelu_done, KD * e + m + 3)
                    nc.scalar.copy(hiddenT[:, PART_HIGH, m, :], hidden[:, m, :]).then_inc(h_high, 1)

                def weigh(e, u, j):
                    act.wait_ge(out_copied, PICKS * e + j + 3)
                    scale = weight[:, bass.ds(e, 1)].rearrange("p e r c -> p (e r c)")[:, j:j + 1]
                    nc.scalar.activation(result[:, u, j, :], result[:, u, j, :], ACT.Copy, scale=scale
                                         ).then_inc(weighted, 1)

                def run(e, u, ahead):
                    for m in range(KD):
                        gelu(e, m)
                        if ahead:
                            split_x(e + 1, 1 - u, m)
                            for n in WEIGHTS_UP[m]:
                                split_w(e + 1, 1 - u, n)
                    for j in range(PICKS):
                        if ahead:
                            for n in WEIGHTS_DOWN[j]:
                                split_w(e + 1, 1 - u, n)
                        weigh(e, u, j)

                for n in range(2 * KD):
                    split_w(0, 0, n)
                for j in range(PICKS):
                    split_x(0, 0, j)
                with act.Fori(0, EXPERTS // 2 - 1) as pair:
                    for u in range(2):
                        run(2 * pair + u, u, True)
                run(EXPERTS - 2, 0, True)
                run(EXPERTS - 1, 1, False)

            @block.vector
            def _(dve):
                dve.sem_inc(turn_copied, 2)
                dve.sem_inc(out_copied, 2)
                dve.sem_inc(result_free, 2)
                dve.wait_ge(b1_turned, 1)
                nc.vector.tensor_copy(b1_col[:].rearrange("p e k -> p (e k)"), ps_out[:, 0, 0:EXPERTS * KD]
                                      ).then_inc(b1_ready, 1)

                def split_w(e, u, n):
                    w_in, w_sb, high_done, done = ((w1_in, w1_sb, w1_high, w1_low),
                                                   (w2_in, w2_sb, w2_high, w2_low))[n // KD]
                    k = n % KD
                    dve.wait_ge(high_done, KD * e + k + 1)
                    nc.vector.tensor_tensor(w_sb[:, u, PART_LOW, k, :], w_in[:, k, :],
                                            high(w_sb[:, u, PART_HIGH, k, :]), ALU.subtract).then_inc(done, 1)

                def split_h(e, m):
                    dve.wait_ge(h_high, KD * e + m + 1)
                    nc.vector.tensor_tensor(hiddenT[:, PART_LOW, m, :], hidden[:, m, :],
                                            high(hiddenT[:, PART_HIGH, m, :]), ALU.subtract).then_inc(h_low, 1)

                def split_x(e, u, j):
                    dve.wait_ge(x_high, PICKS * e + j + 1)
                    cols = slice(j * P, (j + 1) * P)
                    nc.vector.tensor_tensor(xT[:, u, PART_LOW, :, cols], ps_turn[:, j % 2],
                                            high(xT[:, u, PART_HIGH, :, cols]), ALU.subtract
                                            ).then_inc(turn_copied, 1)

                def add_bias(e, u, j):
                    if j == 0:
                        dve.wait_ge(result_free, e + 1)
                    dve.wait_ge(out_done, PICKS * e + j + 1)
                    nc.vector.tensor_tensor(result[:, u, j, :], ps_out[:, j % 2, :], b2_sb[:, u, :], ALU.add
                                            ).then_inc(out_copied, 1)

                def run(e, u, ahead):
                    for m in range(KD):
                        split_h(e, m)
                        if ahead:
                            split_x(e + 1, 1 - u, m)
                            for n in WEIGHTS_UP[m]:
                                split_w(e + 1, 1 - u, n)
                    for j in range(PICKS):
                        if ahead:
                            for n in WEIGHTS_DOWN[j][:1]:
                                split_w(e + 1, 1 - u, n)
                        add_bias(e, u, j)
                        if ahead:
                            for n in WEIGHTS_DOWN[j][1:]:
                                split_w(e + 1, 1 - u, n)

                for n in range(2 * KD):
                    split_w(0, 0, n)
                for j in range(PICKS):
                    split_x(0, 0, j)
                with dve.Fori(0, EXPERTS // 2 - 1) as pair:
                    for u in range(2):
                        run(2 * pair + u, u, True)
                run(EXPERTS - 2, 0, True)
                run(EXPERTS - 1, 1, False)


def front_stages(nc, x, adj, wp, w1, w2, wfold_dram, y_dram, h_dram, ident, stats):
    with ExitStack() as ctx:
        def sb(name, shape, dt=F32):
            return ctx.enter_context(nc.sbuf_tensor(name, shape, dt))

        front = Front(nc, ctx, x, y_dram, ident)
        w1pair = sb("w1pair", [P, PARTS, 2, P], F32R)
        w2pair = sb("w2pair", [P, 32])
        fold_block(nc, adj, wp, w1, w2, wfold_dram, ident, w1pair, w2pair, front)
        wfold = sb("wfold", [P, PARTS, CHUNKS, D], F32R)
        tokenizer_block(nc, front, y_dram, wfold_dram, h_dram, w1pair, w2pair, wfold, stats)


def audio_tower(nc, x, adj, tok_w1, tok_w2, wp, W_in, b_in, Wq, Wk, Wv, W_out, b_out, gate_w, w1, b1, w2, b2, out):
    def scratch(name, shape):
        return nc.dram_tensor(name, shape, F32, kind="Internal").ap()

    wfold_dram = scratch("wfold_dram", [PARTS, NPAD * PATCH, D])
    y_dram = scratch("y_dram", [BLOCKS, NPAD, PATCH, TB])
    h_dram = scratch("h_dram", [TOK, D])
    row_dram = scratch("row_dram", [TOK, D])
    out_rows = out.rearrange("b p n -> (b p) n")

    with ExitStack() as whole:
        def sb(ctx, name, shape, dt=F32):
            return ctx.enter_context(nc.sbuf_tensor(name, shape, dt))

        ident = sb(whole, "ident", [P, P])
        stats = sb(whole, "stats", [P, NTILES, 6])
        row_index = sb(whole, "row_index", [P, EXPERTS, TOP, HALVES], I32)
        weight = sb(whole, "weight", [P, EXPERTS, TOP, HALVES])
        front_stages(nc, x, adj, wp, tok_w1, tok_w2, wfold_dram, y_dram, h_dram, ident, stats)
        affinity = sb(whole, "affinity", [P, HALVES, PATCH, EXPERTS])
        with ExitStack() as ctx:
            h = sb(ctx, "h", [P, NTILES, D])
            attention_block(nc, h_dram, W_in, b_in, Wq, Wk, Wv, W_out, b_out, ident, h, stats,
                            out_rows)
            routing_block(nc, gate_w, ident, h, stats, row_dram, affinity)
        choice_block(nc, affinity, row_index, weight)
        expert_block(nc, w1, b1, w2, b2, ident, row_index, weight, row_dram, out_rows)


_INS = ['x', 'L0_tok_adj', 'L0_tok_w1', 'L0_tok_w2', 'L0_tok_wp', 'L0_attn_W_in', 'L0_attn_b_in', 'L0_attn_Wq',
        'L0_attn_Wk', 'L0_attn_Wv', 'L0_attn_W_out', 'L0_attn_b_out', 'L0_ffn_gate_weight', 'L0_ffn_w1',
        'L0_ffn_b1', 'L0_ffn_w2', 'L0_ffn_b2']
_OUT = ((BATCH, PATCH, D), 'float32')


def kernel(**inputs):
    import numpy as _np
    import concourse.bacc as _bacc
    from concourse.bass_utils import run_bass_kernel_spmd as _run

    nc = _bacc.Bacc("TRN2", target_bir_lowering=False, num_devices=1)
    arrays, args = {}, []
    for name in _INS:
        a = _np.ascontiguousarray(inputs[name])
        arrays[f"in_{name}"] = a
        args.append(nc.dram_tensor(f"in_{name}", a.shape, mybir.dt.from_np(a.dtype), kind="ExternalInput").ap())
    out = nc.dram_tensor("out", _OUT[0], mybir.dt.from_np(_np.dtype(_OUT[1])), kind="ExternalOutput").ap()
    audio_tower(nc, *args, out)
    r = _run(nc, [arrays], core_ids=[0])
    return r.results[0]["out"]
```
